# Optimizing a Trainium2 kernel written in Bass

```python
import numpy as np
import jax
import jax.numpy as jnp

def _softmax(x, axis=-1):
    return jax.nn.softmax(x, axis=axis)

def _gelu(x):
    return jax.nn.gelu(x, approximate=True)

def _silu(x):
    return jax.nn.silu(x)

def _sigmoid(x):
    return jax.nn.sigmoid(x)

def _layernorm(x, axis=-1, eps=1e-05):
    m = jnp.mean(x, axis=axis, keepdims=True)
    v = jnp.var(x, axis=axis, keepdims=True)
    return (x - m) / jnp.sqrt(v + eps)

def _scatter_add(tgt, idx, src, axis=0):
    return tgt.at[idx].add(src)

def _segment_sum(src, seg, n):
    return jax.ops.segment_sum(src, seg, n)
kernel_name = 'mk_seq_postln_d2_jaxref_r8_7b6a93'

def setup_inputs(seed: int=0):
    np.random.seed(seed)
    _w = jnp.asarray

    def _L0_attn_setup():
        import jax, jax.numpy as jnp
        import numpy as np
        import math
        B, T, C = (2, 256, 128)
        H, L = (16, 64)
        DH = C // H
        DHE = DH // 2
        THETA = 10000.0

        def _rope_cache(t, dim):
            inv_freq = 1.0 / THETA ** (jnp.arange(0, dim, 2, dtype=jnp.float32) / dim)
            freqs = jnp.arange(t, dtype=jnp.float32)[:, None] * inv_freq[None, :]
            emb = jnp.concatenate((freqs, freqs), axis=-1)
            return (jnp.cos(emb), jnp.sin(emb))

        def _apply_rope(x, cos, sin):
            x1 = x[..., 0::2]
            x2 = x[..., 1::2]
            rot = jnp.stack((-x2, x1), axis=-1).reshape(x.shape)
            return x * cos[None, None] + rot * sin[None, None]
        key = jax.random.key(seed)
        ks = jax.random.split(key, 10)
        s = 0.02
        return {'x': jax.random.normal(ks[0], (B, T, C), jnp.float32), 'Wq_down': jax.random.normal(ks[1], (C, H * L), jnp.float32) * s, 'Wk_down': jax.random.normal(ks[2], (C, H * L), jnp.float32) * s, 'Wv_down': jax.random.normal(ks[3], (C, H * L), jnp.float32) * s, 'Wq_up_c': jax.random.normal(ks[4], (L, DHE), jnp.float32) * s, 'Wq_up_e': jax.random.normal(ks[5], (L, DHE), jnp.float32) * s, 'Wk_up_c': jax.random.normal(ks[6], (L, DHE), jnp.float32) * s, 'Wk_up_e': jax.random.normal(ks[7], (L, DHE), jnp.float32) * s, 'Wv_up': jax.random.normal(ks[8], (L, DH), jnp.float32) * s, 'Wc': jax.random.normal(ks[9], (C, C), jnp.float32) * s}
    _L0_attn_in = _L0_attn_setup()

    def _L0_ffn_setup():
        import jax, jax.numpy as jnp
        import numpy as np
        B, N, D, E, DFF = (4, 256, 128, 16, 512)
        CAPACITY_FACTOR = 2.0
        CAP = int(N * CAPACITY_FACTOR / E)
        SINKHORN_ITERS = 6

        def _sinkhorn(logits, n_iters=SINKHORN_ITERS, tau=1.0):
            t = logits / tau
            for _ in range(n_iters):
                t = t - jax.scipy.special.logsumexp(t, axis=-2, keepdims=True)
                t = t - jax.scipy.special.logsumexp(t, axis=-1, keepdims=True)
            return jnp.exp(t)
        key = jax.random.key(seed)
        ks = jax.random.split(key, 6)
        scaled = lambda k, sh, fan: (jax.random.normal(k, sh, jnp.float32) / np.sqrt(fan)).astype(jnp.float32)
        return {'x': jax.random.normal(ks[0], (B, N, D), jnp.float32), 'gate_query': scaled(ks[1], (E, D), D), 'log_temp': jnp.asarray(np.log(0.5), jnp.float32), 'w1': scaled(ks[2], (E, D, DFF), D), 'b1': jnp.zeros((E, DFF), jnp.float32), 'w2': scaled(ks[3], (E, DFF, D), DFF), 'b2': jnp.zeros((E, D), jnp.float32)}
    _L0_ffn_in = _L0_ffn_setup()

    def _L1_attn_setup():
        import jax, jax.numpy as jnp
        import numpy as np
        B, S, D = (2, 512, 128)
        LOOKBACK = 32
        TOPK = 16
        CHUNK = 32
        NEG = -1e+30

        def _phrase_states(h):
            b, seq, d = h.shape
            hc = h.reshape(b, seq // CHUNK, CHUNK, d)
            pref = jnp.cumsum(hc, axis=2)
            denom = jnp.arange(1, CHUNK + 1, dtype=h.dtype).reshape(1, 1, CHUNK, 1)
            return (pref / denom).reshape(b, seq, d)

        def _shift1(x):
            return jnp.pad(x, ((0, 0), (1, 0), (0, 0)))[:, :-1]
        key = jax.random.key(seed)
        ks = jax.random.split(key, 11)
        s = 0.02
        inp = {'h': jax.random.normal(ks[0], (B, S, D), jnp.float32)}
        names = ['q_w', 'k_w', 'v_w', 'pk_w', 'pv_w']
        for i, n in enumerate(names):
            inp[n] = jax.random.normal(ks[1 + i], (D, D), jnp.float32) * s
            inp[n.replace('_w', '_b')] = jax.random.normal(ks[6 + i], (D,), jnp.float32) * s
        return inp
    _L1_attn_in = _L1_attn_setup()

    def _L1_ffn_setup():
        import jax, jax.numpy as jnp
        import numpy as np
        DIM = 128
        DEPTH = 6
        HEADS = 16
        DIM_HEAD = 64
        WINDOW = 32
        INNER = HEADS * DIM_HEAD
        DIM_INNER = int(DIM * 4 * 2 / 3)
        QK_SCALE = 8.0

        def shift_tokens(t):
            a, s = jnp.split(t, 2, -1)
            s = jnp.pad(s, ((0, 0), (1, 0), (0, 0)))[:, :-1]
            return jnp.concatenate([a, s], -1)

        def l2norm(t):
            return t / jnp.maximum(jnp.linalg.norm(t, axis=-1, keepdims=True), 1e-12)

        def rotate_half(x):
            x1, x2 = jnp.split(x, 2, -1)
            return jnp.concatenate([-x2, x1], -1)

        def rotary_tables(n):
            half = jnp.arange(0, DIM_HEAD, 2, dtype=jnp.float32)
            inv_freq = 1.0 / 10000.0 ** (half / DIM_HEAD)
            t = jnp.arange(n, dtype=jnp.float32)
            freqs = t[:, None] * inv_freq[None, :]
            freqs = jnp.concatenate([freqs, freqs], -1)
            base_scale = (half + 0.4 * DIM_HEAD) / (1.4 * DIM_HEAD)
            power = (t - n // 2) / (WINDOW // 2)
            scale = base_scale[None, :] ** power[:, None]
            scale = jnp.concatenate([scale, scale], -1)
            return (freqs, scale)

        def local_attention(q, k, v):
            b, h, n, d = q.shape
            w = WINDOW
            nw = n // w
            bq = q.reshape(b, h, nw, w, d)
            bk = k.reshape(b, h, nw, w, d)
            bv = v.reshape(b, h, nw, w, d)

            def look(t):
                p = jnp.pad(t, ((0, 0), (0, 0), (1, 0), (0, 0), (0, 0)))
                return jnp.concatenate([p[:, :, :nw], p[:, :, 1:]], axis=3)
            bk2, bv2 = (look(bk), look(bv))
            seq = jnp.arange(n).reshape(nw, w)
            seq_p = jnp.pad(seq, ((1, 0), (0, 0)), constant_values=-1)
            jt = jnp.concatenate([seq_p[:nw], seq_p[1:]], axis=1)
            it = seq[:, :, None]
            jb = jt[:, None, :]
            mask = (it < jb) | (it > jb + w) | (jb == -1)
            sim = jnp.einsum('bhwie,bhwje->bhwij', bq, bk2) * QK_SCALE
            sim = jnp.where(mask, -jnp.finfo(sim.dtype).max, sim)
            attn = jax.nn.softmax(sim, -1)
            out = jnp.einsum('bhwij,bhwje->bhwie', attn, bv2)
            return out.reshape(b, h, n, d)

        def attn_layer(x, Wqkv, qs, ksc, Wo):
            b, n, _ = x.shape
            qkv = x @ Wqkv
            q, k, v = jnp.split(qkv, 3, -1)
            sh = lambda t: t.reshape(b, n, HEADS, DIM_HEAD).transpose(0, 2, 1, 3)
            q, k, v = (sh(q), sh(k), sh(v))
            q = l2norm(q) * qs
            k = l2norm(k) * ksc
            freqs, scale = rotary_tables(n)
            cos, sin = (jnp.cos(freqs), jnp.sin(freqs))
            q = q * cos * scale + rotate_half(q) * sin * scale
            inv = 1.0 / scale
            k = k * cos * inv + rotate_half(k) * sin * inv
            out = local_attention(q, k, v)
            out = out.transpose(0, 2, 1, 3).reshape(b, n, INNER)
            return out @ Wo

        def ffn_layer(x, g, bln, W1, b1, W2, b2):
            mu = x.mean(-1, keepdims=True)
            var = ((x - mu) ** 2).mean(-1, keepdims=True)
            xn = (x - mu) / jnp.sqrt(var + 1e-05) * g + bln
            hg = xn @ W1 + b1
            a, gate = jnp.split(hg, 2, -1)
            return a * jax.nn.gelu(gate, approximate=False) @ W2 + b2
        key = jax.random.key(seed)
        ks = jax.random.split(key, 8)
        B, N = (2, 256)
        init = lambda k, shape: jax.random.normal(k, shape, jnp.float32) * 0.02
        return {'x': jax.random.normal(ks[0], (B, N, DIM), jnp.float32), 'Wqkv': init(ks[1], (DEPTH, DIM, 3 * INNER)), 'q_scale': jnp.ones((DEPTH, DIM_HEAD), jnp.float32), 'k_scale': jnp.ones((DEPTH, DIM_HEAD), jnp.float32), 'Wo': init(ks[2], (DEPTH, INNER, DIM)), 'ln_g': jnp.ones((DEPTH, DIM), jnp.float32), 'ln_b': jnp.zeros((DEPTH, DIM), jnp.float32), 'W1': init(ks[3], (DEPTH, DIM, 2 * DIM_INNER)), 'b1': jnp.zeros((DEPTH, 2 * DIM_INNER), jnp.float32), 'W2': init(ks[4], (DEPTH, DIM_INNER, DIM)), 'b2': jnp.zeros((DEPTH, DIM), jnp.float32)}
    _L1_ffn_in = _L1_ffn_setup()
    _d = {'L0_attn_x': _L0_attn_in['x'], 'L0_attn_Wq_down': _L0_attn_in['Wq_down'], 'L0_attn_Wk_down': _L0_attn_in['Wk_down'], 'L0_attn_Wv_down': _L0_attn_in['Wv_down'], 'L0_attn_Wq_up_c': _L0_attn_in['Wq_up_c'], 'L0_attn_Wq_up_e': _L0_attn_in['Wq_up_e'], 'L0_attn_Wk_up_c': _L0_attn_in['Wk_up_c'], 'L0_attn_Wk_up_e': _L0_attn_in['Wk_up_e'], 'L0_attn_Wv_up': _L0_attn_in['Wv_up'], 'L0_attn_Wc': _L0_attn_in['Wc'], 'L0_ffn_gate_query': _L0_ffn_in['gate_query'], 'L0_ffn_log_temp': _L0_ffn_in['log_temp'], 'L0_ffn_w1': _L0_ffn_in['w1'], 'L0_ffn_b1': _L0_ffn_in['b1'], 'L0_ffn_w2': _L0_ffn_in['w2'], 'L0_ffn_b2': _L0_ffn_in['b2'], 'L1_attn_q_w': _L1_attn_in['q_w'], 'L1_attn_q_b': _L1_attn_in['q_b'], 'L1_attn_k_w': _L1_attn_in['k_w'], 'L1_attn_k_b': _L1_attn_in['k_b'], 'L1_attn_v_w': _L1_attn_in['v_w'], 'L1_attn_v_b': _L1_attn_in['v_b'], 'L1_attn_pk_w': _L1_attn_in['pk_w'], 'L1_attn_pk_b': _L1_attn_in['pk_b'], 'L1_attn_pv_w': _L1_attn_in['pv_w'], 'L1_attn_pv_b': _L1_attn_in['pv_b'], 'L1_ffn_Wqkv': _L1_ffn_in['Wqkv'], 'L1_ffn_q_scale': _L1_ffn_in['q_scale'], 'L1_ffn_k_scale': _L1_ffn_in['k_scale'], 'L1_ffn_Wo': _L1_ffn_in['Wo'], 'L1_ffn_ln_g': _L1_ffn_in['ln_g'], 'L1_ffn_ln_b': _L1_ffn_in['ln_b'], 'L1_ffn_W1': _L1_ffn_in['W1'], 'L1_ffn_b1': _L1_ffn_in['b1'], 'L1_ffn_W2': _L1_ffn_in['W2'], 'L1_ffn_b2': _L1_ffn_in['b2']}
    _x0 = _d['L0_attn_x']
    _d['L0_attn_x'] = jax.random.normal(jax.random.fold_in(jax.random.key(seed), 1), (16, 256, 128), dtype=_x0.dtype)
    del _x0
    return _d

def reference(L0_attn_x, L0_attn_Wq_down, L0_attn_Wk_down, L0_attn_Wv_down, L0_attn_Wq_up_c, L0_attn_Wq_up_e, L0_attn_Wk_up_c, L0_attn_Wk_up_e, L0_attn_Wv_up, L0_attn_Wc, L0_ffn_gate_query, L0_ffn_log_temp, L0_ffn_w1, L0_ffn_b1, L0_ffn_w2, L0_ffn_b2, L1_attn_q_w, L1_attn_q_b, L1_attn_k_w, L1_attn_k_b, L1_attn_v_w, L1_attn_v_b, L1_attn_pk_w, L1_attn_pk_b, L1_attn_pv_w, L1_attn_pv_b, L1_ffn_Wqkv, L1_ffn_q_scale, L1_ffn_k_scale, L1_ffn_Wo, L1_ffn_ln_g, L1_ffn_ln_b, L1_ffn_W1, L1_ffn_b1, L1_ffn_W2, L1_ffn_b2):

    def _L0_attn_ref(x, Wq_down, Wk_down, Wv_down, Wq_up_c, Wq_up_e, Wk_up_c, Wk_up_e, Wv_up, Wc):
        import jax, jax.numpy as jnp
        import numpy as np
        import math
        B, T, C = (2, 256, 128)
        H, L = (16, 64)
        DH = C // H
        DHE = DH // 2
        THETA = 10000.0

        def _rope_cache(t, dim):
            inv_freq = 1.0 / THETA ** (jnp.arange(0, dim, 2, dtype=jnp.float32) / dim)
            freqs = jnp.arange(t, dtype=jnp.float32)[:, None] * inv_freq[None, :]
            emb = jnp.concatenate((freqs, freqs), axis=-1)
            return (jnp.cos(emb), jnp.sin(emb))

        def _apply_rope(x, cos, sin):
            x1 = x[..., 0::2]
            x2 = x[..., 1::2]
            rot = jnp.stack((-x2, x1), axis=-1).reshape(x.shape)
            return x * cos[None, None] + rot * sin[None, None]
        b, t, c = x.shape
        q_lat = (x @ Wq_down).reshape(b, t, H, L)
        k_lat = (x @ Wk_down).reshape(b, t, H, L)
        v_lat = (x @ Wv_down).reshape(b, t, H, L)
        q_c = jnp.einsum('bthl,ld->bhtd', q_lat, Wq_up_c)
        q_e = jnp.einsum('bthl,ld->bhtd', q_lat, Wq_up_e)
        k_c = jnp.einsum('bthl,ld->bhtd', k_lat, Wk_up_c)
        k_e = jnp.einsum('bthl,ld->bhtd', k_lat, Wk_up_e)
        v = jnp.einsum('bthl,ld->bhtd', v_lat, Wv_up)
        cos, sin = _rope_cache(t, DHE)
        q = jnp.concatenate([q_c, _apply_rope(q_e, cos, sin)], axis=-1)
        k = jnp.concatenate([k_c, _apply_rope(k_e, cos, sin)], axis=-1)
        scale = 1.0 / math.sqrt(DH)
        scores = jnp.einsum('bhqd,bhkd->bhqk', q, k) * scale
        causal = jnp.tril(jnp.ones((t, t), dtype=bool))
        scores = jnp.where(causal[None, None], scores, -jnp.inf)
        att = jax.nn.softmax(scores, axis=-1)
        y = jnp.einsum('bhqk,bhkd->bhqd', att, v)
        y = y.transpose(0, 2, 1, 3).reshape(b, t, c)
        return y @ Wc

    def _L0_ffn_ref(x, gate_query, log_temp, w1, b1, w2, b2):
        import jax, jax.numpy as jnp
        import numpy as np
        B, N, D, E, DFF = (4, 256, 128, 16, 512)
        CAPACITY_FACTOR = 2.0
        CAP = int(N * CAPACITY_FACTOR / E)
        SINKHORN_ITERS = 6

        def _sinkhorn(logits, n_iters=SINKHORN_ITERS, tau=1.0):
            t = logits / tau
            for _ in range(n_iters):
                t = t - jax.scipy.special.logsumexp(t, axis=-2, keepdims=True)
                t = t - jax.scipy.special.logsumexp(t, axis=-1, keepdims=True)
            return jnp.exp(t)
        b, n, d = x.shape
        gate_logits = jnp.einsum('bnd,ed->ben', x, gate_query)
        affinity_logits = gate_logits / jnp.exp(log_temp)
        affinity = _sinkhorn(affinity_logits)
        gates, idx = jax.lax.top_k(affinity, CAP)
        expert_in = jnp.take_along_axis(x[:, None, :, :], idx[..., None], axis=2)
        h = jax.nn.gelu(jnp.einsum('becd,edf->becf', expert_in, w1) + b1[None, :, None, :])
        expert_out = jnp.einsum('becf,efd->becd', h, w2) + b2[None, :, None, :]
        out = jnp.zeros_like(x)
        out = out.at[jnp.arange(b)[:, None, None], idx].add(gates[..., None] * expert_out)
        return out

    def _L1_attn_ref(h, q_w, q_b, k_w, k_b, v_w, v_b, pk_w, pk_b, pv_w, pv_b):
        import jax, jax.numpy as jnp
        import numpy as np
        B, S, D = (2, 512, 128)
        LOOKBACK = 32
        TOPK = 16
        CHUNK = 32
        NEG = -1e+30

        def _phrase_states(h):
            b, seq, d = h.shape
            hc = h.reshape(b, seq // CHUNK, CHUNK, d)
            pref = jnp.cumsum(hc, axis=2)
            denom = jnp.arange(1, CHUNK + 1, dtype=h.dtype).reshape(1, 1, CHUNK, 1)
            return (pref / denom).reshape(b, seq, d)

        def _shift1(x):
            return jnp.pad(x, ((0, 0), (1, 0), (0, 0)))[:, :-1]
        b, seq, d = h.shape
        scale = 1.0 / np.sqrt(d)
        q = h @ q_w.T + q_b
        k = h @ k_w.T + k_b
        v = h @ v_w.T + v_b
        ph = _phrase_states(h)
        pk = ph @ pk_w.T + pk_b
        pv = ph @ pv_w.T + pv_b
        k_prev, v_prev = (_shift1(k), _shift1(v))
        pk_prev, pv_prev = (_shift1(pk), _shift1(pv))
        seq_score = jnp.einsum('bsd,bsd->bs', q, k_prev) * scale
        phr_score = jnp.einsum('bsd,bsd->bs', q, pk_prev) * scale
        k_pad = jnp.pad(k, ((0, 0), (LOOKBACK, 0), (0, 0)))
        t_idx = jnp.arange(seq)

        def step(_, l):
            kl = jax.lax.dynamic_slice_in_dim(k_pad, l, seq, axis=1)
            sc = jnp.einsum('bsd,bsd->bs', q, kl) * scale
            valid = t_idx + l >= LOOKBACK
            return (None, jnp.where(valid[None, :], sc, NEG))
        _, scores = jax.lax.scan(step, None, jnp.arange(LOOKBACK))
        scores = jnp.moveaxis(scores, 0, -1)
        top_sc, top_l = jax.lax.top_k(scores, TOPK)
        gidx = jnp.clip(t_idx[None, :, None] - LOOKBACK + top_l, 0, seq - 1)
        sem_v = jax.vmap(lambda vb, ib: vb[ib])(v, gidx)
        all_sc = jnp.concatenate([seq_score[..., None], top_sc, phr_score[..., None]], axis=-1)
        all_v = jnp.concatenate([v_prev[:, :, None, :], sem_v, pv_prev[:, :, None, :]], axis=2)
        w = jax.nn.softmax(all_sc, axis=-1)
        out = jnp.einsum('bsn,bsnd->bsd', w, all_v)
        return jnp.where(t_idx[None, :, None] > 0, out, jnp.zeros((), out.dtype))

    def _L1_ffn_ref(x, Wqkv, q_scale, k_scale, Wo, ln_g, ln_b, W1, b1, W2, b2):
        import jax, jax.numpy as jnp
        import numpy as np
        DIM = 128
        DEPTH = 6
        HEADS = 16
        DIM_HEAD = 64
        WINDOW = 32
        INNER = HEADS * DIM_HEAD
        DIM_INNER = int(DIM * 4 * 2 / 3)
        QK_SCALE = 8.0

        def shift_tokens(t):
            a, s = jnp.split(t, 2, -1)
            s = jnp.pad(s, ((0, 0), (1, 0), (0, 0)))[:, :-1]
            return jnp.concatenate([a, s], -1)

        def l2norm(t):
            return t / jnp.maximum(jnp.linalg.norm(t, axis=-1, keepdims=True), 1e-12)

        def rotate_half(x):
            x1, x2 = jnp.split(x, 2, -1)
            return jnp.concatenate([-x2, x1], -1)

        def rotary_tables(n):
            half = jnp.arange(0, DIM_HEAD, 2, dtype=jnp.float32)
            inv_freq = 1.0 / 10000.0 ** (half / DIM_HEAD)
            t = jnp.arange(n, dtype=jnp.float32)
            freqs = t[:, None] * inv_freq[None, :]
            freqs = jnp.concatenate([freqs, freqs], -1)
            base_scale = (half + 0.4 * DIM_HEAD) / (1.4 * DIM_HEAD)
            power = (t - n // 2) / (WINDOW // 2)
            scale = base_scale[None, :] ** power[:, None]
            scale = jnp.concatenate([scale, scale], -1)
            return (freqs, scale)

        def local_attention(q, k, v):
            b, h, n, d = q.shape
            w = WINDOW
            nw = n // w
            bq = q.reshape(b, h, nw, w, d)
            bk = k.reshape(b, h, nw, w, d)
            bv = v.reshape(b, h, nw, w, d)

            def look(t):
                p = jnp.pad(t, ((0, 0), (0, 0), (1, 0), (0, 0), (0, 0)))
                return jnp.concatenate([p[:, :, :nw], p[:, :, 1:]], axis=3)
            bk2, bv2 = (look(bk), look(bv))
            seq = jnp.arange(n).reshape(nw, w)
            seq_p = jnp.pad(seq, ((1, 0), (0, 0)), constant_values=-1)
            jt = jnp.concatenate([seq_p[:nw], seq_p[1:]], axis=1)
            it = seq[:, :, None]
            jb = jt[:, None, :]
            mask = (it < jb) | (it > jb + w) | (jb == -1)
            sim = jnp.einsum('bhwie,bhwje->bhwij', bq, bk2) * QK_SCALE
            sim = jnp.where(mask, -jnp.finfo(sim.dtype).max, sim)
            attn = jax.nn.softmax(sim, -1)
            out = jnp.einsum('bhwij,bhwje->bhwie', attn, bv2)
            return out.reshape(b, h, n, d)

        def attn_layer(x, Wqkv, qs, ksc, Wo):
            b, n, _ = x.shape
            qkv = x @ Wqkv
            q, k, v = jnp.split(qkv, 3, -1)
            sh = lambda t: t.reshape(b, n, HEADS, DIM_HEAD).transpose(0, 2, 1, 3)
            q, k, v = (sh(q), sh(k), sh(v))
            q = l2norm(q) * qs
            k = l2norm(k) * ksc
            freqs, scale = rotary_tables(n)
            cos, sin = (jnp.cos(freqs), jnp.sin(freqs))
            q = q * cos * scale + rotate_half(q) * sin * scale
            inv = 1.0 / scale
            k = k * cos * inv + rotate_half(k) * sin * inv
            out = local_attention(q, k, v)
            out = out.transpose(0, 2, 1, 3).reshape(b, n, INNER)
            return out @ Wo

        def ffn_layer(x, g, bln, W1, b1, W2, b2):
            mu = x.mean(-1, keepdims=True)
            var = ((x - mu) ** 2).mean(-1, keepdims=True)
            xn = (x - mu) / jnp.sqrt(var + 1e-05) * g + bln
            hg = xn @ W1 + b1
            a, gate = jnp.split(hg, 2, -1)
            return a * jax.nn.gelu(gate, approximate=False) @ W2 + b2
        for i in range(DEPTH):
            x = attn_layer(shift_tokens(x), Wqkv[i], q_scale[i], k_scale[i], Wo[i]) + x
            x = ffn_layer(shift_tokens(x), ln_g[i], ln_b[i], W1[i], b1[i], W2[i], b2[i]) + x
        return x
    x = L0_attn_x
    x = _layernorm(x + _L0_attn_ref(x, L0_attn_Wq_down, L0_attn_Wk_down, L0_attn_Wv_down, L0_attn_Wq_up_c, L0_attn_Wq_up_e, L0_attn_Wk_up_c, L0_attn_Wk_up_e, L0_attn_Wv_up, L0_attn_Wc), axis=-1)
    x = _layernorm(x + _L0_ffn_ref(x, L0_ffn_gate_query, L0_ffn_log_temp, L0_ffn_w1, L0_ffn_b1, L0_ffn_w2, L0_ffn_b2), axis=-1)
    x = _layernorm(x + _L1_attn_ref(x, L1_attn_q_w, L1_attn_q_b, L1_attn_k_w, L1_attn_k_b, L1_attn_v_w, L1_attn_v_b, L1_attn_pk_w, L1_attn_pk_b, L1_attn_pv_w, L1_attn_pv_b), axis=-1)
    x = _layernorm(x + _L1_ffn_ref(x, L1_ffn_Wqkv, L1_ffn_q_scale, L1_ffn_k_scale, L1_ffn_Wo, L1_ffn_ln_g, L1_ffn_ln_b, L1_ffn_W1, L1_ffn_b1, L1_ffn_W2, L1_ffn_b2), axis=-1)
    return x

_drawn_inputs = setup_inputs


def setup_inputs(seed=0):
    import zlib

    import numpy as np

    out = dict(_drawn_inputs(seed))
    spreads = {'L0_ffn_b1': (0.0, 2.0),
     'L0_ffn_b2': (0.0, 0.8),
     'L1_ffn_q_scale': (1.0, 0.6),
     'L1_ffn_k_scale': (1.0, 0.6),
     'L1_ffn_ln_g': (1.0, 0.6),
     'L1_ffn_ln_b': (0.0, 0.8),
     'L1_ffn_b1': (0.0, 0.8),
     'L1_ffn_b2': (0.0, 0.1)}
    factors = {'L0_attn_Wq_down': 8.0,
     'L0_attn_Wk_down': 8.0,
     'L0_attn_Wv_down': 8.0,
     'L0_attn_Wq_up_c': 8.0,
     'L0_attn_Wq_up_e': 8.0,
     'L0_attn_Wk_up_c': 8.0,
     'L0_attn_Wk_up_e': 8.0,
     'L0_attn_Wv_up': 8.0,
     'L0_attn_Wc': 8.0,
     'L0_ffn_w1': 2.723,
     'L1_attn_q_b': 5.595,
     'L1_attn_k_b': 64.0,
     'L1_attn_v_b': 2.892,
     'L1_attn_pk_w': 23.176,
     'L1_attn_pk_b': 64.0,
     'L1_attn_pv_w': 7.878,
     'L1_attn_pv_b': 36.815,
     'L1_ffn_W1': 3.674,
     'L1_ffn_W2': 3.611}
    for name, (base, spread) in spreads.items():
        noise = np.random.default_rng([zlib.crc32(name.encode()), seed]).standard_normal(out[name].shape)
        drawn = base * np.exp(spread * noise) if base else spread * noise
        out[name] = jnp.asarray(drawn.astype(out[name].dtype))
    for name, factor in factors.items():
        out[name] = (out[name] * factor).astype(out[name].dtype)
    return out
```

```python
from contextlib import ExitStack

import numpy as np
import concourse.bass as bass
from concourse import mybir

ALU = mybir.AluOpType
ACT = mybir.ActivationFunctionType
AX = mybir.AxisListType
F32 = mybir.dt.float32
BF16 = mybir.dt.bfloat16
U32 = mybir.dt.uint32
I32 = mybir.dt.int32

P = 128
NB = 16
T = 256
C = 128
NT = T // P
MASKED = -1.0e30
HUGE = 3.0e38
LN_EPS = 1.0e-5
RSQRT_GUESS = float(0x5F3759DF)


class Steps:

    def __init__(self, eng, sem, per, passed=None):
        self.eng, self.sem, self.per, self.passed = eng, sem, per, passed
        self.base, self.count = 0, 0

    def start(self, n):
        self.base, self.count = n * self.per, 0

    def inc(self, ins):
        ins.then_inc(self.sem, 1)
        self.count += 1

    def wait(self):
        self.eng.wait_ge(self.sem, self.base + self.count)

    def link(self, ins):
        self.inc(ins)
        self.wait()

    def end(self):
        assert self.count == self.per, (self.count, self.per)


def bcast(ap, axis, n):
    a = ap.unsqueeze(axis)
    shape = list(a.shape)
    shape[axis] = n
    return a.broadcast_to(shape)


def ge(eng, sem, value):
    if not (isinstance(value, int) and value <= 0):
        eng.wait_ge(sem, value)


def clear_semaphores(nc, semaphores):
    with nc.Block() as block:
        @block.gpsimd
        def _(pool):
            for s in semaphores:
                pool.sem_clear(s)


def held(eng, passed):
    eng.sem_inc(passed, 1)


def passes(eng, one):
    def pair(i, last):
        one(2 * i, 0, (2 * i + 1, i, 1))
        one(2 * i + 1, 1, None if last else (2 * i + 2, i + 1, 0))
    pair(0, False)
    with eng.Fori(1, NB // 2 - 1) as i:
        pair(i, False)
    pair(NB // 2 - 1, True)


def looped(eng, one):
    def pair(i, last):
        one(2 * i, 0, (2 * i + 1, i, 1))
        one(2 * i + 1, 1, None if last else (2 * i + 2, i + 1, 0))
    with eng.Fori(0, NB // 2 - 1) as i:
        pair(i, False)
    pair(NB // 2 - 1, True)


def layer_norm(nc, dve, steps, z, X, b, st, mv, rstd, s_mv, s_rstd, s_x):
    for j in range(NT):
        steps.inc(nc.vector.bn_stats(st[:, j, :], z[:, j, :]))
    steps.wait()
    held(dve, steps.passed)
    for j in range(NT):
        steps.inc(nc.vector.bn_aggr(mv[:, j, :], st[:, j, :]))
    steps.wait()
    nc.vector.tensor_scalar(mv[:, :, 1], mv[:, :, 1], LN_EPS, None, ALU.add).then_inc(s_mv, 1)
    dve.wait_ge(s_rstd, b + 1)
    for j in range(NT):
        nc.vector.tensor_scalar(X[:, bass.ds(2 * b + j, 1), :].rearrange("p o c -> p (o c)"), z[:, j, :],
                                mv[:, j, 0:1], rstd[:, j:j + 1], ALU.subtract, ALU.mult).then_inc(s_x, 1)
    dve.wait_ge(s_x, 2 * b + 2)


def l0_attention(nc, env, weights, consts):
    H, L, D = 16, 64, 8
    G = H // 4
    NU = (H // 2) * NT
    SCALE = 1.0 / np.sqrt(D)
    ident, X, neghalf = env["ident"], env["X"], env["neghalf"]
    x_dram = env["x_dram"]
    DVE_STEPS = 5

    def heads(n):
        hp = n // 2
        return (hp % 4 + 4 * (2 * (hp // 4)), hp % 4 + 4 * (2 * (hp // 4) + 1))

    with ExitStack() as ctx:
        def sb(name, shape, dt=F32):
            return ctx.enter_context(nc.sbuf_tensor("a_" + name, shape, dt))

        def ps(name, shape):
            return ctx.enter_context(nc.psum_tensor("a_" + name, shape, F32))

        every = []

        def sem(name):
            s = ctx.enter_context(nc.semaphore("a_" + name))
            every.append(s)
            return s

        down = sb("down", [P, 3, H * L])
        up2 = sb("up2", [P, 3, 2, D])
        downT = sb("downT", [P, 2, C])
        weff = sb("weff", [P, 3 * H * D])
        wc_sb = sb("wc", [P, C])
        cos_sb = sb("cos", [P, NT, 4])
        sin_sb = sb("sin", [P, NT, 4])
        causal = sb("causal", [P, T])
        xs = sb("xs", [P, 2, NT, C])
        xT = sb("xT", [P, T])
        pad = sb("pad", [P, NT, 2 * H, 32])
        r1 = sb("r1", [P, NT, 2 * H, 4])
        r2 = sb("r2", [P, NT, 2 * H, 4])
        qkT = sb("qkT", [P, 2, 2, G, T])
        V = sb("V", [P, 2, NT, H * D])
        S = sb("S", [P, 4, 2, T])
        E = sb("E", [P, 4, 2, T])
        ET = sb("ET", [P, 4, 4, P])
        nm = sb("nm", [P, 2, NT, H])
        rs = sb("rs", [P, 2, NT, H])
        ri = sb("ri", [P, NT, H])
        On = sb("On", [P, NT, H * D])
        OT = sb("OT", [P, T])
        z = sb("z", [P, NT, C])
        st = sb("st", [P, NT, 6])
        mv = sb("mv", [P, NT, 2])
        rstd = sb("rstd", [P, NT])

        pp = ps("pp", [P, 2, 512])
        pS = ps("pS", [P, 2, 512])
        pT = ps("pT", [P, 2, 4, P])
        pO = ps("pO", [P, 2, 512])

        s_w = sem("weights_loaded")
        s_xs = [sem("x_staged0"), sem("x_staged1")]
        s_pad0 = sem("pad_cleared")
        s_dT = sem("down_turned")
        s_dTc = sem("downT_copied")
        s_we = sem("weff_made")
        s_wec = sem("weff_copied")
        s_xTp = sem("x_turned")
        s_xT = sem("xT_copied")
        s_proj = sem("projected")
        s_pad = sem("pad_filled")
        s_V = sem("v_copied")
        s_turn = sem("qk_turned")
        s_qkT = sem("qkT_copied")
        s_S = sem("scored")
        s_Sm = sem("maxed")
        s_E = sem("exped")
        s_ETp = sem("weights_turned")
        s_ETa = sem("wT_copied_by_act")
        s_ETd = sem("wT_copied_by_dve")
        s_PV = sem("pv_done")
        s_On = sem("output_normed")
        s_OTp = sem("output_turned")
        s_OT = sem("outT_copied")
        s_y = sem("y_made")
        s_z = sem("summed")
        s_mv = sem("stats_made")
        s_rstd = sem("rstd_made")
        s_x = sem("x_written")
        s_dve = sem("dve_steps")
        s_held = sem("dve_waits_passed")
        ctx.callback(clear_semaphores, nc, every)
        block = ctx.enter_context(nc.Block())


        @block.sync
        def _(sp):
            for n, name in enumerate(("Wq_down", "Wk_down", "Wv_down")):
                sp.dma_start(down[:, n, :], weights[name]).then_inc(s_w, 16)
            sp.dma_start(wc_sb[:, :], weights["Wc"]).then_inc(s_w, 16)
            sp.dma_start(cos_sb[:, :, :], consts["l0_cos"].rearrange("(j p) d -> p j d", p=P)).then_inc(s_w, 16)
            sp.dma_start(sin_sb[:, :, :], consts["l0_sin"].rearrange("(j p) d -> p j d", p=P)).then_inc(s_w, 16)
            sp.dma_start(ident[:, :], consts["ident"]).then_inc(s_w, 16)
            sp.dma_start(causal[:, :], consts["causal"]).then_inc(s_w, 16)
            sp.dma_start(X[:, :, :], x_dram.rearrange("b (j p) c -> p (b j) c", p=P)).then_inc(s_w, 16)
            sp.wait_ge(s_pad0, 2)
            for n, names in enumerate((("Wq_up_c", "Wq_up_e"), ("Wk_up_c", "Wk_up_e"), ("Wv_up",))):
                for m, name in enumerate(names):
                    w = D // len(names)
                    for e in range(2):
                        sp.dma_start(up2[e * L:(e + 1) * L, n, e, m * w:(m + 1) * w],
                                     weights[name]).then_inc(s_w, 16)

            def stage(q, pair, u):
                if not (isinstance(pair, int) and pair == 0):
                    sp.wait_ge(s_xTp, q - 1)
                sp.dma_start(xs[:, u, :, :], x_dram[q:q + 1, :, :].rearrange("o (j p) c -> p (o j) c", p=P)
                             if isinstance(q, int) else
                             x_dram[bass.ds(q, 1), :, :].rearrange("o (j p) c -> p (o j) c", p=P)
                             ).then_inc(s_xs[u], 16)

            stage(0, 0, 0)
            stage(1, 0, 1)
            with sp.Fori(1, NB // 2) as i:
                for u in range(2):
                    stage(2 * i + u, i, u)
        N_W = 16 * 19

        @block.gpsimd
        def _(pool):
            nc.gpsimd.memset(up2[:, :, :, :], 0.0).then_inc(s_pad0, 1)
            nc.gpsimd.memset(pad[:, :, :, :], 0.0).then_inc(s_pad0, 1)
            nc.gpsimd.memset(neghalf[:, :], -0.5).then_inc(s_pad0, 1)
            pool.wait_ge(s_pad0, 3)

            def tail(b):
                pool.wait_ge(s_mv, b + 1)
                nc.gpsimd.tensor_tensor(rstd[:, :], mv[:, :, 1], neghalf[:, 0:NT], ALU.pow).then_inc(s_rstd, 1)

            with pool.Fori(0, NB) as b:
                tail(b)

        @block.tensor
        def _(pe):
            pe.wait_ge(s_w, N_W)
            for m in range(3 * H // 2):
                n, c = m // (H // 2), m % (H // 2)
                ge(pe, s_dTc, m - 1)
                nc.tensor.transpose(pp[:, m % 2, 0:C], down[:, n, c * P:(c + 1) * P],
                                    ident[:, :]).then_inc(s_dT, 1)
                pe.wait_ge(s_dTc, m + 1)
                ge(pe, s_wec, m - 1)
                nc.tensor.matmul(pS[:, m % 2, 0:16], downT[:, m % 2, :], up2[:, n, :, :],
                                 start=True, stop=True).then_inc(s_we, 1)

            def turn_x(q, pair, u):
                pe.wait_ge(s_xs[u], 16 * (pair + 1))
                ge(pe, s_qkT, 4 * q)
                for j in range(NT):
                    last = nc.tensor.transpose(pp[:, 0, j * P:(j + 1) * P], xs[:, u, j, :], ident[:, :])
                last.then_inc(s_xTp, 1)

            def project(q):
                if isinstance(q, int) and q == 0:
                    pe.wait_ge(s_wec, 3 * H // 2)
                ge(pe, s_OT, q - 1)
                pe.wait_ge(s_xT, q + 1)
                for j in range(NT):
                    nc.tensor.matmul(pp[:, 1 - j, 0:3 * C], xT[:, j * P:(j + 1) * P], weff[:, :],
                                     start=True, stop=True).then_inc(s_proj, 1)

            def turn_qk(q, t):
                pe.wait_ge(s_pad, q + 1)
                for k in range(2):
                    n = 2 * t + k
                    if n >= 2:
                        pe.wait_ge(s_qkT, 4 * q + n - 1)
                    for g in range(2):
                        for j in range(NT):
                            h = t * H + 4 * (2 * k + g)
                            last = nc.tensor.transpose(
                                pp[:, 1 - k, g * T + j * P:g * T + (j + 1) * P],
                                pad[:, j, h:h + 4, :].rearrange("p h d -> p (h d)"), ident[:, :])
                    last.then_inc(s_turn, 1)

            def scores(b, u, n):
                j = n % 2
                if n == 0:
                    pe.wait_ge(s_qkT, 4 * b + 4)
                ge(pe, s_Sm, NU * b + n - 1)
                for m, h in enumerate(heads(n)):
                    r, g = 32 * (h % 4), h // 4
                    last = nc.tensor.matmul(pS[:, n % 2, m * T:m * T + (j + 1) * P],
                                            qkT[r:r + 32, u, 0, g, j * P:(j + 1) * P],
                                            qkT[r:r + 32, u, 1, g, 0:(j + 1) * P], start=True, stop=True)
                last.then_inc(s_S, 1)

            def turn_weights(b, u, n):
                j = n % 2
                pe.wait_ge(s_E, NU * b + n + 1)
                ge(pe, (s_ETa, s_ETd)[j], H // 2 * b + n // 2)
                for m in range(2):
                    for c in range(j + 1):
                        last = nc.tensor.transpose(pT[:, j, m * (j + 1) + c, :],
                                                   E[:, n % 4, m, c * P:(c + 1) * P], ident[:, :])
                last.then_inc(s_ETp, 1)

            def weigh(b, u, n):
                j = n % 2
                pe.wait_ge((s_ETa, s_ETd)[j], H // 2 * b + n // 2 + 1)
                if n == 0:
                    pe.wait_ge(s_V, 2 * b + 2)
                    ge(pe, s_z, b - 1)
                for m, h in enumerate(heads(n)):
                    for c in range(j + 1):
                        last = nc.tensor.matmul(pO[:, u, j * P + h * D:j * P + (h + 1) * D],
                                                ET[:, n % 4, m * (j + 1) + c, :],
                                                V[:, u, c, h * D:(h + 1) * D], start=(c == 0), stop=(c == j))
                last.then_inc(s_PV, 1)

            def tail(b, u, q):
                pe.wait_ge(s_On, b + 1)
                ge(pe, s_qkT, 4 * q + 3)
                for j in range(NT):
                    last = nc.tensor.transpose(pp[:, 1, j * P:(j + 1) * P], On[:, j, :], ident[:, :])
                last.then_inc(s_OTp, 1)
                pe.wait_ge(s_OT, b + 1)
                for j in range(NT):
                    last = nc.tensor.matmul(pO[:, u, T + j * P:T + (j + 1) * P], OT[:, j * P:(j + 1) * P],
                                            wc_sb[:, :], start=True, stop=True)
                last.then_inc(s_y, 1)

            def one(b, u, nxt):
                for n in range(NU + 3):
                    if n < NU:
                        scores(b, u, n)
                    if nxt:
                        q, pair, v = nxt
                        if n == 2:
                            turn_x(q, pair, v)
                        if n == 4:
                            project(q)
                        if n == 8:
                            turn_qk(q, 0)
                        if n == 10:
                            turn_qk(q, 1)
                    if 0 <= n - 2 < NU:
                        turn_weights(b, u, n - 2)
                    if 0 <= n - 3 < NU:
                        weigh(b, u, n - 3)
                tail(b, u, nxt[0] if nxt else b)

            turn_x(0, 0, 0)
            project(0)
            turn_qk(0, 0)
            turn_qk(0, 1)
            passes(pe, one)

        @block.scalar
        def _(act):
            def copy_x(q):
                ge(act, s_proj, 2 * q)
                act.wait_ge(s_xTp, q + 1)
                nc.scalar.copy(xT[:, :], pp[:, 0, 0:T]).then_inc(s_xT, 1)

            def copy_qk(q, u, t):
                ge(act, s_S, NU * (q - 1))
                for k in range(2):
                    act.wait_ge(s_turn, 4 * q + 2 * t + k + 1)
                    nc.scalar.copy(qkT[:, u, t, 2 * k:2 * k + 2, :].rearrange("p g t -> p (g t)"),
                                   pp[:, 1 - k, :]).then_inc(s_qkT, 1)

            def exps(b, u, n):
                j = n % 2
                act.wait_ge(s_Sm, NU * b + n + 1)
                ge(act, s_ETp, NU * b + n - 3)
                for m, h in enumerate(heads(n)):
                    last = nc.scalar.activation(E[:, n % 4, m, 0:(j + 1) * P], S[:, n % 4, m, 0:(j + 1) * P],
                                                ACT.Exp, bias=nm[:, u, j, h:h + 1], scale=-1.0,
                                                accum_out=rs[:, u, j, h:h + 1])
                last.then_inc(s_E, 1)

            def copy_weights(b, n):
                act.wait_ge(s_ETp, NU * b + n + 1)
                ge(act, s_PV, NU * b + n - 3)
                nc.scalar.copy(ET[:, n % 4, 0:2, :].rearrange("p m k -> p (m k)"),
                               pT[:, 0, 0:2, :].rearrange("p m k -> p (m k)")).then_inc(s_ETa, 1)

            def one(b, u, nxt):
                for n in range(NU + 3):
                    if n < NU:
                        exps(b, u, n)
                    if nxt:
                        q, pair, v = nxt
                        if n == 2:
                            copy_x(q)
                        if n == 8:
                            copy_qk(q, v, 0)
                        if n == 10:
                            copy_qk(q, v, 1)
                    if 0 <= n - 2 < NU and (n - 2) % 2 == 0:
                        copy_weights(b, n - 2)
                act.wait_ge(s_OTp, b + 1)
                ge(act, s_y, b)
                nc.scalar.copy(OT[:, :], pp[:, 1, 0:T]).then_inc(s_OT, 1)

            copy_x(0)
            copy_qk(0, 0, 0)
            copy_qk(0, 0, 1)
            passes(act, one)

        @block.vector
        def _(dve):
            steps = Steps(dve, s_dve, DVE_STEPS, s_held)
            dve.wait_ge(s_w, N_W)
            for m in range(3 * H // 2):
                dve.wait_ge(s_dT, m + 1)
                ge(dve, s_we, m - 1)
                nc.vector.tensor_copy(downT[:, m % 2, :], pp[:, m % 2, 0:C]).then_inc(s_dTc, 1)
                dve.wait_ge(s_we, m + 1)
                nc.vector.tensor_copy(weff[:, 16 * m:16 * m + 16], pS[:, m % 2, 0:16]).then_inc(s_wec, 1)

            def rope(q, u, link):
                ge(dve, s_turn, 4 * q)
                ge(dve, s_PV, NU * (q - 1))
                for j in range(NT):
                    dve.wait_ge(s_proj, 2 * q + 1 + j)
                    qk = pp[:, 1 - j, 0:2 * C].rearrange("p (h d) -> p h d", d=D)
                    nc.vector.tensor_copy(pad[:, j, :, 0:4], qk[:, :, 0:4])
                    nc.vector.tensor_tensor(r1[:, j, :, :], qk[:, :, 4:8], bcast(cos_sb[:, j, :], 1, 2 * H), ALU.mult)
                    for e in range(2):
                        nc.vector.tensor_tensor(r2[:, j, :, e:4:2], qk[:, :, 5 - e:8:2],
                                                bcast(sin_sb[:, j, e:4:2], 1, 2 * H), ALU.mult)
                    nc.vector.tensor_copy(V[:, u, j, :], pp[:, 1 - j, 2 * C:3 * C]).then_inc(s_V, 1)
                dve.wait_ge(s_V, 2 * q + 2)
                nc.vector.tensor_tensor(pad[:, :, :, 4:8].rearrange("p j h d -> p (j h) d"),
                                        r1[:, :, :, :].rearrange("p j h d -> p (j h) d"),
                                        r2[:, :, :, :].rearrange("p j h d -> p (j h) d"), ALU.add).then_inc(s_pad, 1)
                dve.wait_ge(s_pad, q + 1)

            def maxima(b, u, n):
                j = n % 2
                ge(dve, s_E, NU * b + n - 3)
                dve.wait_ge(s_S, NU * b + n + 1)
                held(dve, s_held)
                for m, h in enumerate(heads(n)):
                    last = nc.vector.tensor_tensor_reduce(
                        out=S[:, n % 4, m, 0:(j + 1) * P], in0=pS[:, n % 2, m * T:m * T + (j + 1) * P],
                        in1=causal[:, (1 - j) * P:T], scale=-SCALE, scalar=HUGE, op0=ALU.add, op1=ALU.min,
                        accum_out=nm[:, u, j, h:h + 1])
                last.then_inc(s_Sm, 1)

            def copy_weights(b, n):
                dve.wait_ge(s_ETp, NU * b + n + 1)
                ge(dve, s_PV, NU * b + n - 3)
                nc.vector.tensor_copy(ET[:, n % 4, :, :], pT[:, 1, :, :]).then_inc(s_ETd, 1)

            def tail(b, u):
                dve.wait_ge(s_E, NU * b + NU)
                steps.link(nc.vector.reciprocal(ri[:, :, :], rs[:, u, :, :]))
                dve.wait_ge(s_PV, NU * b + NU)
                ge(dve, s_OTp, b)
                nc.vector.tensor_tensor(
                    On[:, :, :].rearrange("p j (h d) -> p (j h) d", d=D),
                    pO[:, u, 0:T].rearrange("p (h d) -> p h d", d=D),
                    bcast(ri[:, :, :].rearrange("p j h -> p (j h)"), 2, D), ALU.mult).then_inc(s_On, 1)
                dve.wait_ge(s_y, b + 1)
                xb = X[:, bass.ds(2 * b, 2), :]
                nc.vector.tensor_tensor(z[:, :, :], pO[:, u, T:2 * T].rearrange("p (j c) -> p j c", j=NT),
                                        xb, ALU.add).then_inc(s_z, 1)
                dve.wait_ge(s_z, b + 1)
                layer_norm(nc, dve, steps, z, X, b, st, mv, rstd, s_mv, s_rstd, s_x)

            def one(b, u, nxt):
                steps.start(b)
                for n in range(NU + 3):
                    if n < NU:
                        maxima(b, u, n)
                    if nxt and n == 4:
                        rope(nxt[0], nxt[2], steps.link)
                    if 0 <= n - 2 < NU and (n - 2) % 2 == 1:
                        copy_weights(b, n - 2)
                tail(b, u)
                steps.end()

            rope(0, 0, None)
            passes(dve, one)


EX, CAP, FF = 16, 32, 512
EG = NB * EX // P
BG = NB // EG
START = 64


def after(eng, s, value):
    eng.wait_ge(s, value + START)


def router(nc, env, weights, consts, idx, val):
    ITERS = 6
    ident, X = env["ident"], env["X"]
    R = NT * NB
    with ExitStack() as ctx:
        def sb(name, shape, dt=F32):
            return ctx.enter_context(nc.sbuf_tensor("r_" + name, shape, dt))

        def ps(name, shape):
            return ctx.enter_context(nc.psum_tensor("r_" + name, shape, F32))

        sems, every = [], []

        def sem(name, counted=True):
            s = ctx.enter_context(nc.semaphore("r_" + name))
            every.append(s)
            if counted:
                sems.append(s)
            return s

        gq = sb("gq", [EX, C])
        gqT = sb("gqT", [P, EX])
        temp = sb("temp", [P, 1])
        itemp = sb("itemp", [P, 1])
        xs = sb("xs", [P, 2, NT, C])
        xT = sb("xT", [P, 2, T])
        tok = sb("tok", [P, NT, NB * EX])
        top = sb("top", [P, R])
        ex = sb("ex", [P, NT, NB * EX])
        total = sb("total", [P, R])
        logs = sb("logs", [P, R])
        row = sb("row", [P, EG, T])
        ntopA = sb("ntopA", [P, EG])
        totalA = sb("totalA", [P, EG])
        logsA = sb("logsA", [P, EG])
        aff = sb("aff", [P, EG, T])
        idx_u = sb("idx_u", [P, EG, CAP], U32)
        pX = ps("pX", [P, 2, 512])
        pL = ps("pL", [P, 2, 512])
        pA = ps("pA", [P, 512])
        pB = ps("pB", [P, 512])

        s_c = sem("loaded", False)
        s_g = sem("gq_turned", False)
        s_gc = sem("gq_copied", False)
        s_t = sem("temp_inverted", False)
        s_xs = sem("x_staged")
        s_xTp = sem("x_turned")
        s_xT = sem("xT_copied")
        s_l = sem("logits")
        s_lc = sem("logits_copied")
        s_top = sem("top_found")
        s_sub = sem("top_taken_off")
        s_ex = sem("exped")
        s_sum = sem("summed")
        s_ln = sem("logged")
        s_B = sem("expert_half_done")
        s_TA = sem("turned_to_rows")
        s_topA = sem("row_top_found")
        s_exA = sem("rows_exped")
        s_lnA = sem("rows_logged")
        s_A = sem("token_half_done")
        s_TB = sem("turned_back")
        s_tok = sem("copied_back")
        s_aff = sem("affinities", False)
        s_k = sem("top_k_steps", False)
        s_held = sem("waits_passed", False)
        ctx.callback(clear_semaphores, nc, every)
        block = ctx.enter_context(nc.Block())

        @block.sync
        def _(sp):
            sp.dma_start(gq[:, :], weights["gate_query"]).then_inc(s_c, 16)
            sp.dma_start(temp[:, :], weights["log_temp"].broadcast_to([P, 1])).then_inc(s_c, 16)

        @block.gpsimd
        def _(pool):
            for s in sems:
                pool.sem_inc(s, START)

            with pool.Fori(0, NB // 2) as i:
                for u in range(2):
                    b = 2 * i + u
                    after(pool, s_xTp, b - 1)
                    held(pool, s_held)
                    nc.gpsimd.tensor_copy(xs[:, u, :, :], X[:, bass.ds(NT * b, NT), :]).then_inc(s_xs, 1)

        @block.tensor
        def _(pe):
            pe.wait_ge(s_c, 32)
            nc.tensor.transpose(pA[:, 0:EX], gq[:, :], ident[0:EX, 0:EX]).then_inc(s_g, 1)
            pe.wait_ge(s_gc, 1)
            with pe.Fori(0, NB // 2) as i:
                for u in range(2):
                    b = 2 * i + u
                    after(pe, s_xs, b + 1)
                    after(pe, s_xT, b - 1)
                    for j in range(NT):
                        last = nc.tensor.transpose(pX[:, u, j * P:(j + 1) * P], xs[:, u, j, :], ident[:, :])
                    last.then_inc(s_xTp, 1)
                    after(pe, s_xT, b + 1)
                    after(pe, s_lc, b - 1)
                    for j in range(NT):
                        last = nc.tensor.matmul(pL[:, u, j * EX:(j + 1) * EX], xT[:, u, j * P:(j + 1) * P], gqT[:, :],
                                                start=True, stop=True)
                    last.then_inc(s_l, 1)
            with pe.Fori(0, ITERS) as k:
                after(pe, s_B, k + 1)
                for g in range(EG):
                    for j in range(NT):
                        last = nc.tensor.transpose(pA[:, g * T + j * P:g * T + (j + 1) * P],
                                                   tok[:, j, g * P:(g + 1) * P], ident[:, :])
                last.then_inc(s_TA, 1)
                after(pe, s_A, k + 1)
                for j in range(NT):
                    for g in range(EG):
                        last = nc.tensor.transpose(pB[:, j * NB * EX + g * P:j * NB * EX + (g + 1) * P],
                                                   row[:, g, j * P:(j + 1) * P], ident[:, :])
                last.then_inc(s_TB, 1)

        @block.scalar
        def _(act):
            act.wait_ge(s_c, 32)
            nc.scalar.activation(itemp[:, :], temp[:, :], ACT.Exp, scale=-1.0).then_inc(s_t, 1)
            with act.Fori(0, NB // 2) as i:
                for u in range(2):
                    b = 2 * i + u
                    after(act, s_l, b - 1)
                    after(act, s_xTp, b + 1)
                    nc.scalar.copy(xT[:, u, :], pX[:, u, 0:T]).then_inc(s_xT, 1)
            with act.Fori(0, ITERS) as k:
                after(act, s_sub, k + 1)
                nc.scalar.activation(ex[:, :, :], tok[:, :, :], ACT.Exp).then_inc(s_ex, 1)
                after(act, s_sum, k + 1)
                nc.scalar.activation(logs[:, :], total[:, :], ACT.Ln).then_inc(s_ln, 1)
                after(act, s_topA, k + 1)
                for g in range(EG):
                    last = nc.scalar.activation(aff[:, g, :], pA[:, g * T:(g + 1) * T], ACT.Exp,
                                                bias=ntopA[:, g:g + 1], accum_out=totalA[:, g:g + 1])
                last.then_inc(s_exA, 1)
                after(act, s_exA, k + 1)
                nc.scalar.activation(logsA[:, :], totalA[:, :], ACT.Ln).then_inc(s_lnA, 1)
                after(act, s_TB, k + 1)
                nc.scalar.copy(tok[:, :, :].rearrange("p j r -> p (j r)"), pB[:, :]).then_inc(s_tok, 1)
            nc.scalar.activation(aff[:, :, :], row[:, :, :], ACT.Exp).then_inc(s_aff, 1)

        @block.vector
        def _(dve):
            dve.wait_ge(s_g, 1)
            nc.vector.tensor_copy(gqT[:, :], pA[:, 0:EX]).then_inc(s_gc, 1)
            dve.wait_ge(s_t, 1)
            with dve.Fori(0, NB // 2) as i:
                for u in range(2):
                    b = 2 * i + u
                    after(dve, s_l, b + 1)
                    nc.vector.tensor_scalar(tok[:, :, bass.ds(b * EX, EX)],
                                            pL[:, u, 0:NT * EX].rearrange("p (j e) -> p j e", j=NT),
                                            itemp[:, 0:1], None, ALU.mult).then_inc(s_lc, 1)
            tok_e = tok[:, :, :].rearrange("p j (b e) -> p (j b) e", e=EX)
            ex_e = ex[:, :, :].rearrange("p j (b e) -> p (j b) e", e=EX)
            after(dve, s_lc, NB)
            with dve.Fori(0, ITERS) as k:
                after(dve, s_tok, k)
                nc.vector.tensor_reduce(top[:, :], tok_e, AX.X, ALU.max).then_inc(s_top, 1)
                after(dve, s_top, k + 1)
                nc.vector.tensor_tensor(tok_e, tok_e, bcast(top[:, :], 2, EX), ALU.subtract).then_inc(s_sub, 1)
                after(dve, s_ex, k + 1)
                nc.vector.tensor_reduce(total[:, :], ex_e, AX.X, ALU.add).then_inc(s_sum, 1)
                after(dve, s_ln, k + 1)
                nc.vector.tensor_tensor(tok_e, tok_e, bcast(logs[:, :], 2, EX), ALU.subtract).then_inc(s_B, 1)
                after(dve, s_TA, k + 1)
                nc.vector.tensor_reduce(ntopA[:, :], pA[:, :].rearrange("p (g n) -> p g n", g=EG), AX.X, ALU.max,
                                        negate=True).then_inc(s_topA, 1)
                after(dve, s_lnA, k + 1)
                for g in range(EG):
                    last = nc.vector.tensor_scalar(row[:, g, :], pA[:, g * T:(g + 1) * T], ntopA[:, g:g + 1],
                                                   logsA[:, g:g + 1], ALU.add, ALU.subtract)
                last.then_inc(s_A, 1)
            dve.wait_ge(s_aff, 1)
            at = 0
            for r in range(CAP // 8):
                for g in range(EG):
                    best = val[:, g, 8 * r:8 * r + 8]
                    nc.vector.max(best, aff[:, g, :]).then_inc(s_k, 1)
                    at += 1
                    dve.wait_ge(s_k, at)
                    nc.vector.max_index(idx_u[:, g, 8 * r:8 * r + 8], best, aff[:, g, :]).then_inc(s_k, 1)
                    nc.vector.match_replace(aff[:, g, :], best, aff[:, g, :], -1.0).then_inc(s_k, 1)
                    at += 2
                    dve.wait_ge(s_k, at)
            nc.vector.tensor_copy(idx[:, :, :], idx_u[:, :, :]).then_inc(s_k, 1)


def gather(nc, env, consts, idx, val, XG, slot_idx, slot_val):
    X = env["X"]
    ident = env["ident"]
    with ExitStack() as ctx:
        def sb(name, shape, dt=F32):
            return ctx.enter_context(nc.sbuf_tensor("g_" + name, shape, dt))

        def ps(name, shape):
            return ctx.enter_context(nc.psum_tensor("g_" + name, shape, F32))

        sems, every = [], []

        def sem(name, counted=True):
            s = ctx.enter_context(nc.semaphore("g_" + name))
            every.append(s)
            if counted:
                sems.append(s)
            return s

        sel_f = sb("sel_f", [P, BG])
        sel = sb("sel", [P, BG, P], BF16)
        own = sb("own", [P, EX])
        token = sb("token", [P, NT])
        diag = sb("diag", [P, EG, EX, CAP], BF16)
        wide = sb("wide", [P, EG, EX, CAP])
        xs = sb("xs", [P, 2, NT, C])
        hot = sb("hot", [P, 2, NT, EX * CAP])
        pI = ps("pI", [P, 2, 512])
        pG = ps("pG", [P, 2, 512])
        pT = ps("pT", [P, 2, 2, P])
        s_c = sem("loaded", False)
        s_wide = sem("idx_widened", False)
        s_sel = sem("selectors_made", False)
        s_T = sem("idx_turned", False)
        s_xs = sem("x_staged")
        s_I = sem("idx_spread")
        s_hot = sem("one_hot_made")
        s_G = sem("gathered")
        s_XG = sem("gathered_copied")
        s_held = sem("waits_passed", False)
        ctx.callback(clear_semaphores, nc, every)
        block = ctx.enter_context(nc.Block())

        @block.sync
        def _(sp):
            sp.dma_start(sel_f[:, :], consts["row_sequence"]).then_inc(s_c, 16)
            sp.dma_start(own[:, :], consts["row_expert"]).then_inc(s_c, 16)
            sp.dma_start(token[:, :], consts["token"]).then_inc(s_c, 16)

        @block.gpsimd
        def _(pool):
            for s in sems:
                pool.sem_inc(s, START)
            with pool.Fori(0, NB // 2) as i:
                for u in range(2):
                    b = 2 * i + u
                    after(pool, s_G, b - 1)
                    held(pool, s_held)
                    nc.gpsimd.tensor_copy(xs[:, u, :, :], X[:, bass.ds(NT * b, NT), :]).then_inc(s_xs, 1)

        @block.tensor
        def _(pe):
            for g in range(EG):
                for n, src in enumerate((idx, val)):
                    last = nc.tensor.transpose(pT[0:CAP, g, n, :], src[:, g, :], ident[:, :])
            last.then_inc(s_T, 1)
            pe.wait_ge(s_sel, 2)
            for g in range(EG):
                with pe.Fori(0, BG // 2) as i:
                    for u in range(2):
                        bb = 2 * i + u
                        b = g * BG + bb
                        after(pe, s_hot, b - 1)
                        nc.tensor.matmul(pI[:, u, :], sel[:, bass.ds(bb, 1), :].rearrange("p o n -> p (o n)"),
                                         diag[:, g, :, :], start=True, stop=True).then_inc(s_I, 1)
                        after(pe, s_hot, b + 1)
                        after(pe, s_xs, b + 1)
                        after(pe, s_XG, b - 1)
                        for j in range(NT):
                            last = nc.tensor.matmul(pG[:, u, :], xs[:, u, j, :], hot[:, u, j, :],
                                                    start=(j == 0), stop=(j == NT - 1))
                        last.then_inc(s_G, 1)

        @block.vector
        def _(dve):
            dve.wait_ge(s_c, 48)
            for g in range(EG):
                nc.vector.tensor_tensor(diag[:, g, :, :], bcast(idx[:, g, :], 1, EX), bcast(own[:, :], 2, CAP),
                                        ALU.mult)
            nc.vector.memset(wide[:, 0, :, :], 1.0).then_inc(s_wide, 1)
            dve.wait_ge(s_wide, 1)
            for bb in range(BG):
                last = nc.vector.tensor_scalar(sel[:, bb, :], wide[:, 0, 0:P // CAP, :].rearrange("p e s -> p (e s)"),
                                               sel_f[:, bb:bb + 1], None, ALU.mult)
            last.then_inc(s_sel, 2)
            dve.wait_ge(s_T, 1)
            for g in range(EG):
                for n, dst in enumerate((slot_idx, slot_val)):
                    t = pT[0:CAP, g, n, :].rearrange("p (b q k) -> p b q k", b=BG, k=4)
                    for k in range(4):
                        nc.vector.tensor_copy(dst[CAP * k:CAP * (k + 1), g * BG:(g + 1) * BG, :], t[:, :, :, k])
            with dve.Fori(0, NB // 2) as i:
                for u in range(2):
                    b = 2 * i + u
                    after(dve, s_I, b + 1)
                    after(dve, s_G, b - 1)
                    for j in range(NT):
                        last = nc.vector.tensor_scalar(hot[:, u, j, :], pI[:, u, :], token[:, j:j + 1], None,
                                                       ALU.is_equal)
                    last.then_inc(s_hot, 1)

        @block.scalar
        def _(act):
            with act.Fori(0, NB // 2) as i:
                for u in range(2):
                    b = 2 * i + u
                    after(act, s_G, b + 1)
                    nc.scalar.copy(XG[:, :, bass.ds(b * CAP, CAP)],
                                   pG[:, u, :].rearrange("p (e s) -> p e s", e=EX)).then_inc(s_XG, 1)


def experts(nc, env, weights, XG, Y):
    KF = FF // P
    NTK = NB * CAP // P
    ident = env["ident"]
    with ExitStack() as ctx:
        def sb(name, shape, dt=F32):
            return ctx.enter_context(nc.sbuf_tensor("e_" + name, shape, dt))

        def ps(name, shape):
            return ctx.enter_context(nc.psum_tensor("e_" + name, shape, F32))

        sems, every = [], []

        def sem(name, counted=True):
            s = ctx.enter_context(nc.semaphore("e_" + name))
            every.append(s)
            if counted:
                sems.append(s)
            return s

        w1 = sb("w1", [P, 2, FF])
        w2 = sb("w2", [P, 2, KF, C])
        b2 = sb("b2", [P, 2, C])
        b1r = sb("b1r", [EX * KF, P])
        b1 = sb("b1", [P, EX * KF])
        b1e = sb("b1e", [P, 2, KF])
        hT = sb("hT", [P, 2, KF, NB * CAP])
        ye = sb("ye", [P, 2, NTK, C])
        pH = ps("pH", [P, 4, 512])
        pY = ps("pY", [P, 2, 512])
        pB = ps("pB", [P, 512])
        s_b = sem("b1_loaded", False)
        s_bT = sem("b1_turned", False)
        s_bc = sem("b1_copied", False)
        s_w = [sem(f"weights_loaded{u}", False) for u in range(2)]
        s_be = sem("expert_bias")
        s_h = sem("hidden")
        s_g = sem("gelu_done")
        s_y = sem("out_made")
        s_ye = sem("out_copied")
        s_Y = [sem(f"out_moved{u}", False) for u in range(2)]
        s_init = sem("init", False)
        ctx.callback(clear_semaphores, nc, every)
        block = ctx.enter_context(nc.Block())

        @block.sync
        def _(sp):
            sp.dma_start(b1r[:, :], weights["b1"].rearrange("e (k p) -> (e k) p", p=P)).then_inc(s_b, 16)

            def load(e, u):
                after(sp, s_y, e - 1)
                sp.dma_start(w1[:, u, :], weights["w1"][bass.ds(e, 1)].rearrange("o d f -> d (o f)")
                             ).then_inc(s_w[u], 16)
                sp.dma_start(w2[:, u, :, :], weights["w2"][bass.ds(e, 1)].rearrange("o (k p) d -> p (o k) d", p=P)
                             ).then_inc(s_w[u], 16)
                after(sp, s_ye, e - 1)
                sp.dma_start(b2[:, u, :], weights["b2"][bass.ds(e, 1)].broadcast_to([P, C])).then_inc(s_w[u], 16)

            def move(q, r):
                after(sp, s_ye, 4 * q + r + 1)
                for g in range(4):
                    sp.dma_start(
                        Y[CAP * r:CAP * (r + 1), bass.ds(q, 1), :, :]
                        .rearrange("p o (k g) c -> p (o k) g c", g=4)[:, :, g, :],
                        ye[CAP * g:CAP * (g + 1), r % 2, :, :]).then_inc(s_Y[r % 2], 16)

            def four(q, first):
                for r in range(4):
                    load(4 * q + r, r % 2)
                    if not (first and r == 0):
                        move(q if r else q - 1, (r - 1) % 4)

            four(0, True)
            with sp.Fori(1, EX // 4) as q:
                four(q, False)
            move(EX // 4 - 1, 3)
            for u in range(2):
                sp.wait_ge(s_Y[u], 64 * EX // 2 + START)

        @block.gpsimd
        def _(pool):
            for s in sems + s_Y:
                pool.sem_inc(s, START)

        @block.tensor
        def _(pe):
            pe.wait_ge(s_b, 16)
            nc.tensor.transpose(pB[:, 0:EX * KF], b1r[:, :], ident[0:EX * KF, 0:EX * KF]).then_inc(s_bT, 1)

            def hidden(e, i, u):
                pe.wait_ge(s_w[u], 48 * (i + 1))
                for k in range(KF):
                    after(pe, s_g, KF * (e - 1) + k + 1)
                    nc.tensor.matmul(pH[:, k, :], w1[:, u, k * P:(k + 1) * P],
                                     XG[:, bass.ds(e, 1), :].rearrange("p o t -> p (o t)"),
                                     start=True, stop=True).then_inc(s_h, 1)

            def outputs(e, u):
                after(pe, s_g, KF * e + KF)
                after(pe, s_ye, e - 1)
                for t in range(NTK):
                    for k in range(KF):
                        last = nc.tensor.matmul(pY[:, u, t * C:(t + 1) * C], hT[:, u, k, t * P:(t + 1) * P],
                                                w2[:, u, k, :], start=(k == 0), stop=(k == KF - 1))
                last.then_inc(s_y, 1)

            with pe.Fori(0, EX // 2) as i:
                for u in range(2):
                    hidden(2 * i + u, i, u)
                    outputs(2 * i + u, u)

        @block.scalar
        def _(act):
            act.wait_ge(s_bc, 1)
            with act.Fori(0, EX // 2) as i:
                for u in range(2):
                    e = 2 * i + u
                    nc.scalar.copy(b1e[:, u, :], b1[:, bass.ds(KF * e, KF)]).then_inc(s_be, 1)
                    after(act, s_be, e + 1)
                    after(act, s_y, e - 1)
                    for k in range(KF):
                        after(act, s_h, KF * e + k + 1)
                        nc.scalar.activation(hT[:, u, k, :], pH[:, k, :], ACT.Gelu_apprx_tanh,
                                             bias=b1e[:, u, k:k + 1]).then_inc(s_g, 1)

        @block.vector
        def _(dve):
            dve.wait_ge(s_bT, 1)
            nc.vector.tensor_copy(b1[:, :], pB[:, 0:EX * KF]).then_inc(s_bc, 1)
            with dve.Fori(0, EX // 2) as i:
                for u in range(2):
                    e = 2 * i + u
                    after(dve, s_y, e + 1)
                    dve.wait_ge(s_w[u], 48 * (i + 1))
                    dve.wait_ge(s_Y[u], 64 * i + START)
                    nc.vector.tensor_tensor(ye[:, u, :, :], pY[:, u, :].rearrange("p (t c) -> p t c", t=NTK),
                                            bcast(b2[:, u, :], 1, NTK), ALU.add).then_inc(s_ye, 1)


def scatter(nc, env, consts, slot_idx, slot_val, Y):
    X, neghalf = env["X"], env["neghalf"]
    Q = EX // 4
    DVE_STEPS = 5
    with ExitStack() as ctx:
        def sb(name, shape, dt=F32):
            return ctx.enter_context(nc.sbuf_tensor("s_" + name, shape, dt))

        sems, every = [], []

        def sem(name, counted=True):
            s = ctx.enter_context(nc.semaphore("s_" + name))
            every.append(s)
            if counted:
                sems.append(s)
            return s

        iota = sb("iota", [P, T])
        sib = sb("sib", [P, 2, Q])
        svb = sb("svb", [P, 2, Q])
        hot = sb("hot", [P, 2, Q, T])
        z = sb("z", [P, NT, C])
        st = sb("st", [P, NT, 6])
        mv = sb("mv", [P, NT, 2])
        rstd = sb("rstd", [P, NT])
        pO = ctx.enter_context(nc.psum_tensor("s_pO", [P, 2, 512], F32))
        s_c = sem("loaded", False)
        s_s = sem("slots_staged")
        s_hot = sem("gates_placed")
        s_O = sem("scattered")
        s_z = sem("summed")
        s_mv = sem("stats_made")
        s_rstd = sem("rstd_made")
        s_x = sem("x_written")
        s_dve = sem("dve_steps")
        s_held = sem("waits_passed", False)
        ctx.callback(clear_semaphores, nc, every)
        block = ctx.enter_context(nc.Block())

        @block.sync
        def _(sp):
            sp.dma_start(iota[:, :], consts["iota"]).then_inc(s_c, 16)

        @block.gpsimd
        def _(pool):
            for s in sems:
                pool.sem_inc(s, START)

            def one(b, u, nxt):
                after(pool, s_mv, b + 1)
                nc.gpsimd.tensor_tensor(rstd[:, :], mv[:, :, 1], neghalf[:, 0:NT], ALU.pow).then_inc(s_rstd, 1)
            looped(pool, one)

        @block.scalar
        def _(act):
            def stage(q, u):
                after(act, s_hot, q - 1)
                nc.scalar.copy(sib[:, u, :], slot_idx[:, bass.ds(q, 1), :].rearrange("p o q -> p (o q)"))
                nc.scalar.copy(svb[:, u, :], slot_val[:, bass.ds(q, 1), :].rearrange("p o q -> p (o q)")
                               ).then_inc(s_s, 1)
            stage(0, 0)
            looped(act, lambda b, u, nxt: stage(nxt[0], nxt[2]) if nxt else None)

        @block.tensor
        def _(pe):
            def one(b, u, nxt):
                after(pe, s_hot, b + 1)
                after(pe, s_z, b - 1)
                for j in range(NT):
                    for q in range(Q):
                        last = nc.tensor.matmul(
                            pO[:, u, j * C:(j + 1) * C], hot[:, u, q, j * P:(j + 1) * P],
                            Y[:, q, bass.ds(b, 1), :].rearrange("p o c -> p (o c)"),
                            start=(q == 0), stop=(q == Q - 1))
                last.then_inc(s_O, 1)
            looped(pe, one)

        @block.vector
        def _(dve):
            steps = Steps(dve, s_dve, DVE_STEPS, s_held)
            dve.wait_ge(s_c, 16)

            def place(q, u):
                after(dve, s_s, q + 1)
                after(dve, s_O, q - 1)
                for k in range(Q):
                    last = nc.vector.tensor_scalar(hot[:, u, k, :], iota[:, :], sib[:, u, k:k + 1],
                                                   svb[:, u, k:k + 1], ALU.is_equal, ALU.mult)
                last.then_inc(s_hot, 1)

            def one(b, u, nxt):
                steps.start(b)
                if nxt:
                    place(nxt[0], nxt[2])
                after(dve, s_O, b + 1)
                nc.vector.tensor_tensor(z[:, :, :], pO[:, u, 0:T].rearrange("p (j c) -> p j c", j=NT),
                                        X[:, bass.ds(NT * b, NT), :], ALU.add).then_inc(s_z, 1)
                after(dve, s_z, b + 1)
                for j in range(NT):
                    steps.inc(nc.vector.bn_stats(st[:, j, :], z[:, j, :]))
                after(dve, s_dve, steps.base + steps.count)
                held(dve, s_held)
                for j in range(NT):
                    steps.inc(nc.vector.bn_aggr(mv[:, j, :], st[:, j, :]))
                after(dve, s_dve, steps.base + steps.count)
                steps.inc(nc.vector.tensor_scalar(mv[:, :, 1], mv[:, :, 1], LN_EPS, None, ALU.add))
                after(dve, s_dve, steps.base + steps.count)
                dve.sem_inc(s_mv, 1)
                after(dve, s_rstd, b + 1)
                for j in range(NT):
                    last = nc.vector.tensor_scalar(
                        X[:, bass.ds(NT * b + j, 1), :].rearrange("p o c -> p (o c)"), z[:, j, :],
                        mv[:, j, 0:1], rstd[:, j:j + 1], ALU.subtract, ALU.mult)
                last.then_inc(s_x, 1)
                after(dve, s_x, b + 1)
                held(dve, s_held)
                steps.end()

            place(0, 0)
            looped(dve, one)


def l0_experts(nc, env, weights, consts):
    with ExitStack() as ctx:
        def sb(name, shape):
            return ctx.enter_context(nc.sbuf_tensor("m_" + name, shape, F32))

        idx = sb("idx", [P, EG, CAP])
        val = sb("val", [P, EG, CAP])
        slot_idx = sb("slot_idx", [P, NB, EX // 4])
        slot_val = sb("slot_val", [P, NB, EX // 4])
        XG = sb("XG", [P, EX, NB * CAP])
        Y = sb("Y", [P, EX // 4, NB, C])
        router(nc, env, weights, consts, idx, val)
        gather(nc, env, consts, idx, val, XG, slot_idx, slot_val)
        experts(nc, env, weights, XG, Y)
        scatter(nc, env, consts, slot_idx, slot_val, Y)


def l1_attention(nc, env, weights, consts):
    LOOK, START = 32, 64
    KW = LOOK + P
    SCALE = 1.0 / np.sqrt(C)
    TAKEN = -3.0e38
    DVE_STEPS = 16
    ident, X, neghalf = env["ident"], env["X"], env["neghalf"]
    with ExitStack() as ctx:
        def sb(name, shape, dt=F32):
            return ctx.enter_context(nc.sbuf_tensor("c_" + name, shape, dt))

        def ps(name, shape):
            return ctx.enter_context(nc.psum_tensor("c_" + name, shape, F32))

        sems, every = [], []

        def sem(name, counted=True):
            s = ctx.enter_context(nc.semaphore("c_" + name))
            every.append(s)
            if counted:
                sems.append(s)
            return s

        raw = sb("raw", [P, 5, C])
        wT = sb("wT", [P, 5, C])
        bias = sb("bias", [P, 3])
        vbias = sb("vbias", [P, 2, C])
        prefix = sb("prefix", [P, P])
        mask = sb("mask", [P, 2, KW])
        prev = sb("prev", [P, KW])
        notfirst = sb("notfirst", [P, NT])
        xs = sb("xs", [P, 2, NT, C])
        xT = sb("xT", [P, 2, T])
        qT = sb("qT", [P, 2, 3, T])
        v = sb("v", [P, 2, NT, 2, C])
        vp = sb("vp", [LOOK, 2, 2, C])
        S = sb("S", [P, NT, 2, KW])
        B = sb("B", [P, NT, KW])
        best = sb("best", [P, NT, 2, 8])
        E = sb("E", [P, NT, 2, KW])
        pick = sb("pick", [P, NT, 2, KW])
        Wt = sb("Wt", [P, NT, 2, KW])
        WT = sb("WT", [P, NT, 2 * P + 2 * LOOK])
        mx = sb("mx", [P, NT])
        nmx = sb("nmx", [P, NT])
        rs = sb("rs", [P, NT])
        ri = sb("ri", [P, NT])
        z = sb("z", [P, NT, C])
        st = sb("st", [P, NT, 6])
        mv = sb("mv", [P, NT, 2])
        rstd = sb("rstd", [P, NT])

        pX = ps("pX", [P, 512])
        pQ = ps("pQ", [P, 512])
        pK = ps("pK", [P, 512])
        pV = ps("pV", [P, 512])
        pS = ps("pS", [P, 2, 512])
        pT = ps("pT", [P, 512])
        pO = ps("pO", [P, 512])

        s_c = sem("constants_loaded", False)
        s_w = sem("weights_turned", False)
        s_wc = sem("weights_copied", False)
        s_one = sem("pick_set", False)
        s_xs = sem("x_staged")
        s_xTp = sem("x_turned")
        s_xT = sem("xT_copied")
        s_proj = sem("projected")
        s_q = sem("q_k_copied")
        s_pk = sem("pk_copied")
        s_v = sem("v_copied")
        s_S = sem("scored")
        s_m = sem("maxed")
        s_nm = sem("max_negated")
        s_E = sem("exped")
        s_W = sem("weights_made")
        s_T = sem("wts_turned")
        s_WT = sem("wts_copied")
        s_PV = sem("pv_done")
        s_z = sem("summed")
        s_mv = sem("stats_made")
        s_rstd = sem("rstd_made")
        s_x = sem("x_written")
        s_dve = sem("dve_steps")
        s_held = sem("waits_passed", False)
        ctx.callback(clear_semaphores, nc, every)
        block = ctx.enter_context(nc.Block())

        def after(eng, s, value):
            eng.wait_ge(s, value + START)

        NAMES = ["q", "k", "pk", "v", "pv"]

        @block.sync
        def _(sp):
            for n, name in enumerate(NAMES):
                sp.dma_start(raw[:, n, :], weights[name + "_w"]).then_inc(s_c, 16)
            for n, name in enumerate(NAMES[:3]):
                sp.dma_start(bias[:, n:n + 1], weights[name + "_b"].rearrange("(p o) -> p o", o=1)).then_inc(s_c, 16)
            for n, name in enumerate(NAMES[3:]):
                sp.dma_start(vbias[:, n, :], weights[name + "_b"].rearrange("(o p) -> o p", o=1)
                             .broadcast_to([P, C])).then_inc(s_c, 16)
            sp.dma_start(prefix[:, :], consts["prefix"]).then_inc(s_c, 16)
            sp.dma_start(mask[:, :, :], consts["look_mask"].rearrange("p (t k) -> p t k", t=2)).then_inc(s_c, 16)
            sp.dma_start(prev[:, :], consts["prev"]).then_inc(s_c, 16)
            sp.dma_start(notfirst[:, :], consts["notfirst"]).then_inc(s_c, 16)
        N_C = 16 * 14

        @block.gpsimd
        def _(pool):
            for s in sems:
                pool.sem_inc(s, START)
            nc.gpsimd.memset(pick[:, :, 1, :], 1.0).then_inc(s_one, 1)

            def stage(q, u):
                after(pool, s_xTp, q - 1)
                held(pool, s_held)
                nc.gpsimd.tensor_copy(xs[:, u, :, :], X[:, bass.ds(NT * q, NT), :]).then_inc(s_xs, 1)

            def one(b, u, nxt):
                if nxt:
                    stage(nxt[0], nxt[2])
                after(pool, s_mv, b + 1)
                nc.gpsimd.tensor_tensor(rstd[:, :], mv[:, :, 1], neghalf[:, 0:NT], ALU.pow).then_inc(s_rstd, 1)

            stage(0, 0)
            looped(pool, one)

        @block.tensor
        def _(pe):
            pe.wait_ge(s_c, N_C)
            for n in range(5):
                if n >= 4:
                    pe.wait_ge(s_wc, n - 3)
                nc.tensor.transpose((pX, pQ, pK, pV)[n % 4][:, 0:C], raw[:, n, :], ident[:, :]).then_inc(s_w, 1)
            pe.wait_ge(s_wc, 5)

            def turn_x(q, u):
                after(pe, s_xs, q + 1)
                after(pe, s_xT, q)
                for j in range(NT):
                    nc.tensor.transpose(pX[:, j * P:(j + 1) * P], xs[:, u, j, :], ident[:, :])
                for j in range(NT):
                    last = nc.tensor.matmul(pX[:, T + j * P:T + (j + 1) * P], xs[:, u, j, :], prefix[:, :],
                                            start=True, stop=True)
                last.then_inc(s_xTp, 1)

            def project(q):
                after(pe, s_xT, q + 1)
                after(pe, s_q, 2 * q)
                for n in range(2):
                    last = nc.tensor.matmul(pQ[:, n * T:(n + 1) * T], wT[:, n, :], xT[:, 0, :], start=True, stop=True)
                last.then_inc(s_proj, 1)
                after(pe, s_pk, q)
                nc.tensor.matmul(pK[:, 0:T], wT[:, 2, :], xT[:, 1, :], start=True, stop=True)
                for n in range(2):
                    last = nc.tensor.matmul(pK[0:LOOK, T + n * C:T + (n + 1) * C], xT[:, n, P - LOOK:P],
                                            wT[:, 3 + n, :], start=True, stop=True)
                last.then_inc(s_proj, 1)
                after(pe, s_v, q)
                for j in range(NT):
                    for n in range(2):
                        last = nc.tensor.matmul(pV[:, (2 * j + n) * C:(2 * j + n + 1) * C],
                                                xT[:, n, j * P:(j + 1) * P], wT[:, 3 + n, :], start=True, stop=True)
                last.then_inc(s_proj, 1)

            def scores(b, u, j):
                if j == 0:
                    after(pe, s_q, 2 * b + 2)
                    after(pe, s_pk, b + 1)
                after(pe, s_m, 2 * b + j - 1)
                o = LOOK * (1 - j)
                lo = 0 if j == 0 else P - LOOK
                for n in range(2):
                    last = nc.tensor.matmul(pS[:, j, n * KW + o:(n + 1) * KW], qT[:, u, 0, j * P:(j + 1) * P],
                                            qT[:, u, 1 + n, lo:(j + 1) * P], start=True, stop=True)
                last.then_inc(s_S, 1)

            def mix(b, u, j):
                after(pe, s_W, 2 * b + j + 1)
                after(pe, s_WT, 2 * b + j)
                for n in range(2):
                    last = nc.tensor.transpose(pT[:, n * P:(n + 1) * P], Wt[:, j, n, LOOK:KW], ident[:, :])
                if j:
                    for n in range(2):
                        o = 2 * P + n * LOOK
                        last = nc.tensor.transpose(pT[0:LOOK, o:o + LOOK], Wt[0:LOOK, j, n, 0:LOOK],
                                                   ident[0:LOOK, 0:LOOK])
                last.then_inc(s_T, 1)
                after(pe, s_WT, 2 * b + j + 1)
                if j == 0:
                    after(pe, s_v, b + 1)
                    after(pe, s_z, b)
                out = pO[:, j * C:(j + 1) * C]
                for n in range(2):
                    last = nc.tensor.matmul(out, WT[:, j, n * P:(n + 1) * P], v[:, u, j, n, :],
                                            start=(n == 0), stop=(n == 1))
                if j:
                    for n in range(2):
                        o = 2 * P + n * LOOK
                        last = nc.tensor.matmul(out[0:LOOK, :], WT[0:LOOK, j, o:o + LOOK], vp[:, u, n, :],
                                                start=False, stop=True, skip_group_check=True)
                last.then_inc(s_PV, 1)

            def one(b, u, nxt):
                if nxt:
                    turn_x(nxt[0], nxt[2])
                scores(b, u, 0)
                scores(b, u, 1)
                if nxt:
                    project(nxt[0])
                mix(b, u, 0)
                mix(b, u, 1)

            turn_x(0, 0)
            project(0)
            looped(pe, one)

        @block.scalar
        def _(act):
            act.wait_ge(s_c, N_C)

            def copy_x(q):
                after(act, s_proj, 3 * q)
                after(act, s_xTp, q + 1)
                nc.scalar.copy(xT[:, :, :].rearrange("p n t -> p (n t)"), pX[:, :]).then_inc(s_xT, 1)

            def copy_q(q, u):
                after(act, s_S, 2 * (q - 1))
                after(act, s_proj, 3 * q + 1)
                for n in range(2):
                    nc.scalar.activation(qT[:, u, n, :], pQ[:, n * T:(n + 1) * T], ACT.Identity,
                                         bias=bias[:, n:n + 1]).then_inc(s_q, 1)

            def exps(b, j):
                after(act, s_nm, 2 * b + j + 1)
                after(act, s_W, 2 * b + j - 1)
                o = LOOK * (1 - j)
                nc.scalar.activation(E[:, j, :, o:KW], S[:, j, :, o:KW], ACT.Exp, bias=nmx[:, j:j + 1]
                                     ).then_inc(s_E, 1)

            def copy_weights(b, j):
                after(act, s_T, 2 * b + j + 1)
                after(act, s_PV, 2 * b + j - 1)
                last = nc.scalar.copy(WT[:, j, 0:2 * P], pT[:, 0:2 * P])
                if j:
                    last = nc.scalar.copy(WT[0:LOOK, j, 2 * P:], pT[0:LOOK, 2 * P:2 * P + 2 * LOOK])
                last.then_inc(s_WT, 1)

            def one(b, u, nxt):
                if nxt:
                    copy_x(nxt[0])
                exps(b, 0)
                if nxt:
                    copy_q(nxt[0], nxt[2])
                exps(b, 1)
                copy_weights(b, 0)
                copy_weights(b, 1)

            copy_x(0)
            copy_q(0, 0)
            looped(act, one)

        @block.vector
        def _(dve):
            steps = Steps(dve, s_dve, DVE_STEPS, s_held)

            def linked(ins):
                steps.inc(ins)
                after(dve, s_dve, steps.base + steps.count)
                held(dve, s_held)

            dve.wait_ge(s_c, N_C)
            for n in range(5):
                dve.wait_ge(s_w, n + 1)
                nc.vector.tensor_copy(wT[:, n, :], (pX, pQ, pK, pV)[n % 4][:, 0:C]).then_inc(s_wc, 1)
            dve.wait_ge(s_one, 1)

            def copy_pk_v(q, u):
                after(dve, s_PV, 2 * (q - 1))
                after(dve, s_proj, 3 * q + 2)
                nc.vector.tensor_scalar(qT[:, u, 2, :], pK[:, 0:T], bias[:, 2:3], None, ALU.add)
                nc.vector.tensor_tensor(vp[:, u, :, :], pK[0:LOOK, T:2 * T].rearrange("p (n c) -> p n c", n=2),
                                        vbias[0:LOOK, :, :], ALU.add).then_inc(s_pk, 1)
                after(dve, s_proj, 3 * q + 3)
                nc.vector.tensor_tensor(v[:, u, :, :, :].rearrange("p j n c -> p j (n c)"),
                                        pV[:, :].rearrange("p (j nc) -> p j nc", j=NT),
                                        bcast(vbias[:, :, :].rearrange("p n c -> p (n c)"), 1, NT), ALU.add
                                        ).then_inc(s_v, 1)

            def best_16(b, j):
                o = LOOK * (1 - j)
                after(dve, s_E, 2 * b + j - 1)
                after(dve, s_S, 2 * b + j + 1)
                held(dve, s_held)
                nc.vector.tensor_tensor_reduce(
                    out=S[:, j, :, o:KW], in0=pS[:, j, 0:2 * KW].rearrange("p (n k) -> p n k", n=2)[:, :, o:KW],
                    in1=mask[:, :, o:KW], scale=SCALE, scalar=-HUGE, op0=ALU.add, op1=ALU.max,
                    accum_out=mx[:, j:j + 1]).then_inc(s_m, 1)
                after(dve, s_m, 2 * b + j + 1)
                nc.vector.tensor_scalar(nmx[:, j:j + 1], mx[:, j:j + 1], -1.0, None, ALU.mult).then_inc(s_nm, 1)
                linked(nc.vector.max(best[:, j, 0, :], S[:, j, 0, o:KW]))
                linked(nc.vector.match_replace(B[:, j, o:KW], best[:, j, 0, :], S[:, j, 0, o:KW], TAKEN))
                linked(nc.vector.max(best[:, j, 1, :], B[:, j, o:KW]))
                linked(nc.vector.match_replace(B[:, j, o:KW], best[:, j, 1, :], B[:, j, o:KW], TAKEN))
                nc.vector.scalar_tensor_tensor(pick[:, j, 0, o:KW], B[:, j, o:KW], -2.0e38, prev[:, o:KW],
                                               ALU.is_lt, ALU.add).then_inc(s_dve, 1)
                steps.count += 1

            def make_weights(b, j):
                o = LOOK * (1 - j)
                after(dve, s_T, 2 * b + j - 1)
                after(dve, s_dve, steps.base + 5 * (j + 1))
                after(dve, s_E, 2 * b + j + 1)
                held(dve, s_held)
                nc.vector.tensor_tensor_reduce(
                    out=Wt[:, j, :, o:KW], in0=pick[:, j, :, o:KW], in1=E[:, j, :, o:KW], scale=1.0, scalar=0.0,
                    op0=ALU.mult, op1=ALU.add, accum_out=rs[:, j:j + 1]).then_inc(s_W, 1)

            def tail(b, u):
                after(dve, s_W, 2 * b + 2)
                linked(nc.vector.reciprocal(ri[:, :], rs[:, :]))
                linked(nc.vector.tensor_tensor(ri[:, :], ri[:, :], notfirst[:, :], ALU.mult))
                after(dve, s_PV, 2 * b + 2)
                for j in range(NT):
                    last = nc.vector.scalar_tensor_tensor(
                        z[:, j, :], pO[:, j * C:(j + 1) * C], ri[:, j:j + 1],
                        X[:, bass.ds(NT * b + j, 1), :].rearrange("p o c -> p (o c)"), ALU.mult, ALU.add)
                last.then_inc(s_z, 1)
                after(dve, s_z, b + 1)
                for j in range(NT):
                    steps.inc(nc.vector.bn_stats(st[:, j, :], z[:, j, :]))
                after(dve, s_dve, steps.base + steps.count)
                held(dve, s_held)
                for j in range(NT):
                    steps.inc(nc.vector.bn_aggr(mv[:, j, :], st[:, j, :]))
                after(dve, s_dve, steps.base + steps.count)
                nc.vector.tensor_scalar(mv[:, :, 1], mv[:, :, 1], LN_EPS, None, ALU.add).then_inc(s_mv, 1)
                after(dve, s_rstd, b + 1)
                for j in range(NT):
                    last = nc.vector.tensor_scalar(
                        X[:, bass.ds(NT * b + j, 1), :].rearrange("p o c -> p (o c)"), z[:, j, :],
                        mv[:, j, 0:1], rstd[:, j:j + 1], ALU.subtract, ALU.mult)
                last.then_inc(s_x, 1)
                after(dve, s_x, b + 1)
                held(dve, s_held)

            def one(b, u, nxt):
                steps.start(b)
                best_16(b, 0)
                if nxt:
                    copy_pk_v(nxt[0], nxt[2])
                best_16(b, 1)
                make_weights(b, 0)
                make_weights(b, 1)
                tail(b, u)
                steps.end()

            copy_pk_v(0, 0)
            looped(dve, one)


def l1_network(nc, env, weights, consts):
    LAYERS, H, D, W = 6, 16, 64, 32
    I = H * D
    F = 341
    FC = [(0, P), (P, P), (2 * P, F - 2 * P)]
    KW = W + P
    NU, START, GR = 16, 64, 2
    NG = NB // GR
    TG = GR * NT
    NORM_STEPS = 13
    ident, X, neghalf = env["ident"], env["X"], env["neghalf"]

    def heads(n):
        h = 8 * (n % 8 // 4) + 4 * (n % 4 // 2) + n % 2
        return h, h + 2

    OWN = {11: [("o", 0)], 15: [("o", 1)], 19: [("o", 2)], 23: [("o", 3)], 25: [("y", 0)]}
    NEXT = {0: [("x", 0)]}
    for kind, at in (("qk", (1, 2, 3, 5, 6, 8, 10, 11)), ("v", (4, 7, 12, 13)),
                     ("turn", (11, 12, 13, 13, 14, 14, 15, 15))):
        for c, n in enumerate(at):
            NEXT.setdefault(n, []).append((kind, c))
    EXP_LAG, TURN_LAG, WEIGH_LAG, NORM_LAG, END = 1, 3, 5, 6, 26

    def place(c):
        return 1 - c // 4, c // 2 % 2, c % 2

    def slots(prev, nxt):
        before = [("turn", 6, 0), ("turn", 7, 0)]
        at = 0 if prev else 1
        out = {}
        for n in range(NU if nxt else END):
            out[n] = []
            for d, there, uses in ((-1, prev, OWN.get(n + NU, [])), (0, True, OWN.get(n, [])),
                                   (1, nxt, NEXT.get(n, []))):
                for kind, c in uses if there else []:
                    out[n].append((kind, c, d, at % 2, before[-2]))
                    before.append((kind, c, d))
                    at += 1
        assert not nxt or at % 2 == 0
        return out

    def lagged(N, u, n, lag, prev):
        m = n - lag
        if m < 0:
            return [(N - 1, 1 - u, m + NU)] if prev else []
        return [(N, u, m)] if m < NU else []

    PROLOGUE = [("x", 0)] + [("qk", c) for c in range(8)] + [("v", c) for c in range(4)] + \
        [("turn", k) for k in range(8)]

    with ExitStack() as ctx:
        def sb(name, shape, dt=F32):
            return ctx.enter_context(nc.sbuf_tensor("n_" + name, shape, dt))

        def ps(name, shape):
            return ctx.enter_context(nc.psum_tensor("n_" + name, shape, F32))

        sems, every = [], []

        def sem(name, counted=True):
            s = ctx.enter_context(nc.semaphore("n_" + name))
            every.append(s)
            if counted:
                sems.append(s)
            return s

        wqkv = sb("wqkv", [P, 3 * I])
        wo = sb("wo", [P, I // P, C])
        qks = sb("qks", [P, 2, D])
        w1 = sb("w1", [P, 2 * F])
        w2 = sb("w2", [P, 3, C])
        b1 = sb("b1", [P, 2, 3])
        lng = sb("lng", [P, 1])
        lnb = sb("lnb", [P, 1])
        b2 = sb("b2", [P, C])
        cos_c = sb("cos_c", [P, 2, NT, D])
        sin_c = sb("sin_c", [P, 2, NT, D])
        cosT = sb("cosT", [P, 2, NT, D])
        sinT = sb("sinT", [P, 2, NT, D])
        band = sb("band", [P, KW])
        xs = sb("xs", [P, 2, NT, C])
        xT = sb("xT", [P, T + 1])
        sq = sb("sq", [P, 2, 512])
        t1 = sb("t1", [P, 4, 512])
        t2 = sb("t2", [P, 4, 512])
        ss = sb("ss", [P, 2, 2, NT, H])
        rn = sb("rn", [P, 2, 2, NT, H])
        nt = sb("nt", [P, NT * H])
        pre = sb("pre", [P, NT, 2, I])
        qkT = sb("qkT", [P, 2, 2, I // P, T])
        V = sb("V", [P, 2, NT, I])
        vp = sb("vp", [W, 2, I])
        S = sb("S", [P, 4, 2, KW])
        E = sb("E", [P, 4, 2, KW])
        ET = sb("ET", [P, 4, 2 * P + 2 * W])
        nm = sb("nm", [P, 2, NT, H])
        rs = sb("rs", [P, 2, NT, H])
        ri = sb("ri", [P, 8])
        On = sb("On", [P, NT, I])
        OT = sb("OT", [P, NT, I // P, P])
        fxs = sb("fxs", [P, TG, C])
        fsT = sb("fsT", [P, GR, T + 1])
        xn = sb("xn", [P, TG, C])
        xnT = sb("xnT", [P, TG * P])
        gate = sb("gate", [P, 2, TG * P])
        hT = sb("hT", [P, 3, TG * P])
        st = sb("st", [P, TG, 6])
        mv = sb("mv", [P, TG, 2])
        rstd = sb("rstd", [P, TG])
        ysum = sb("ysum", [P, TG, C])

        pp = ps("pp", [P, 2, 512])
        pS = ps("pS", [P, 2, 512])
        pT = ps("pT", [P, 2, 512])
        pO = ps("pO", [P, 2, 512])

        s_c = sem("constants_loaded", False)
        s_wa = sem("attention_weights_loaded", False)
        s_wf = sem("ff_weights_loaded", False)
        s_kept = sem("input_kept", False)
        s_clear = sem("cleared", False)
        s_vp = [sem(f"window_before_copied{u}", False) for u in range(2)]
        s_xs = sem("x_staged")
        s_xTp = sem("x_turned")
        s_xT = sem("xT_copied")
        s_qk = sem("qk_projected")
        s_v = sem("v_projected")
        s_V = sem("v_copied")
        s_sq = sem("squared")
        s_ss = sem("squares_summed")
        s_t = sem("rotary_products")
        s_add = sem("rotary_added")
        s_rn = sem("norms_made")
        s_kn = sem("k_normed")
        s_turn = sem("qk_turned")
        s_qkT = sem("qkT_copied")
        s_S = sem("scored")
        s_Sm = sem("maxed")
        s_E = sem("exped")
        s_ETp = sem("weights_turned")
        s_ETa = sem("wT_copied_by_act")
        s_ETd = sem("wT_copied_by_dve")
        s_PV = sem("pv_done")
        s_On = sem("output_normed")
        s_OTp = sem("output_turned")
        s_OT = sem("outT_copied")
        s_y = sem("y_made")
        s_x = sem("attention_added")
        f_xs = sem("ff_x_staged")
        f_T1 = sem("ff_x_turned")
        f_sT = sem("ff_shifted")
        f_T2 = sem("ff_turned_back")
        f_mv = sem("ff_stats")
        f_rstd = sem("ff_rstd")
        f_xn = sem("ff_normed")
        f_T3 = sem("ff_normed_turned")
        f_xnT = sem("ff_normedT_copied")
        f_h = sem("ff_hidden")
        f_g = sem("ff_gelu")
        f_hT = sem("ff_gated")
        f_o = sem("ff_out")
        f_y = sem("ff_summed")
        f_x = sem("ff_added")
        s_dve = sem("dve_steps")
        f_dve = sem("ff_dve_steps")
        s_tab = sem("tables_made")
        s_nd = sem("norm_steps")
        s_held = sem("waits_passed", False)
        ctx.callback(clear_semaphores, nc, every)
        block = ctx.enter_context(nc.Block())

        def after(eng, s, value):
            eng.wait_ge(s, value + START)

        def visits(attention, l, on_pair=None):
            def pair(i, first, last):
                if on_pair:
                    on_pair(i)
                for u in range(2):
                    attention(l * NB + 2 * i + u, u, 2 * i + u, not (first and u == 0), not (last and u))
            return pair

        def layers(eng, attention, feed_forward, prologue, layer_start=None, on_pair=None):
            with eng.Fori(0, LAYERS) as l:
                if layer_start:
                    layer_start(l)
                prologue(l * NB)
                pair = visits(attention, l, on_pair and (lambda i: on_pair(l * (NB // 2) + i)))
                pair(0, True, False)
                with eng.Fori(1, NB // 2 - 1) as i:
                    pair(i, False, False)
                pair(NB // 2 - 1, False, True)
                feed_forward(l, l * NG)

        def groups(eng, l, M0, first, one):
            first(M0, 0)
            with eng.Fori(0, NG - 1) as g:
                one(M0 + g, g, True)
            one(M0 + NG - 1, NG - 1, False)


        @block.sync
        def _(sp):
            sp.dma_start(env["x_kept"], X[:, :, :]).then_inc(s_kept, 16)
            for t, (c, s) in enumerate((("l1_cos_q", "l1_sin_q"), ("l1_cos_k", "l1_sin_k"))):
                sp.dma_start(cos_c[:, t, :, :], consts[c].rearrange("(j p) d -> p j d", p=P)).then_inc(s_c, 16)
                sp.dma_start(sin_c[:, t, :, :], consts[s].rearrange("(j p) d -> p j d", p=P)).then_inc(s_c, 16)
            sp.dma_start(band[:, :], consts["band"]).then_inc(s_c, 16)
            with sp.Fori(0, LAYERS) as l:
                def of(name):
                    return weights[name][bass.ds(l, 1)]

                after(sp, s_x, NB * l)
                sp.dma_start(wqkv[:, :], of("Wqkv").rearrange("o c n -> c (o n)")).then_inc(s_wa, 16)
                sp.dma_start(wo[:, :, :], of("Wo").rearrange("o (k p) n -> p (o k) n", p=P)).then_inc(s_wa, 16)
                sp.dma_start(qks[:, 0, :], of("q_scale").broadcast_to([P, D])).then_inc(s_wa, 16)
                sp.dma_start(qks[:, 1, :], of("k_scale").broadcast_to([P, D])).then_inc(s_wa, 16)
                after(sp, f_x, NG * l)
                sp.dma_start(w1[:, :], of("W1").rearrange("o c n -> c (o n)")).then_inc(s_wf, 16)
                sp.dma_start(w2[:, 0:2, :], of("W2")[:, 0:2 * P, :].rearrange("o (k p) n -> p (o k) n", p=P)
                             ).then_inc(s_wf, 16)
                sp.dma_start(w2[0:F - 2 * P, 2, :], of("W2")[:, 2 * P:F, :].rearrange("o p n -> p (o n)")
                             ).then_inc(s_wf, 16)
                for part in range(2):
                    for k, (o, w) in enumerate(FC):
                        sp.dma_start(b1[0:w, part, k:k + 1],
                                     of("b1")[:, part * F + o:part * F + o + w].rearrange("o p -> p o")
                                     ).then_inc(s_wf, 16)
                sp.dma_start(lng[:, :], of("ln_g").rearrange("o p -> p o")).then_inc(s_wf, 16)
                sp.dma_start(lnb[:, :], of("ln_b").rearrange("o p -> p o")).then_inc(s_wf, 16)
                sp.dma_start(b2[:, :], of("b2").broadcast_to([P, C])).then_inc(s_wf, 16)

                with sp.Fori(0, NB // 2) as i:
                    for u in range(2):
                        N = l * NB + 2 * i + u
                        after(sp, s_V, 4 * N + 2)
                        after(sp, s_PV, NU * (N - 1))
                        sp.dma_start(vp[:, u, :], V[P - W:P, u, 0, :]).then_inc(s_vp[u], 16)
        W_A, W_F = 16 * 4, 16 * 12

        @block.gpsimd
        def _(pool):
            for s in sems:
                pool.sem_inc(s, START)
            nc.gpsimd.memset(xT[:, 0:1], 0.0).then_inc(s_clear, 1)
            nc.gpsimd.memset(fsT[:, :, 0:1], 0.0).then_inc(s_clear, 1)
            norm_steps = Steps(pool, s_nd, NORM_STEPS)

            def stage(N, u, b):
                after(pool, s_xTp, N - 1)
                held(pool, s_held)
                nc.gpsimd.tensor_copy(xs[:, u, :, :], X[:, bass.ds(2 * b, NT), :]).then_inc(s_xs, 1)

            def chunk(N, u, c):
                t, j, half = place(c)
                cols = slice(512 * half, 512 * half + 512)
                after(pool, s_turn, 8 * N)
                after(pool, s_t, 8 * N + c + 1)
                nc.gpsimd.tensor_tensor(pre[:, j, t, cols], t1[:, c % 4, :], t2[:, c % 4, :], ALU.add
                                        ).then_inc(s_add, 1)

            def inverse_norms(N, u, t):
                x = ss[:, u, t, :, :].rearrange("p j h -> p (j h)")
                y = rn[:, u, t, :, :].rearrange("p j h -> p (j h)")
                norm_steps.start(2 * N + 1 - t)

                def link(ins):
                    norm_steps.inc(ins)
                    after(pool, s_nd, norm_steps.base + norm_steps.count)
                    held(pool, s_held)

                after(pool, s_ss, 8 * N + 8 - 4 * t)
                after(pool, s_Sm, NU * (N - 1))
                held(pool, s_held)
                link(nc.gpsimd.tensor_scalar(x, x, 1e-24, None, ALU.max))
                link(nc.gpsimd.tensor_scalar(y.bitcast(I32), x.bitcast(I32), -0.5, RSQRT_GUESS,
                                             ALU.mult, ALU.add))
                for it in range(3):
                    link(nc.gpsimd.tensor_tensor(nt[:, :], x, y, ALU.mult))
                    link(nc.gpsimd.tensor_tensor(nt[:, :], nt[:, :], y, ALU.mult))
                    link(nc.gpsimd.tensor_scalar(nt[:, :], nt[:, :], -0.5, 1.5, ALU.mult, ALU.add))
                    last = nc.gpsimd.tensor_tensor(y, nt[:, :], y, ALU.mult)
                    if it < 2:
                        link(last)
                last.then_inc(s_rn, 1)
                norm_steps.end()
                after(pool, s_rn, 2 * N + 2 - t)
                held(pool, s_held)

            def norm_k(N, u):
                after(pool, s_add, 8 * N + 4)
                for half in range(2):
                    for j in range(NT):
                        k = pre[:, j, 1, 512 * half:512 * half + 512].rearrange("p (h d) -> p h d", d=D)
                        nc.gpsimd.tensor_tensor(
                            k, k, bcast(rn[:, u, 1, j, 8 * half:8 * half + 8], 2, D), ALU.mult
                        ).then_inc(s_kn, 1)

            def next_sequence(N, u, b):
                stage(N, u, b)
                for c in range(8):
                    chunk(N, u, c)
                    if c == 3:
                        inverse_norms(N, u, 1)
                        norm_k(N, u)
                inverse_norms(N, u, 0)

            def prologue(N):
                next_sequence(N, 0, 0)

            def attention(N, u, b, prev, nxt):
                if nxt:
                    next_sequence(N + 1, 1 - u, b + 1)

            def ff_stage(M, g):
                after(pool, f_T1, M)
                held(pool, s_held)
                nc.gpsimd.tensor_copy(fxs[:, :, :], X[:, bass.ds(TG * g, TG), :]).then_inc(f_xs, 1)
                after(pool, f_mv, M + 1)
                nc.gpsimd.tensor_tensor(rstd[:, :], mv[:, :, 1], neghalf[:, 0:TG], ALU.pow).then_inc(f_rstd, 1)

            def feed_forward(l, M0):
                after(pool, s_x, NB * (l + 1))
                groups(pool, l, M0, ff_stage, lambda M, g, nxt: ff_stage(M + 1, g + 1) if nxt else None)
                after(pool, f_x, NG * (l + 1))

            layers(pool, attention, feed_forward, prologue)

        @block.tensor
        def _(pe):
            def freed(kind, c, N):
                if kind == "x":
                    after(pe, s_xT, N + 1)
                elif kind == "qk":
                    after(pe, s_t, 8 * N + c + 1)
                elif kind == "v":
                    after(pe, s_V, 4 * N + c + 1)
                elif kind == "turn":
                    after(pe, s_qkT, 8 * N + c + 1)
                elif kind == "o":
                    after(pe, s_OT, 4 * N + c + 1)
                elif kind == "y":
                    after(pe, s_x, N + 1)

            def use(kind, c, bank, N, u):
                if kind == "x":
                    after(pe, s_xs, N + 1)
                    for j in range(NT):
                        last = nc.tensor.transpose(pp[:, bank, j * P:(j + 1) * P], xs[:, u, j, :], ident[:, :])
                    last.then_inc(s_xTp, 1)
                elif kind == "qk":
                    t, j, half = place(c)
                    after(pe, s_xT, N + 1)
                    nc.tensor.matmul(pp[:, bank, :], xT[:, j * P:(j + 1) * P],
                                     wqkv[:, t * I + 512 * half:t * I + 512 * half + 512],
                                     start=True, stop=True).then_inc(s_qk, 1)
                elif kind == "v":
                    j, half = c // 2, c % 2
                    nc.tensor.matmul(pp[:, bank, :], xT[:, j * P:(j + 1) * P],
                                     wqkv[:, 2 * I + 512 * half:2 * I + 512 * half + 512],
                                     start=True, stop=True).then_inc(s_v, 1)
                elif kind == "turn":
                    t, two = 1 - c // 4, c % 4
                    if t == 0:
                        after(pe, s_add, 8 * N + 8)
                    else:
                        after(pe, s_kn, 4 * N + 2 + 2 * (two // 2))
                    for g in range(2):
                        for j in range(NT):
                            o = (2 * two + g) * P
                            last = nc.tensor.transpose(pp[:, bank, g * T + j * P:g * T + (j + 1) * P],
                                                       pre[:, j, t, o:o + P], ident[:, :])
                    last.then_inc(s_turn, 1)
                elif kind == "o":
                    j, a = c // 2, c % 2
                    after(pe, s_On, 4 * N + c + 1)
                    for i in range(4):
                        o = a * 512 + i * P
                        last = nc.tensor.transpose(pp[:, bank, i * P:(i + 1) * P], On[:, j, o:o + P], ident[:, :])
                    last.then_inc(s_OTp, 1)
                elif kind == "y":
                    after(pe, s_OT, 4 * N + 4)
                    for j in range(NT):
                        for k in range(I // P):
                            last = nc.tensor.matmul(pp[:, bank, j * P:(j + 1) * P], OT[:, j, k, :], wo[:, k, :],
                                                    start=(k == 0), stop=(k == I // P - 1))
                    last.then_inc(s_y, 1)

            def scores(N, u, n):
                j = n // 8
                if n == 0:
                    after(pe, s_qkT, 8 * N + 8)
                after(pe, s_Sm, NU * N + n - 1)
                for m, h in enumerate(heads(n)):
                    r = D * (h % 2)
                    lo = 0 if j == 0 else P - W
                    last = nc.tensor.matmul(pS[:, n % 2, m * KW + W * (1 - j):(m + 1) * KW],
                                            qkT[r:r + D, u, 0, h // 2, j * P:(j + 1) * P],
                                            qkT[r:r + D, u, 1, h // 2, lo:(j + 1) * P], start=True, stop=True)
                last.then_inc(s_S, 1)

            def turn_weights(N, u, n):
                after(pe, s_E, NU * N + n + 1)
                after(pe, (s_ETa, s_ETd)[n % 2], 8 * N + n // 2)
                for m in range(2):
                    last = nc.tensor.transpose(pT[:, n % 2, m * P:(m + 1) * P], E[:, n % 4, m, W:KW], ident[:, :])
                if n >= 8:
                    for m in range(2):
                        last = nc.tensor.transpose(pT[0:W, n % 2, 2 * P + m * W:2 * P + (m + 1) * W],
                                                   E[0:W, n % 4, m, 0:W], ident[0:W, 0:W])
                last.then_inc(s_ETp, 1)

            def weigh(pair, N, u, n):
                j, r = n // 8, n // 4
                after(pe, (s_ETa, s_ETd)[n % 2], 8 * N + n // 2 + 1)
                if n == 0:
                    after(pe, s_V, 4 * N + 4)
                if n == 8:
                    pe.wait_ge(s_vp[u], 16 * (pair + 1))
                if n % 4 == 0:
                    after(pe, s_On, 4 * N + r - 1)
                for m, h in enumerate(heads(n)):
                    o = (h % 8) * D
                    last = nc.tensor.matmul(pO[:, r % 2, o:o + D], ET[:, n % 4, m * P:(m + 1) * P],
                                            V[:, u, j, h * D:(h + 1) * D], start=True, stop=True)
                    if j:
                        last = nc.tensor.matmul(pO[0:W, r % 2, o:o + D],
                                                ET[0:W, n % 4, 2 * P + m * W:2 * P + (m + 1) * W],
                                                vp[:, u, h * D:(h + 1) * D], start=False, stop=True,
                                                skip_group_check=True)
                last.then_inc(s_PV, 1)

            def prologue(N):
                for at, (kind, c) in enumerate(PROLOGUE):
                    if at >= 2:
                        freed(*PROLOGUE[at - 2], N)
                    use(kind, c, at % 2, N, 0)

            def attention(N, u, b, prev, nxt):
                for n, uses in slots(prev, nxt).items():
                    if n < NU:
                        scores(N, u, n)
                    for kind, c, d, bank, (kind2, c2, d2) in uses:
                        freed(kind2, c2, N + d2)
                        use(kind, c, bank, N + d, (u + d) % 2)
                    for unit in lagged(N, u, n, TURN_LAG, prev):
                        turn_weights(*unit)
                    for unit in lagged(N, u, n, WEIGH_LAG, prev):
                        weigh(pairs[0], *unit)

            def hidden(M, k):
                o, w = FC[k]
                after(pe, f_g, 3 * M + k - 1)
                after(pe, f_hT, 3 * M + k - 1)
                after(pe, f_xnT, M + 1)
                nc.tensor.matmul(pS[0:w, k % 2, :], w1[:, F + o:F + o + w], xnT[:, :], start=True, stop=True)
                nc.tensor.matmul(pT[0:w, k % 2, :], w1[:, o:o + w], xnT[:, :], start=True, stop=True
                                 ).then_inc(f_h, 1)

            def ff_out(M):
                after(pe, f_hT, 3 * M + 3)
                after(pe, f_x, M)
                for t in range(TG):
                    for k, (o, w) in enumerate(FC):
                        last = nc.tensor.matmul(pO[:, 1, t * P:(t + 1) * P], hT[0:w, k, t * P:(t + 1) * P],
                                                w2[0:w, k, :], start=(k == 0), stop=(k == 2))
                last.then_inc(f_o, 1)

            def ff_turn(M):
                after(pe, f_xs, M + 1)
                after(pe, f_sT, M)
                for t in range(TG):
                    last = nc.tensor.transpose(pp[:, 0, t * P:(t + 1) * P], fxs[:, t, :], ident[:, :])
                last.then_inc(f_T1, 1)

            def ff_turn_back(M):
                after(pe, f_sT, M + 1)
                after(pe, f_xn, M)
                for t in range(TG):
                    last = nc.tensor.transpose(pp[:, 1, t * P:(t + 1) * P],
                                               fsT[:, t // NT, t % NT * P:(t % NT + 1) * P], ident[:, :])
                last.then_inc(f_T2, 1)

            def ff_turn_normed(M):
                after(pe, f_xn, M + 1)
                after(pe, f_xnT, M)
                for t in range(TG):
                    last = nc.tensor.transpose(pO[:, 0, t * P:(t + 1) * P], xn[:, t, :], ident[:, :])
                last.then_inc(f_T3, 1)

            def ff_first(M, g):
                ff_turn(M)
                ff_turn_back(M)
                ff_turn_normed(M)

            def ff_one(M, g, nxt):
                if nxt:
                    ff_turn(M + 1)
                hidden(M, 0)
                hidden(M, 1)
                if nxt:
                    ff_turn_back(M + 1)
                hidden(M, 2)
                if nxt:
                    ff_turn_normed(M + 1)
                ff_out(M)

            def feed_forward(l, M0):
                pe.wait_ge(s_wf, W_F * (l + 1))
                after(pe, s_x, NB * (l + 1))
                groups(pe, l, M0, ff_first, ff_one)
                after(pe, f_x, NG * (l + 1))

            pairs = [None]
            pe.wait_ge(s_clear, 4)
            def on_pair(i):
                pairs[0] = i

            layers(pe, attention, feed_forward, prologue, lambda l: pe.wait_ge(s_wa, W_A * (l + 1)), on_pair)

        @block.scalar
        def _(act):
            act.wait_ge(s_clear, 4)

            def use(kind, c, bank, N, u):
                if kind == "x":
                    after(act, s_qk, 8 * N)
                    after(act, s_v, 4 * N)
                    after(act, s_xTp, N + 1)
                    nc.scalar.copy(xT[0:64, 0:T], pp[0:64, bank, 0:T])
                    nc.scalar.copy(xT[64:P, 1:T + 1], pp[64:P, bank, 0:T]).then_inc(s_xT, 1)
                elif kind == "qk":
                    after(act, s_ss, 8 * N + c - 1)
                    after(act, s_qk, 8 * N + c + 1)
                    nc.scalar.activation(sq[:, c % 2, :], pp[:, bank, :], ACT.Square).then_inc(s_sq, 1)
                elif kind == "v":
                    after(act, s_PV, NU * (N - 1))
                    after(act, s_v, 4 * N + c + 1)
                    nc.scalar.copy(V[:, u, c // 2, 512 * (c % 2):512 * (c % 2) + 512], pp[:, bank, :]
                                   ).then_inc(s_V, 1)
                elif kind == "turn":
                    after(act, s_S, NU * (N - 1))
                    after(act, s_turn, 8 * N + c + 1)
                    k = 2 * (c % 4)
                    nc.scalar.copy(qkT[:, u, 1 - c // 4, k:k + 2, :].rearrange("p g t -> p (g t)"), pp[:, bank, :]
                                   ).then_inc(s_qkT, 1)
                elif kind == "o":
                    after(act, s_y, N)
                    after(act, s_OTp, 4 * N + c + 1)
                    nc.scalar.copy(OT[:, c // 2, 4 * (c % 2):4 * (c % 2) + 4, :].rearrange("p k q -> p (k q)"),
                                   pp[:, bank, :]).then_inc(s_OT, 1)

            def exps(N, u, n):
                j = n // 8
                o = W * (1 - j)
                after(act, s_Sm, NU * N + n + 1)
                after(act, s_ETp, NU * N + n - 3)
                for m, h in enumerate(heads(n)):
                    last = nc.scalar.activation(E[:, n % 4, m, o:KW], S[:, n % 4, m, o:KW], ACT.Exp,
                                                bias=nm[:, u, j, h:h + 1], scale=-1.0,
                                                accum_out=rs[:, u, j, h:h + 1])
                last.then_inc(s_E, 1)

            def copy_weights(N, n):
                w = 2 * P + (2 * W if n >= 8 else 0)
                after(act, s_ETp, NU * N + n + 1)
                after(act, s_PV, NU * N + n - 3)
                nc.scalar.copy(ET[:, n % 4, 0:w], pT[:, 0, 0:w]).then_inc(s_ETa, 1)

            def prologue(N):
                for at, (kind, c) in enumerate(PROLOGUE):
                    use(kind, c, at % 2, N, 0)

            def attention(N, u, b, prev, nxt):
                for n, uses in slots(prev, nxt).items():
                    for kind, c, d, bank, _ in uses:
                        use(kind, c, bank, N + d, (u + d) % 2)
                    for unit in lagged(N, u, n, EXP_LAG, prev):
                        exps(*unit)
                    for V_, u_, m in lagged(N, u, n, TURN_LAG, prev):
                        if m % 2 == 0:
                            copy_weights(V_, m)

            def shift(M):
                after(act, f_T1, M + 1)
                after(act, f_T2, M)
                for e in range(2):
                    last = nc.scalar.copy(fsT[64 * e:64 * e + 64, :, e:T + e],
                                          pp[64 * e:64 * e + 64, 0, :].rearrange("p (s t) -> p s t", s=GR))
                last.then_inc(f_sT, 1)

            def copy_normed(M):
                after(act, f_T3, M + 1)
                after(act, f_h, 3 * M)
                nc.scalar.activation(xnT[:, :], pO[:, 0, :], ACT.Identity, bias=lnb[:, :], scale=lng[:, :]
                                     ).then_inc(f_xnT, 1)

            def gelu(M, k):
                w = FC[k][1]
                after(act, f_h, 3 * M + k + 1)
                after(act, f_hT, 3 * M + k - 1)
                nc.scalar.activation(gate[0:w, k % 2, :], pS[0:w, k % 2, :], ACT.Gelu, bias=b1[0:w, 1, k:k + 1]
                                     ).then_inc(f_g, 1)

            def ff_first(M, g):
                shift(M)
                copy_normed(M)

            def ff_one(M, g, nxt):
                if nxt:
                    shift(M + 1)
                gelu(M, 0)
                gelu(M, 1)
                gelu(M, 2)
                if nxt:
                    copy_normed(M + 1)

            def feed_forward(l, M0):
                act.wait_ge(s_wf, W_F * (l + 1))
                groups(act, l, M0, ff_first, ff_one)

            layers(act, attention, feed_forward, prologue)

        @block.vector
        def _(dve):
            for n in range(2):
                nc.vector.memset(pT[:, n, 2 * P:2 * P + 2 * W], 0.0).then_inc(s_clear, 1)
            dve.wait_ge(s_c, 16 * 5)
            dve.wait_ge(s_kept, 16)
            ff_steps = Steps(dve, f_dve, 8, s_held)

            def tables(l):
                dve.wait_ge(s_wa, W_A * (l + 1))
                for t in range(2):
                    nc.vector.tensor_tensor(cosT[:, t, :, :], cos_c[:, t, :, :], bcast(qks[:, t, :], 1, NT), ALU.mult)
                    for e in range(2):
                        a, b = 32 * e, 32 * (1 - e)
                        nc.vector.tensor_tensor(sinT[:, t, :, a:a + 32], sin_c[:, t, :, a:a + 32],
                                                bcast(qks[:, t, b:b + 32], 1, NT), ALU.mult).then_inc(s_tab, 1)
                after(dve, s_tab, 4 * (l + 1))

            def chunk(N, u, c, bank):
                t, j, half = place(c)
                p = pp[:, bank, :].rearrange("p (h d) -> p h d", d=D)
                after(dve, s_add, 8 * N + c - 3)
                after(dve, s_sq, 8 * N + c + 1)
                nc.vector.tensor_tensor(t1[:, c % 4, :].rearrange("p (h d) -> p h d", d=D), p,
                                        bcast(cosT[:, t, j, :], 1, 8), ALU.mult)
                for e in range(2):
                    a, b = 32 * e, 32 * (1 - e)
                    last = nc.vector.tensor_tensor(
                        t2[:, c % 4, :].rearrange("p (h d) -> p h d", d=D)[:, :, a:a + 32], p[:, :, b:b + 32],
                        bcast(sinT[:, t, j, a:a + 32], 1, 8), ALU.mult)
                last.then_inc(s_t, 1)
                after(dve, s_rn, 2 * (N - 1))
                nc.vector.tensor_reduce(ss[:, u, t, j, 8 * half:8 * half + 8],
                                        sq[:, c % 2, :].rearrange("p (h d) -> p h d", d=D), AX.X, ALU.add
                                        ).then_inc(s_ss, 1)

            def maxima(N, u, n):
                j = n // 8
                o = W * (1 - j)
                after(dve, s_E, NU * N + n - 3)
                if n == 0:
                    after(dve, s_rn, 2 * N + 2)
                after(dve, s_S, NU * N + n + 1)
                held(dve, s_held)
                for m, h in enumerate(heads(n)):
                    last = nc.vector.tensor_tensor_reduce(
                        out=S[:, n % 4, m, o:KW], in0=pS[:, n % 2, m * KW + o:(m + 1) * KW], in1=band[:, o:KW],
                        scale=rn[:, u, 0, j, h:h + 1], scalar=HUGE, op0=ALU.add, op1=ALU.min,
                        accum_out=nm[:, u, j, h:h + 1])
                last.then_inc(s_Sm, 1)

            def copy_weights(N, n):
                w = 2 * P + (2 * W if n >= 8 else 0)
                after(dve, s_ETp, NU * N + n + 1)
                after(dve, s_PV, NU * N + n - 3)
                nc.vector.tensor_copy(ET[:, n % 4, 0:w], pT[:, 1, 0:w]).then_inc(s_ETd, 1)

            def norm_output(N, u, r):
                j, a = r // 2, r % 2
                after(dve, s_E, NU * N + 4 * r + 4)
                nc.vector.reciprocal(ri[:, :], rs[:, u, j, 8 * a:8 * a + 8]).then_inc(s_dve, 1)
                after(dve, s_dve, 4 * N + r + 1)
                after(dve, s_OTp, 4 * N + r - 3)
                after(dve, s_PV, NU * N + 4 * r + 4)
                nc.vector.tensor_tensor(
                    On[:, j, 512 * a:512 * a + 512].rearrange("p (h d) -> p h d", d=D),
                    pO[:, r % 2, :].rearrange("p (h d) -> p h d", d=D), bcast(ri[:, :], 2, D), ALU.mult
                ).then_inc(s_On, 1)
                after(dve, s_On, 4 * N + r + 1)

            def add_attention(N, b, bank):
                after(dve, s_y, N + 1)
                x = X[:, bass.ds(2 * b, NT), :]
                nc.vector.tensor_tensor(x, pp[:, bank, 0:T].rearrange("p (j c) -> p j c", j=NT), x, ALU.add
                                        ).then_inc(s_x, 1)

            def prologue(N):
                for at, (kind, c) in enumerate(PROLOGUE):
                    if kind == "qk":
                        chunk(N, 0, c, at % 2)

            def attention(N, u, b, prev, nxt):
                for n, uses in slots(prev, nxt).items():
                    if n < NU:
                        maxima(N, u, n)
                    for kind, c, d, bank, _ in uses:
                        if kind == "qk":
                            chunk(N + d, (u + d) % 2, c, bank)
                        elif kind == "y":
                            add_attention(N + d, b + d, bank)
                    for V_, u_, m in lagged(N, u, n, TURN_LAG, prev):
                        if m % 2 == 1:
                            copy_weights(V_, m)
                    for V_, u_, m in lagged(N, u, n, NORM_LAG, prev):
                        if m % 4 == 3:
                            norm_output(V_, u_, m // 4)

            def stats(M):
                after(dve, f_T2, M + 1)
                ff_steps.start(M)
                for t in range(TG):
                    ff_steps.inc(nc.vector.bn_stats(st[:, t, :], pp[:, 1, t * P:(t + 1) * P]))
                after(dve, f_dve, ff_steps.base + ff_steps.count)
                held(dve, s_held)
                for t in range(TG):
                    ff_steps.inc(nc.vector.bn_aggr(mv[:, t, :], st[:, t, :]))
                after(dve, f_dve, ff_steps.base + ff_steps.count)
                nc.vector.tensor_scalar(mv[:, :, 1], mv[:, :, 1], LN_EPS, None, ALU.add).then_inc(f_mv, 1)
                ff_steps.end()

            def normalise(M):
                after(dve, f_rstd, M + 1)
                after(dve, f_T3, M)
                for t in range(TG):
                    last = nc.vector.tensor_scalar(xn[:, t, :], pp[:, 1, t * P:(t + 1) * P], mv[:, t, 0:1],
                                                   rstd[:, t:t + 1], ALU.subtract, ALU.mult)
                last.then_inc(f_xn, 1)
                after(dve, f_xn, M + 1)
                held(dve, s_held)

            def gated(M, k):
                w = FC[k][1]
                after(dve, f_o, M)
                after(dve, f_g, 3 * M + k + 1)
                nc.vector.scalar_tensor_tensor(hT[0:w, k, :], pT[0:w, k % 2, :], b1[0:w, 0, k:k + 1],
                                               gate[0:w, k % 2, :], ALU.add, ALU.mult).then_inc(f_hT, 1)

            def add_ff(M, g):
                after(dve, f_o, M + 1)
                x = X[:, bass.ds(TG * g, TG), :]
                nc.vector.tensor_tensor(ysum[:, :, :], pO[:, 1, :].rearrange("p (t c) -> p t c", t=TG), x, ALU.add
                                        ).then_inc(f_y, 1)
                after(dve, f_y, M + 1)
                nc.vector.tensor_tensor(x, ysum[:, :, :], bcast(b2[:, :], 1, TG), ALU.add).then_inc(f_x, 1)

            def ff_first(M, g):
                stats(M)
                normalise(M)

            def ff_one(M, g, nxt):
                gated(M, 0)
                gated(M, 1)
                if nxt:
                    stats(M + 1)
                gated(M, 2)
                if nxt:
                    normalise(M + 1)
                add_ff(M, g)

            def feed_forward(l, M0):
                dve.wait_ge(s_wf, W_F * (l + 1))
                groups(dve, l, M0, ff_first, ff_one)

            layers(dve, attention, feed_forward, prologue, tables)


def last_norm(nc, env, out):
    X, neghalf = env["X"], env["neghalf"]
    with ExitStack() as ctx:
        def sb(name, shape):
            return ctx.enter_context(nc.sbuf_tensor("z_" + name, shape, F32))

        def sem(name):
            return ctx.enter_context(nc.semaphore("z_" + name))

        x0 = sb("x0", [P, NB * NT, C])
        st = sb("st", [P, NB * NT, 6])
        mv = sb("mv", [P, NB * NT, 2])
        rstd = sb("rstd", [P, NB * NT])
        s_st, s_ag, s_mv, s_rstd, s_x, s_out, s_x0, s_add = (
            sem(n) for n in ("stats", "aggregated", "eps_added", "rstd", "normed", "stored", "input_loaded", "input_added"))
        block = ctx.enter_context(nc.Block())
        NTILES = NB * NT

        @block.vector
        def _(dve):
            dve.wait_ge(s_x0, 16)
            for q in range(4):
                tiles = slice(NTILES // 4 * q, NTILES // 4 * (q + 1))
                nc.vector.tensor_tensor(X[:, tiles, :], X[:, tiles, :], x0[:, tiles, :], ALU.add).then_inc(s_add, 1)
            dve.wait_ge(s_add, 4)
            for t in range(NTILES):
                nc.vector.bn_stats(st[:, t, :], X[:, t, :]).then_inc(s_st, 1)
            dve.wait_ge(s_st, NTILES)
            for t in range(NTILES):
                nc.vector.bn_aggr(mv[:, t, :], st[:, t, :]).then_inc(s_ag, 1)
            dve.wait_ge(s_ag, NTILES)
            nc.vector.tensor_scalar(mv[:, :, 1], mv[:, :, 1], LN_EPS, None, ALU.add).then_inc(s_mv, 1)
            dve.wait_ge(s_rstd, 1)
            for t in range(NTILES):
                nc.vector.tensor_scalar(X[:, t, :], X[:, t, :], mv[:, t, 0:1], rstd[:, t:t + 1],
                                        ALU.subtract, ALU.mult).then_inc(s_x, 1)

        @block.gpsimd
        def _(pool):
            pool.wait_ge(s_mv, 1)
            nc.gpsimd.tensor_tensor(rstd[:, :], mv[:, :, 1], neghalf[:, 0:NTILES], ALU.pow).then_inc(s_rstd, 1)

        @block.sync
        def _(sp):
            sp.dma_start(x0[:, :, :], env["x_kept"]).then_inc(s_x0, 16)
            for q in range(4):
                sp.wait_ge(s_x, NTILES // 4 * (q + 1))
                b = NB // 4 * q
                sp.dma_start(out[b:b + NB // 4].rearrange("b (j p) c -> p (b j) c", p=P),
                             X[:, NT * b:NT * (b + NB // 4), :]).then_inc(s_out, 16)
            sp.wait_ge(s_out, 16 * 4)


def program(nc, ins, consts, out):
    with ExitStack() as ctx:
        X = ctx.enter_context(nc.sbuf_tensor("X", [P, NB * NT, C], F32))
        ident = ctx.enter_context(nc.sbuf_tensor("ident", [P, P], F32))
        neghalf = ctx.enter_context(nc.sbuf_tensor("neghalf", [P, 64], F32))
        x_kept = nc.dram_tensor("x_kept", (P, NB * NT, C), F32).ap()
        env = {"x_kept": x_kept, "X": X, "ident": ident, "neghalf": neghalf, "x_dram": ins["L0_attn_x"]}

        def of(prefix):
            return {k[len(prefix):]: v for k, v in ins.items() if k.startswith(prefix)}

        l0_attention(nc, env, of("L0_attn_"), consts)
        l0_experts(nc, env, of("L0_ffn_"), consts)
        l1_attention(nc, env, of("L1_attn_"), consts)
        l1_network(nc, env, of("L1_ffn_"), consts)
        last_norm(nc, env, out)


def shape_constants():
    f = np.float32
    t = np.arange(T, dtype=f)
    inv = (1.0 / 10000.0 ** (np.arange(0, 4, 2, dtype=f) / f(4))).astype(f)
    emb = np.concatenate([t[:, None] * inv[None, :]] * 2, axis=-1).astype(f)
    sign = np.array([-1, 1, -1, 1], f)
    row, col = np.arange(P)[:, None], np.arange(P)[None, :]
    causal = np.concatenate([np.zeros((P, P), f), np.where(col <= row, 0, MASKED).astype(f)], axis=1)
    half = np.arange(0, 64, 2, dtype=f)
    inv_freq = (1.0 / f(10000.0) ** (half / f(64))).astype(f)
    freqs = (t[:, None] * inv_freq[None, :]).astype(f)
    freqs = np.concatenate([freqs, freqs], -1)
    base = ((half + f(0.4 * 64)) / f(1.4 * 64)).astype(f)
    power = ((t - T // 2) / f(16)).astype(f)
    scale = (base[None, :] ** power[:, None]).astype(f)
    scale = np.concatenate([scale, scale], -1)
    cos, sin = np.cos(freqs).astype(f), np.sin(freqs).astype(f)
    sin[:, :32] *= -1
    rel = row - (np.arange(160)[None, :] - 32)
    chunk = (row // 32 == col // 32) & (row <= col)
    look = np.where((rel >= 1) & (rel <= 32), 0, MASKED).astype(f)
    before = np.where(rel == 1, 0, MASKED).astype(f)
    notfirst = np.ones((P, NT), f)
    notfirst[0, 0] = 0
    pr = np.arange(P)
    return {
        "row_sequence": (pr[:, None] // 16 == np.arange(8)[None, :]).astype(f),
        "row_expert": (pr[:, None] % 16 == np.arange(16)[None, :]).astype(f),
        "token": (pr[:, None] + P * np.arange(NT)[None, :]).astype(f),
        "iota": np.broadcast_to(t[None, :], (P, T)),
        "prefix": np.where(chunk, f(1) / (col % 32 + 1).astype(f), 0).astype(f),
        "look_mask": np.concatenate([look, before], axis=1),
        "prev": (rel == 1).astype(f),
        "notfirst": notfirst,
        "l1_cos_q": -8 * cos * scale, "l1_sin_q": -8 * sin * scale,
        "l1_cos_k": cos / scale, "l1_sin_k": sin / scale,
        "band": np.where((rel >= 0) & (rel <= 32), 0, -MASKED).astype(f),
        "ident": np.eye(P, dtype=f),
        "causal": causal,
        "l0_cos": np.cos(emb).astype(f),
        "l0_sin": (np.sin(emb) * sign).astype(f),
    }


def kernel(**inputs):
    import concourse.bacc as bacc
    from concourse.bass_utils import run_bass_kernel_spmd as run

    nc = bacc.Bacc("TRN2", target_bir_lowering=False, num_devices=1)
    arrays, ins, consts = {}, {}, {}
    for name, value in inputs.items():
        a = np.ascontiguousarray(value)
        if a.ndim == 0:
            a = a.reshape(1, 1)
        arrays[f"in_{name}"] = a
        ins[name] = nc.dram_tensor(f"in_{name}", a.shape, mybir.dt.from_np(a.dtype), kind="ExternalInput").ap()
    for name, a in shape_constants().items():
        a = np.ascontiguousarray(a)
        arrays[f"const_{name}"] = a
        consts[name] = nc.dram_tensor(f"const_{name}", a.shape, mybir.dt.from_np(a.dtype), kind="ExternalInput").ap()
    out = nc.dram_tensor("out", (NB, T, C), F32, kind="ExternalOutput").ap()
    program(nc, ins, consts, out)
    return run(nc, [arrays], core_ids=[0]).results[0]["out"]
```

```python
from contextlib import ExitStack

import numpy as np
import concourse.bass as bass
from concourse import mybir

ALU = mybir.AluOpType
ACT = mybir.ActivationFunctionType
AX = mybir.AxisListType
F32 = mybir.dt.float32
BF16 = mybir.dt.bfloat16
U32 = mybir.dt.uint32
I32 = mybir.dt.int32

P = 128
NB = 16
T = 256
C = 128
NT = T // P
MASKED = -1.0e30
HUGE = 3.0e38
LN_EPS = 1.0e-5
RSQRT_GUESS = float(0x5F3759DF)


class Steps:

    def __init__(self, eng, sem, per, passed=None):
        self.eng, self.sem, self.per, self.passed = eng, sem, per, passed
        self.base, self.count = 0, 0

    def start(self, n):
        self.base, self.count = n * self.per, 0

    def inc(self, ins):
        ins.then_inc(self.sem, 1)
        self.count += 1

    def wait(self):
        self.eng.wait_ge(self.sem, self.base + self.count)

    def link(self, ins):
        self.inc(ins)
        self.wait()

    def end(self):
        assert self.count == self.per, (self.count, self.per)


def bcast(ap, axis, n):
    a = ap.unsqueeze(axis)
    shape = list(a.shape)
    shape[axis] = n
    return a.broadcast_to(shape)


def ge(eng, sem, value):
    if not (isinstance(value, int) and value <= 0):
        eng.wait_ge(sem, value)


def clear_semaphores(nc, semaphores):
    with nc.Block() as block:
        @block.gpsimd
        def _(pool):
            for s in semaphores:
                pool.sem_clear(s)


def held(eng, passed):
    eng.sem_inc(passed, 1)


def passes(eng, one):
    def pair(i, last):
        one(2 * i, 0, (2 * i + 1, i, 1))
        one(2 * i + 1, 1, None if last else (2 * i + 2, i + 1, 0))
    pair(0, False)
    with eng.Fori(1, NB // 2 - 1) as i:
        pair(i, False)
    pair(NB // 2 - 1, True)


def lagged(b, u, n, lag, units):
    m = n - lag
    if m < 0:
        return [] if isinstance(b, int) and b == 0 else [(b - 1, 1 - u, m + units)]
    return [(b, u, m)] if m < units else []


def looped(eng, one):
    def pair(i, last):
        one(2 * i, 0, (2 * i + 1, i, 1))
        one(2 * i + 1, 1, None if last else (2 * i + 2, i + 1, 0))
    with eng.Fori(0, NB // 2 - 1) as i:
        pair(i, False)
    pair(NB // 2 - 1, True)


def layer_norm_stats(nc, dve, steps, z, st, mv, s_mv):
    for j in range(NT):
        steps.inc(nc.vector.bn_stats(st[:, j, :], z[:, j, :]))
    steps.wait()
    held(dve, steps.passed)
    for j in range(NT):
        steps.inc(nc.vector.bn_aggr(mv[:, j, :], st[:, j, :]))
    steps.wait()
    nc.vector.tensor_scalar(mv[:, :, 1], mv[:, :, 1], LN_EPS, None, ALU.add).then_inc(s_mv, 1)


def layer_norm_write(nc, dve, z, X, b, mv, rstd, s_rstd, s_x):
    dve.wait_ge(s_rstd, b + 1)
    for j in range(NT):
        nc.vector.tensor_scalar(X[:, bass.ds(2 * b + j, 1), :].rearrange("p o c -> p (o c)"), z[:, j, :],
                                mv[:, j, 0:1], rstd[:, j:j + 1], ALU.subtract, ALU.mult).then_inc(s_x, 1)
    dve.wait_ge(s_x, 2 * b + 2)


def l0_attention(nc, env, weights, consts):
    H, L, D = 16, 64, 8
    G = H // 4
    NU = (H // 2) * NT
    SCALE = 1.0 / np.sqrt(D)
    ident, X, neghalf = env["ident"], env["X"], env["neghalf"]
    x_dram = env["x_dram"]
    DVE_STEPS = 4

    def heads(n):
        hp = n // 2
        return (hp % 4 + 4 * (2 * (hp // 4)), hp % 4 + 4 * (2 * (hp // 4) + 1))

    EXP_LAG, TURN_LAG, WEIGH_LAG = 1, 3, 5
    COPY_O, NORM_O = (14, 21), (15, 22)
    TURN_O, MULTIPLY_O, ADD_O, WRITE_X, END = 23, 24, 25, 26, 27
    TURN_X, PROJECT, TURN_QK = 3, (10, 11), (13, 14)

    def ends(b, u, n, at):
        if at < NU:
            return [(b, u)] if n == at else []
        return [(ob, ou) for ob, ou, m in lagged(b, u, n, at - NU + 1, NU) if m == NU - 1]

    with ExitStack() as ctx:
        def sb(name, shape, dt=F32):
            return ctx.enter_context(nc.sbuf_tensor("a_" + name, shape, dt))

        def ps(name, shape):
            return ctx.enter_context(nc.psum_tensor("a_" + name, shape, F32))

        every = []

        def sem(name):
            s = ctx.enter_context(nc.semaphore("a_" + name))
            every.append(s)
            return s

        down = sb("down", [P, 3, H * L])
        up2 = sb("up2", [P, 3, 2, D])
        downT = sb("downT", [P, 2, C])
        weff = sb("weff", [P, 3 * H * D])
        wc_sb = sb("wc", [P, C])
        cos_sb = sb("cos", [P, NT, 4])
        sin_sb = sb("sin", [P, NT, 4])
        causal = sb("causal", [P, T])
        xs = sb("xs", [P, 2, NT, C])
        xT = sb("xT", [P, T])
        pad = sb("pad", [P, NT, 2 * H, 32])
        r1 = sb("r1", [P, NT, 2 * H, 4])
        r2 = sb("r2", [P, NT, 2 * H, 4])
        qkT = sb("qkT", [P, 2, 2, G, T])
        V = sb("V", [P, 2, NT, H, 32])
        S = sb("S", [P, 4, 2, T])
        E = sb("E", [P, 4, 2, T])
        ET = sb("ET", [P, 4, 4, P])
        nm = sb("nm", [P, 2, NT, H])
        rs = sb("rs", [P, 2, NT, H])
        ri = sb("ri", [P, NT, H])
        OR = sb("OR", [P, 2, 2 * T])
        On = sb("On", [P, NT, H * D])
        OT = sb("OT", [P, T])
        z = sb("z", [P, NT, C])
        st = sb("st", [P, NT, 6])
        mv = sb("mv", [P, NT, 2])
        rstd = sb("rstd", [P, NT])

        pp = ps("pp", [P, 2, 512])
        pS = ps("pS", [P, 2, 512])
        pT = ps("pT", [P, 2, 4, P])
        pO = ps("pO", [P, 2, 512])

        s_w = sem("weights_loaded")
        s_xs = [sem("x_staged0"), sem("x_staged1")]
        s_pad0 = sem("pad_cleared")
        s_dT = sem("down_turned")
        s_dTc = sem("downT_copied")
        s_we = sem("weff_made")
        s_wec = sem("weff_copied")
        s_xTp = sem("x_turned")
        s_xT = sem("xT_copied")
        s_proj = sem("projected")
        s_pad = sem("pad_filled")
        s_V = sem("v_copied")
        s_turn = sem("qk_turned")
        s_qkT = sem("qkT_copied")
        s_S = sem("scored")
        s_Sm = sem("maxed")
        s_E = sem("exped")
        s_ETp = sem("weights_turned")
        s_ETa = sem("wT_copied_by_act")
        s_ETd = sem("wT_copied_by_dve")
        s_PV = sem("pv_done")
        s_Oc = sem("output_copied")
        s_OB = sem("output_turned_back")
        s_ri = sem("sums_inverted")
        s_On = sem("output_normed")
        s_OTp = sem("output_turned")
        s_OT = sem("outT_copied")
        s_y = sem("y_made")
        s_z = sem("summed")
        s_mv = sem("stats_made")
        s_rstd = sem("rstd_made")
        s_x = sem("x_written")
        s_dve = sem("dve_steps")
        s_held = sem("dve_waits_passed")
        ctx.callback(clear_semaphores, nc, every)
        block = ctx.enter_context(nc.Block())


        @block.sync
        def _(sp):
            for n, name in enumerate(("Wq_down", "Wk_down", "Wv_down")):
                sp.dma_start(down[:, n, :], weights[name]).then_inc(s_w, 16)
            sp.dma_start(wc_sb[:, :], weights["Wc"]).then_inc(s_w, 16)
            sp.dma_start(cos_sb[:, :, :], consts["l0_cos"].rearrange("(j p) d -> p j d", p=P)).then_inc(s_w, 16)
            sp.dma_start(sin_sb[:, :, :], consts["l0_sin"].rearrange("(j p) d -> p j d", p=P)).then_inc(s_w, 16)
            sp.dma_start(ident[:, :], consts["ident"]).then_inc(s_w, 16)
            sp.dma_start(causal[:, :], consts["causal"]).then_inc(s_w, 16)
            sp.dma_start(X[:, :, :], x_dram.rearrange("b (j p) c -> p (b j) c", p=P)).then_inc(s_w, 16)
            sp.wait_ge(s_pad0, 2)
            for n, names in enumerate((("Wq_up_c", "Wq_up_e"), ("Wk_up_c", "Wk_up_e"), ("Wv_up",))):
                for m, name in enumerate(names):
                    w = D // len(names)
                    for e in range(2):
                        sp.dma_start(up2[e * L:(e + 1) * L, n, e, m * w:(m + 1) * w],
                                     weights[name]).then_inc(s_w, 16)

            def stage(q, pair, u):
                if not (isinstance(pair, int) and pair == 0):
                    sp.wait_ge(s_xTp, q - 1)
                sp.dma_start(xs[:, u, :, :], x_dram[q:q + 1, :, :].rearrange("o (j p) c -> p (o j) c", p=P)
                             if isinstance(q, int) else
                             x_dram[bass.ds(q, 1), :, :].rearrange("o (j p) c -> p (o j) c", p=P)
                             ).then_inc(s_xs[u], 16)

            stage(0, 0, 0)
            stage(1, 0, 1)
            with sp.Fori(1, NB // 2) as i:
                for u in range(2):
                    stage(2 * i + u, i, u)
        N_W = 16 * 19

        @block.gpsimd
        def _(pool):
            nc.gpsimd.memset(up2[:, :, :, :], 0.0).then_inc(s_pad0, 1)
            nc.gpsimd.memset(pad[:, :, :, :], 0.0).then_inc(s_pad0, 1)
            nc.gpsimd.memset(neghalf[:, :], -0.5).then_inc(s_pad0, 1)
            nc.gpsimd.memset(V[:, :, :, :, :], 0.0).then_inc(s_pad0, 1)
            pool.wait_ge(s_pad0, 4)

            def tail(b):
                pool.wait_ge(s_mv, b + 1)
                nc.gpsimd.tensor_tensor(rstd[:, :], mv[:, :, 1], neghalf[:, 0:NT], ALU.pow).then_inc(s_rstd, 1)

            with pool.Fori(0, NB) as b:
                tail(b)

        @block.tensor
        def _(pe):
            pe.wait_ge(s_w, N_W)

            def turn_down(m):
                n, c = m // (H // 2), m % (H // 2)
                ge(pe, s_dTc, m - 1)
                nc.tensor.transpose(pp[:, m % 2, 0:C], down[:, n, c * P:(c + 1) * P],
                                    ident[:, :]).then_inc(s_dT, 1)

            turn_down(0)
            for m in range(3 * H // 2):
                n = m // (H // 2)
                if m + 1 < 3 * H // 2:
                    turn_down(m + 1)
                pe.wait_ge(s_dTc, m + 1)
                ge(pe, s_wec, m - 1)
                nc.tensor.matmul(pS[:, m % 2, 0:16], downT[:, m % 2, :], up2[:, n, :, :],
                                 start=True, stop=True).then_inc(s_we, 1)

            def turn_x(q, pair, u):
                pe.wait_ge(s_xs[u], 16 * (pair + 1))
                ge(pe, s_qkT, 4 * q)
                ge(pe, s_On, 2 * q - 3)
                for j in range(NT):
                    last = nc.tensor.transpose(pp[:, 0, j * P:(j + 1) * P], xs[:, u, j, :], ident[:, :])
                last.then_inc(s_xTp, 1)

            def project(q, j):
                if isinstance(q, int) and q == 0:
                    pe.wait_ge(s_wec, 3 * H // 2)
                if j == 0:
                    ge(pe, s_OT, q - 1)
                else:
                    ge(pe, s_z, q - 1)
                pe.wait_ge(s_xT, q + 1)
                nc.tensor.matmul(pp[:, 1 - j, 0:3 * C], xT[:, j * P:(j + 1) * P], weff[:, :],
                                 start=True, stop=True).then_inc(s_proj, 1)

            def turn_qk(q, t):
                pe.wait_ge(s_pad, 2 * q + 2)
                for k in range(2):
                    n = 2 * t + k
                    if n >= 2:
                        pe.wait_ge(s_qkT, 4 * q + n - 1)
                    for g in range(2):
                        for j in range(NT):
                            h = t * H + 4 * (2 * k + g)
                            last = nc.tensor.transpose(
                                pp[:, 1 - k, g * T + j * P:g * T + (j + 1) * P],
                                pad[:, j, h:h + 4, :].rearrange("p h d -> p (h d)"), ident[:, :])
                    last.then_inc(s_turn, 1)

            def scores(b, u, n):
                j = n % 2
                if n == 0:
                    pe.wait_ge(s_qkT, 4 * b + 4)
                ge(pe, s_Sm, NU * b + n - 1)
                for m, h in enumerate(heads(n)):
                    r, g = 32 * (h % 4), h // 4
                    last = nc.tensor.matmul(pS[:, n % 2, m * T:m * T + (j + 1) * P],
                                            qkT[r:r + 32, u, 0, g, j * P:(j + 1) * P],
                                            qkT[r:r + 32, u, 1, g, 0:(j + 1) * P], start=True, stop=True)
                last.then_inc(s_S, 1)

            def turn_weights(b, u, n):
                j = n % 2
                pe.wait_ge(s_E, NU * b + n + 1)
                ge(pe, (s_ETa, s_ETd)[j], H // 2 * b + n // 2)
                for m in range(2):
                    for c in range(j + 1):
                        last = nc.tensor.transpose(pT[:, j, m * (j + 1) + c, :],
                                                   E[:, n % 4, m, c * P:(c + 1) * P], ident[:, :])
                last.then_inc(s_ETp, 1)

            def weigh(b, u, n):
                j = n % 2
                pe.wait_ge((s_ETa, s_ETd)[j], H // 2 * b + n // 2 + 1)
                if n == 0:
                    pe.wait_ge(s_V, 2 * b + 2)
                half = n // 8
                if n % 8 == 0:
                    ge(pe, s_Oc, 2 * b + half - 1)
                for m, h in enumerate(heads(n)):
                    r = 32 * (h % 4)
                    for c in range(j + 1):
                        last = nc.tensor.matmul(pO[r:r + 32, half, m * T + j * P:m * T + (j + 1) * P],
                                                V[:, u, c, h, :], ET[:, n % 4, m * (j + 1) + c, :],
                                                start=(c == 0), stop=(c == j))
                last.then_inc(s_PV, 1)

            def turn_back(b, half, turned_x, turned_qk):
                pe.wait_ge(s_Oc, 2 * b + half + 1)
                if turned_x:
                    pe.wait_ge(s_xT, b + 3)
                if turned_qk:
                    pe.wait_ge(s_qkT, 4 * b + 8)
                ge(pe, s_z, b)
                ge(pe, s_On, 2 * b + half)
                for j in range(NT):
                    for g in range(2):
                        last = nc.tensor.transpose(pp[:, 0, (2 * j + g) * P:(2 * j + g + 1) * P],
                                                   OR[:, half, g * T + j * P:g * T + (j + 1) * P], ident[:, :])
                last.then_inc(s_OB, 1)

            def turn_output(b):
                pe.wait_ge(s_On, 2 * b + 2)
                ge(pe, s_OT, b)
                for j in range(NT):
                    last = nc.tensor.transpose(pp[:, 1, j * P:(j + 1) * P], On[:, j, :], ident[:, :])
                last.then_inc(s_OTp, 1)

            def multiply_output(b):
                pe.wait_ge(s_OT, b + 1)
                for j in range(NT):
                    last = nc.tensor.matmul(pp[:, 0, j * P:(j + 1) * P], OT[:, j * P:(j + 1) * P],
                                            wc_sb[:, :], start=True, stop=True)
                last.then_inc(s_y, 1)

            def one(b, u, nxt):
                for n in range(NU if nxt else END):
                    if n < NU:
                        scores(b, u, n)
                    for half in range(2):
                        for ob, _ in ends(b, u, n, NORM_O[half]):
                            turn_back(ob, half, half == 1 and n < NU and nxt, half == 0 and nxt)
                    for ob, _ in ends(b, u, n, TURN_O):
                        turn_output(ob)
                    for ob, _ in ends(b, u, n, MULTIPLY_O):
                        multiply_output(ob)
                    if nxt:
                        q, pair, v = nxt
                        if n == TURN_X:
                            turn_x(q, pair, v)
                        for j in range(NT):
                            if n == PROJECT[j]:
                                project(q, j)
                            if n == TURN_QK[j]:
                                turn_qk(q, j)
                    for unit in lagged(b, u, n, TURN_LAG, NU):
                        turn_weights(*unit)
                    for unit in lagged(b, u, n, WEIGH_LAG, NU):
                        weigh(*unit)

            turn_x(0, 0, 0)
            project(0, 0)
            project(0, 1)
            turn_qk(0, 0)
            turn_qk(0, 1)
            passes(pe, one)

        @block.scalar
        def _(act):
            for m in range(3 * H // 2):
                act.wait_ge(s_we, m + 1)
                nc.scalar.copy(weff[:, 16 * m:16 * m + 16], pS[:, m % 2, 0:16]).then_inc(s_wec, 1)

            def copy_x(q):
                ge(act, s_proj, 2 * q)
                act.wait_ge(s_xTp, q + 1)
                nc.scalar.copy(xT[:, :], pp[:, 0, 0:T]).then_inc(s_xT, 1)

            def copy_qk(q, u, t):
                ge(act, s_S, NU * (q - 1))
                for k in range(2):
                    act.wait_ge(s_turn, 4 * q + 2 * t + k + 1)
                    nc.scalar.copy(qkT[:, u, t, 2 * k:2 * k + 2, :].rearrange("p g t -> p (g t)"),
                                   pp[:, 1 - k, :]).then_inc(s_qkT, 1)

            def exps(b, u, n):
                j = n % 2
                act.wait_ge(s_Sm, NU * b + n + 1)
                ge(act, s_ETp, NU * b + n - 3)
                for m, h in enumerate(heads(n)):
                    last = nc.scalar.activation(E[:, n % 4, m, 0:(j + 1) * P], S[:, n % 4, m, 0:(j + 1) * P],
                                                ACT.Exp, bias=nm[:, u, j, h:h + 1], scale=-1.0,
                                                accum_out=rs[:, u, j, h:h + 1])
                last.then_inc(s_E, 1)

            def copy_weights(b, n):
                act.wait_ge(s_ETp, NU * b + n + 1)
                ge(act, s_PV, NU * b + n - 3)
                nc.scalar.copy(ET[:, n % 4, 0:2, :].rearrange("p m k -> p (m k)"),
                               pT[:, 0, 0:2, :].rearrange("p m k -> p (m k)")).then_inc(s_ETa, 1)

            def copy_raw(b, half):
                act.wait_ge(s_PV, NU * b + 8 * half + 8)
                ge(act, s_OB, 2 * b + half - 1)
                nc.scalar.copy(OR[:, half, :], pO[:, half, :]).then_inc(s_Oc, 1)

            def copy_output(b):
                act.wait_ge(s_OTp, b + 1)
                ge(act, s_y, b)
                nc.scalar.copy(OT[:, :], pp[:, 1, 0:T]).then_inc(s_OT, 1)

            def one(b, u, nxt):
                for n in range(NU if nxt else END):
                    for half in range(2):
                        for ob, _ in ends(b, u, n, COPY_O[half]):
                            copy_raw(ob, half)
                    for ob, _ in ends(b, u, n, TURN_O):
                        copy_output(ob)
                    if nxt:
                        q, pair, v = nxt
                        if n == TURN_X:
                            copy_x(q)
                        for t in range(2):
                            if n == TURN_QK[t]:
                                copy_qk(q, v, t)
                    for unit in lagged(b, u, n, EXP_LAG, NU):
                        exps(*unit)
                    for ub, _, m in lagged(b, u, n, TURN_LAG, NU):
                        if m % 2 == 0:
                            copy_weights(ub, m)

            copy_x(0)
            copy_qk(0, 0, 0)
            copy_qk(0, 0, 1)
            passes(act, one)

        @block.vector
        def _(dve):
            steps = Steps(dve, s_dve, DVE_STEPS, s_held)
            dve.wait_ge(s_w, N_W)
            dve.wait_ge(s_pad0, 4)
            for m in range(3 * H // 2):
                dve.wait_ge(s_dT, m + 1)
                ge(dve, s_we, m - 1)
                nc.vector.tensor_copy(downT[:, m % 2, :], pp[:, m % 2, 0:C]).then_inc(s_dTc, 1)

            def rope(q, u, j):
                ge(dve, s_turn, 4 * q)
                ge(dve, s_PV, NU * (q - 1))
                dve.wait_ge(s_proj, 2 * q + 1 + j)
                qk = pp[:, 1 - j, 0:2 * C].rearrange("p (h d) -> p h d", d=D)
                nc.vector.tensor_copy(pad[:, j, :, 0:4], qk[:, :, 0:4])
                nc.vector.tensor_tensor(r1[:, j, :, :], qk[:, :, 4:8], bcast(cos_sb[:, j, :], 1, 2 * H), ALU.mult)
                for e in range(2):
                    nc.vector.tensor_tensor(r2[:, j, :, e:4:2], qk[:, :, 5 - e:8:2],
                                            bcast(sin_sb[:, j, e:4:2], 1, 2 * H), ALU.mult)
                nc.vector.tensor_copy(V[:, u, j, :, 0:D], pp[:, 1 - j, 2 * C:3 * C].rearrange(
                    "p (h d) -> p h d", d=D)).then_inc(s_V, 1)
                dve.wait_ge(s_V, 2 * q + 1 + j)
                nc.vector.tensor_tensor(pad[:, j, :, 4:8], r1[:, j, :, :], r2[:, j, :, :], ALU.add
                                        ).then_inc(s_pad, 1)
                dve.wait_ge(s_pad, 2 * q + 1 + j)

            def maxima(b, u, n):
                j = n % 2
                ge(dve, s_E, NU * b + n - 3)
                dve.wait_ge(s_S, NU * b + n + 1)
                held(dve, s_held)
                for m, h in enumerate(heads(n)):
                    last = nc.vector.tensor_tensor_reduce(
                        out=S[:, n % 4, m, 0:(j + 1) * P], in0=pS[:, n % 2, m * T:m * T + (j + 1) * P],
                        in1=causal[:, (1 - j) * P:T], scale=-SCALE, scalar=HUGE, op0=ALU.add, op1=ALU.min,
                        accum_out=nm[:, u, j, h:h + 1])
                last.then_inc(s_Sm, 1)

            def copy_weights(b, n):
                dve.wait_ge(s_ETp, NU * b + n + 1)
                ge(dve, s_PV, NU * b + n - 3)
                nc.vector.tensor_copy(ET[:, n % 4, :, :], pT[:, 1, :, :]).then_inc(s_ETd, 1)

            def norm_output(b, u, half):
                h = slice(8 * half, 8 * half + 8)
                dve.wait_ge(s_E, NU * b + 8 * half + 8)
                ge(dve, s_On, 2 * b + half)
                nc.vector.reciprocal(ri[:, :, h], rs[:, u, :, h]).then_inc(s_ri, 1)
                dve.wait_ge(s_ri, 2 * b + half + 1)
                dve.wait_ge(s_OB, 2 * b + half + 1)
                ge(dve, s_OTp, b)
                nc.vector.tensor_tensor(
                    On[:, :, 64 * half:64 * half + 64].rearrange("p j (h d) -> p j h d", d=D),
                    pp[:, 0, :].rearrange("p (j h e) -> p j h e", j=NT, e=32)[:, :, :, 0:D],
                    bcast(ri[:, :, h], 3, D), ALU.mult).then_inc(s_On, 1)

            def add_output(b, u):
                dve.wait_ge(s_y, b + 1)
                xb = X[:, bass.ds(2 * b, 2), :]
                steps.start(b)
                nc.vector.tensor_tensor(z[:, :, :], pp[:, 0, 0:T].rearrange("p (j c) -> p j c", j=NT),
                                        xb, ALU.add).then_inc(s_z, 1)
                dve.wait_ge(s_z, b + 1)
                layer_norm_stats(nc, dve, steps, z, st, mv, s_mv)
                steps.end()

            def one(b, u, nxt):
                for n in range(NU if nxt else END):
                    if n < NU:
                        maxima(b, u, n)
                    for half in range(2):
                        for ob, ou in ends(b, u, n, NORM_O[half]):
                            norm_output(ob, ou, half)
                    for ob, ou in ends(b, u, n, ADD_O):
                        add_output(ob, ou)
                    for ob, _ in ends(b, u, n, WRITE_X):
                        layer_norm_write(nc, dve, z, X, ob, mv, rstd, s_rstd, s_x)
                    for ub, _, m in lagged(b, u, n, TURN_LAG, NU):
                        if m % 2 == 1:
                            copy_weights(ub, m)
                    for j in range(NT):
                        if nxt and n == PROJECT[j]:
                            rope(nxt[0], nxt[2], j)

            rope(0, 0, 0)
            rope(0, 0, 1)
            passes(dve, one)


EX, CAP, FF = 16, 32, 512
EG = NB * EX // P
BG = NB // EG
START = 64


def after(eng, s, value):
    eng.wait_ge(s, value + START)


def router(nc, env, weights, consts, idx, val):
    ITERS = 6
    ident, X = env["ident"], env["X"]
    R = NT * NB
    with ExitStack() as ctx:
        def sb(name, shape, dt=F32):
            return ctx.enter_context(nc.sbuf_tensor("r_" + name, shape, dt))

        def ps(name, shape):
            return ctx.enter_context(nc.psum_tensor("r_" + name, shape, F32))

        sems, every = [], []

        def sem(name, counted=True):
            s = ctx.enter_context(nc.semaphore("r_" + name))
            every.append(s)
            if counted:
                sems.append(s)
            return s

        gq = sb("gq", [EX, C])
        gqT = sb("gqT", [P, EX])
        temp = sb("temp", [P, 1])
        itemp = sb("itemp", [P, 1])
        xs = sb("xs", [P, 2, NT, C])
        xT = sb("xT", [P, 2, T])
        tok = sb("tok", [P, NT, NB * EX])
        top = sb("top", [P, R])
        ex = sb("ex", [P, NT, NB * EX])
        total = sb("total", [P, R])
        logs = sb("logs", [P, R])
        row = sb("row", [P, EG, T])
        ntopA = sb("ntopA", [P, EG])
        totalA = sb("totalA", [P, EG])
        logsA = sb("logsA", [P, EG])
        aff = sb("aff", [P, EG, T])
        idx_u = sb("idx_u", [P, EG, CAP], U32)
        pX = ps("pX", [P, 2, 512])
        pL = ps("pL", [P, 2, 512])
        pA = ps("pA", [P, 512])
        pB = ps("pB", [P, 512])

        s_c = sem("loaded", False)
        s_g = sem("gq_turned", False)
        s_gc = sem("gq_copied", False)
        s_t = sem("temp_inverted", False)
        s_xs = sem("x_staged")
        s_xTp = sem("x_turned")
        s_xT = sem("xT_copied")
        s_l = sem("logits")
        s_lc = sem("logits_copied")
        s_top = sem("top_found")
        s_sub = sem("top_taken_off")
        s_ex = sem("exped")
        s_sum = sem("summed")
        s_ln = sem("logged")
        s_B = sem("expert_half_done")
        s_TA = sem("turned_to_rows")
        s_topA = sem("row_top_found")
        s_exA = sem("rows_exped")
        s_lnA = sem("rows_logged")
        s_A = sem("token_half_done")
        s_TB = sem("turned_back")
        s_tok = sem("copied_back")
        s_aff = sem("affinities", False)
        s_k = sem("top_k_steps", False)
        s_held = sem("waits_passed", False)
        ctx.callback(clear_semaphores, nc, every)
        block = ctx.enter_context(nc.Block())

        @block.sync
        def _(sp):
            sp.dma_start(gq[:, :], weights["gate_query"]).then_inc(s_c, 16)
            sp.dma_start(temp[:, :], weights["log_temp"].broadcast_to([P, 1])).then_inc(s_c, 16)

        @block.gpsimd
        def _(pool):
            for s in sems:
                pool.sem_inc(s, START)

            with pool.Fori(0, NB // 2) as i:
                for u in range(2):
                    b = 2 * i + u
                    after(pool, s_xTp, b - 1)
                    held(pool, s_held)
                    nc.gpsimd.tensor_copy(xs[:, u, :, :], X[:, bass.ds(NT * b, NT), :]).then_inc(s_xs, 1)

        @block.tensor
        def _(pe):
            pe.wait_ge(s_c, 32)
            nc.tensor.transpose(pA[:, 0:EX], gq[:, :], ident[0:EX, 0:EX]).then_inc(s_g, 1)
            pe.wait_ge(s_gc, 1)
            with pe.Fori(0, NB // 2) as i:
                for u in range(2):
                    b = 2 * i + u
                    after(pe, s_xs, b + 1)
                    after(pe, s_xT, b - 1)
                    for j in range(NT):
                        last = nc.tensor.transpose(pX[:, u, j * P:(j + 1) * P], xs[:, u, j, :], ident[:, :])
                    last.then_inc(s_xTp, 1)
                    after(pe, s_xT, b + 1)
                    after(pe, s_lc, b - 1)
                    for j in range(NT):
                        last = nc.tensor.matmul(pL[:, u, j * EX:(j + 1) * EX], xT[:, u, j * P:(j + 1) * P], gqT[:, :],
                                                start=True, stop=True)
                    last.then_inc(s_l, 1)
            with pe.Fori(0, ITERS) as k:
                after(pe, s_B, k + 1)
                for g in range(EG):
                    for j in range(NT):
                        last = nc.tensor.transpose(pA[:, g * T + j * P:g * T + (j + 1) * P],
                                                   tok[:, j, g * P:(g + 1) * P], ident[:, :])
                last.then_inc(s_TA, 1)
                after(pe, s_A, k + 1)
                for j in range(NT):
                    for g in range(EG):
                        last = nc.tensor.transpose(pB[:, j * NB * EX + g * P:j * NB * EX + (g + 1) * P],
                                                   row[:, g, j * P:(j + 1) * P], ident[:, :])
                last.then_inc(s_TB, 1)

        @block.scalar
        def _(act):
            act.wait_ge(s_c, 32)
            nc.scalar.activation(itemp[:, :], temp[:, :], ACT.Exp, scale=-1.0).then_inc(s_t, 1)
            with act.Fori(0, NB // 2) as i:
                for u in range(2):
                    b = 2 * i + u
                    after(act, s_l, b - 1)
                    after(act, s_xTp, b + 1)
                    nc.scalar.copy(xT[:, u, :], pX[:, u, 0:T]).then_inc(s_xT, 1)
            with act.Fori(0, ITERS) as k:
                after(act, s_sub, k + 1)
                nc.scalar.activation(ex[:, :, :], tok[:, :, :], ACT.Exp).then_inc(s_ex, 1)
                after(act, s_sum, k + 1)
                nc.scalar.activation(logs[:, :], total[:, :], ACT.Ln).then_inc(s_ln, 1)
                after(act, s_topA, k + 1)
                for g in range(EG):
                    last = nc.scalar.activation(aff[:, g, :], pA[:, g * T:(g + 1) * T], ACT.Exp,
                                                bias=ntopA[:, g:g + 1], accum_out=totalA[:, g:g + 1])
                last.then_inc(s_exA, 1)
                after(act, s_exA, k + 1)
                nc.scalar.activation(logsA[:, :], totalA[:, :], ACT.Ln).then_inc(s_lnA, 1)
                after(act, s_TB, k + 1)
                nc.scalar.copy(tok[:, :, :].rearrange("p j r -> p (j r)"), pB[:, :]).then_inc(s_tok, 1)
            nc.scalar.activation(aff[:, :, :], row[:, :, :], ACT.Exp).then_inc(s_aff, 1)

        @block.vector
        def _(dve):
            dve.wait_ge(s_g, 1)
            nc.vector.tensor_copy(gqT[:, :], pA[:, 0:EX]).then_inc(s_gc, 1)
            dve.wait_ge(s_t, 1)
            with dve.Fori(0, NB // 2) as i:
                for u in range(2):
                    b = 2 * i + u
                    after(dve, s_l, b + 1)
                    nc.vector.tensor_scalar(tok[:, :, bass.ds(b * EX, EX)],
                                            pL[:, u, 0:NT * EX].rearrange("p (j e) -> p j e", j=NT),
                                            itemp[:, 0:1], None, ALU.mult).then_inc(s_lc, 1)
            tok_e = tok[:, :, :].rearrange("p j (b e) -> p (j b) e", e=EX)
            ex_e = ex[:, :, :].rearrange("p j (b e) -> p (j b) e", e=EX)
            after(dve, s_lc, NB)
            with dve.Fori(0, ITERS) as k:
                after(dve, s_tok, k)
                nc.vector.tensor_reduce(top[:, :], tok_e, AX.X, ALU.max).then_inc(s_top, 1)
                after(dve, s_top, k + 1)
                nc.vector.tensor_tensor(tok_e, tok_e, bcast(top[:, :], 2, EX), ALU.subtract).then_inc(s_sub, 1)
                after(dve, s_ex, k + 1)
                nc.vector.tensor_reduce(total[:, :], ex_e, AX.X, ALU.add).then_inc(s_sum, 1)
                after(dve, s_ln, k + 1)
                nc.vector.tensor_tensor(tok_e, tok_e, bcast(logs[:, :], 2, EX), ALU.subtract).then_inc(s_B, 1)
                after(dve, s_TA, k + 1)
                nc.vector.tensor_reduce(ntopA[:, :], pA[:, :].rearrange("p (g n) -> p g n", g=EG), AX.X, ALU.max,
                                        negate=True).then_inc(s_topA, 1)
                after(dve, s_lnA, k + 1)
                for g in range(EG):
                    last = nc.vector.tensor_scalar(row[:, g, :], pA[:, g * T:(g + 1) * T], ntopA[:, g:g + 1],
                                                   logsA[:, g:g + 1], ALU.add, ALU.subtract)
                last.then_inc(s_A, 1)
            dve.wait_ge(s_aff, 1)
            at = 0
            for r in range(CAP // 8):
                for g in range(EG):
                    best = val[:, g, 8 * r:8 * r + 8]
                    nc.vector.max(best, aff[:, g, :]).then_inc(s_k, 1)
                    at += 1
                    dve.wait_ge(s_k, at)
                    nc.vector.max_index(idx_u[:, g, 8 * r:8 * r + 8], best, aff[:, g, :]).then_inc(s_k, 1)
                    nc.vector.match_replace(aff[:, g, :], best, aff[:, g, :], -1.0).then_inc(s_k, 1)
                    at += 2
                    dve.wait_ge(s_k, at)
            nc.vector.tensor_copy(idx[:, :, :], idx_u[:, :, :]).then_inc(s_k, 1)


def gather(nc, env, consts, idx, val, XG, slot_idx, slot_val):
    X = env["X"]
    ident = env["ident"]
    with ExitStack() as ctx:
        def sb(name, shape, dt=F32):
            return ctx.enter_context(nc.sbuf_tensor("g_" + name, shape, dt))

        def ps(name, shape):
            return ctx.enter_context(nc.psum_tensor("g_" + name, shape, F32))

        sems, every = [], []

        def sem(name, counted=True):
            s = ctx.enter_context(nc.semaphore("g_" + name))
            every.append(s)
            if counted:
                sems.append(s)
            return s

        sel_f = sb("sel_f", [P, BG])
        sel = sb("sel", [P, BG, P], BF16)
        own = sb("own", [P, EX])
        token = sb("token", [P, NT])
        diag = sb("diag", [P, EG, EX, CAP], BF16)
        wide = sb("wide", [P, EG, EX, CAP])
        xs = sb("xs", [P, 2, NT, C])
        hot = sb("hot", [P, 2, NT, EX * CAP])
        pI = ps("pI", [P, 2, 512])
        pG = ps("pG", [P, 2, 512])
        pT = ps("pT", [P, 2, 2, P])
        s_c = sem("loaded", False)
        s_wide = sem("idx_widened", False)
        s_sel = sem("selectors_made", False)
        s_T = sem("idx_turned", False)
        s_xs = sem("x_staged")
        s_I = sem("idx_spread")
        s_hot = sem("one_hot_made")
        s_G = sem("gathered")
        s_XG = sem("gathered_copied")
        s_held = sem("waits_passed", False)
        ctx.callback(clear_semaphores, nc, every)
        block = ctx.enter_context(nc.Block())

        @block.sync
        def _(sp):
            sp.dma_start(sel_f[:, :], consts["row_sequence"]).then_inc(s_c, 16)
            sp.dma_start(own[:, :], consts["row_expert"]).then_inc(s_c, 16)
            sp.dma_start(token[:, :], consts["token"]).then_inc(s_c, 16)

        @block.gpsimd
        def _(pool):
            for s in sems:
                pool.sem_inc(s, START)
            with pool.Fori(0, NB // 2) as i:
                for u in range(2):
                    b = 2 * i + u
                    after(pool, s_G, b - 1)
                    held(pool, s_held)
                    nc.gpsimd.tensor_copy(xs[:, u, :, :], X[:, bass.ds(NT * b, NT), :]).then_inc(s_xs, 1)

        @block.tensor
        def _(pe):
            for g in range(EG):
                for n, src in enumerate((idx, val)):
                    last = nc.tensor.transpose(pT[0:CAP, g, n, :], src[:, g, :], ident[:, :])
            last.then_inc(s_T, 1)
            pe.wait_ge(s_sel, 2)

            def spread(g, bb, u):
                after(pe, s_hot, g * BG + bb - 1)
                nc.tensor.matmul(pI[:, u, :], sel[:, bass.ds(bb, 1), :].rearrange("p o n -> p (o n)"),
                                 diag[:, g, :, :], start=True, stop=True).then_inc(s_I, 1)

            def collect(b, u):
                after(pe, s_hot, b + 1)
                after(pe, s_xs, b + 1)
                after(pe, s_XG, b - 1)
                for j in range(NT):
                    last = nc.tensor.matmul(pG[:, u, :], xs[:, u, j, :], hot[:, u, j, :],
                                            start=(j == 0), stop=(j == NT - 1))
                last.then_inc(s_G, 1)

            for g in range(EG):
                spread(g, 0, 0)
                with pe.Fori(0, BG // 2 - 1) as i:
                    for u in range(2):
                        spread(g, 2 * i + u + 1, 1 - u)
                        collect(g * BG + 2 * i + u, u)
                spread(g, BG - 1, 1)
                collect(g * BG + BG - 2, 0)
                collect(g * BG + BG - 1, 1)

        @block.vector
        def _(dve):
            dve.wait_ge(s_c, 48)
            for g in range(EG):
                nc.vector.tensor_tensor(diag[:, g, :, :], bcast(idx[:, g, :], 1, EX), bcast(own[:, :], 2, CAP),
                                        ALU.mult)
            nc.vector.memset(wide[:, 0, :, :], 1.0).then_inc(s_wide, 1)
            dve.wait_ge(s_wide, 1)
            for bb in range(BG):
                last = nc.vector.tensor_scalar(sel[:, bb, :], wide[:, 0, 0:P // CAP, :].rearrange("p e s -> p (e s)"),
                                               sel_f[:, bb:bb + 1], None, ALU.mult)
            last.then_inc(s_sel, 2)
            dve.wait_ge(s_T, 1)
            for g in range(EG):
                for n, dst in enumerate((slot_idx, slot_val)):
                    t = pT[0:CAP, g, n, :].rearrange("p (b q k) -> p b q k", b=BG, k=4)
                    for k in range(4):
                        nc.vector.tensor_copy(dst[CAP * k:CAP * (k + 1), g * BG:(g + 1) * BG, :], t[:, :, :, k])
            with dve.Fori(0, NB // 2) as i:
                for u in range(2):
                    b = 2 * i + u
                    after(dve, s_I, b + 1)
                    after(dve, s_G, b - 1)
                    for j in range(NT):
                        last = nc.vector.tensor_scalar(hot[:, u, j, :], pI[:, u, :], token[:, j:j + 1], None,
                                                       ALU.is_equal)
                    last.then_inc(s_hot, 1)

        @block.scalar
        def _(act):
            with act.Fori(0, NB // 2) as i:
                for u in range(2):
                    b = 2 * i + u
                    after(act, s_G, b + 1)
                    nc.scalar.copy(XG[:, :, bass.ds(b * CAP, CAP)],
                                   pG[:, u, :].rearrange("p (e s) -> p e s", e=EX)).then_inc(s_XG, 1)


def experts(nc, env, weights, XG, Y):
    KF = FF // P
    NTK = NB * CAP // P
    ident = env["ident"]
    with ExitStack() as ctx:
        def sb(name, shape, dt=F32):
            return ctx.enter_context(nc.sbuf_tensor("e_" + name, shape, dt))

        def ps(name, shape):
            return ctx.enter_context(nc.psum_tensor("e_" + name, shape, F32))

        sems, every = [], []

        def sem(name, counted=True):
            s = ctx.enter_context(nc.semaphore("e_" + name))
            every.append(s)
            if counted:
                sems.append(s)
            return s

        w1 = sb("w1", [P, 4, FF])
        w2 = sb("w2", [P, 4, KF, C])
        b2 = sb("b2", [P, 4, C])
        b1r = sb("b1r", [EX * KF, P])
        b1 = sb("b1", [P, EX * KF])
        b1e = sb("b1e", [P, 2, KF])
        hT = sb("hT", [P, 2, KF, NB * CAP])
        ye = sb("ye", [P, 2, NTK, C])
        pH = ps("pH", [P, 4, 512])
        pY = ps("pY", [P, 2, 512])
        pB = ps("pB", [P, 512])
        s_b = sem("b1_loaded", False)
        s_bT = sem("b1_turned", False)
        s_bc = sem("b1_copied", False)
        s_w = [sem(f"weights_loaded{r}", False) for r in range(4)]
        s_be = sem("expert_bias")
        s_h = sem("hidden")
        s_g = sem("gelu_done")
        s_y = sem("out_made")
        s_ye = sem("out_copied")
        s_Y = [sem(f"out_moved{u}", False) for u in range(2)]
        s_held = sem("waits_passed", False)
        ctx.callback(clear_semaphores, nc, every)
        block = ctx.enter_context(nc.Block())

        @block.sync
        def _(sp):
            sp.dma_start(b1r[:, :], weights["b1"].rearrange("e (k p) -> (e k) p", p=P)).then_inc(s_b, 16)

            def load(e, r):
                after(sp, s_y, e - 3)
                sp.dma_start(w1[:, r, :], weights["w1"][bass.ds(e, 1)].rearrange("o d f -> d (o f)")
                             ).then_inc(s_w[r], 16)
                sp.dma_start(w2[:, r, :, :], weights["w2"][bass.ds(e, 1)].rearrange("o (k p) d -> p (o k) d", p=P)
                             ).then_inc(s_w[r], 16)
                after(sp, s_ye, e - 3)
                sp.dma_start(b2[:, r, :], weights["b2"][bass.ds(e, 1)].broadcast_to([P, C])).then_inc(s_w[r], 16)

            def move(q, r):
                after(sp, s_ye, 4 * q + r + 1)
                for g in range(4):
                    sp.dma_start(
                        Y[CAP * r:CAP * (r + 1), bass.ds(q, 1), :, :]
                        .rearrange("p o (k g) c -> p (o k) g c", g=4)[:, :, g, :],
                        ye[CAP * g:CAP * (g + 1), r % 2, :, :]).then_inc(s_Y[r % 2], 16)

            def four(q, last):
                for r in range(4):
                    if not (last and r):
                        load(4 * q + r + 3, (r + 3) % 4)
                    move(q, r)

            for r in range(3):
                load(r, r)
            with sp.Fori(0, EX // 4 - 1) as q:
                four(q, False)
            four(EX // 4 - 1, True)
            for u in range(2):
                sp.wait_ge(s_Y[u], 64 * EX // 2 + START)

        @block.gpsimd
        def _(pool):
            for s in sems + s_Y:
                pool.sem_inc(s, START)
            pool.wait_ge(s_bc, 1)
            held(pool, s_held)
            with pool.Fori(0, EX // 2) as i:
                for u in range(2):
                    e = 2 * i + u
                    after(pool, s_g, KF * (e - 1))
                    held(pool, s_held)
                    nc.gpsimd.tensor_copy(b1e[:, u, :], b1[:, bass.ds(KF * e, KF)]).then_inc(s_be, 1)

        @block.tensor
        def _(pe):
            pe.wait_ge(s_b, 16)
            nc.tensor.transpose(pB[:, 0:EX * KF], b1r[:, :], ident[0:EX * KF, 0:EX * KF]).then_inc(s_bT, 1)

            def hidden(e, q, r):
                pe.wait_ge(s_w[r], 48 * (q + 1))
                for k in range(KF):
                    after(pe, s_g, KF * (e - 1) + k + 1)
                    nc.tensor.matmul(pH[:, k, :], w1[:, r, k * P:(k + 1) * P],
                                     XG[:, bass.ds(e, 1), :].rearrange("p o t -> p (o t)"),
                                     start=True, stop=True).then_inc(s_h, 1)

            def outputs(e, r):
                u = r % 2
                after(pe, s_g, KF * e + KF)
                after(pe, s_ye, e - 1)
                for t in range(NTK):
                    for k in range(KF):
                        last = nc.tensor.matmul(pY[:, u, t * C:(t + 1) * C], hT[:, u, k, t * P:(t + 1) * P],
                                                w2[:, r, k, :], start=(k == 0), stop=(k == KF - 1))
                last.then_inc(s_y, 1)

            def four(q, last):
                for r in range(4):
                    if not (last and r == 3):
                        hidden(4 * q + r + 1, q + (r + 1) // 4, (r + 1) % 4)
                    outputs(4 * q + r, r)

            hidden(0, 0, 0)
            with pe.Fori(0, EX // 4 - 1) as q:
                four(q, False)
            four(EX // 4 - 1, True)

        @block.scalar
        def _(act):
            with act.Fori(0, EX // 2) as i:
                for u in range(2):
                    e = 2 * i + u
                    after(act, s_be, e + 1)
                    after(act, s_y, e - 1)
                    for k in range(KF):
                        after(act, s_h, KF * e + k + 1)
                        nc.scalar.activation(hT[:, u, k, :], pH[:, k, :], ACT.Gelu_apprx_tanh,
                                             bias=b1e[:, u, k:k + 1]).then_inc(s_g, 1)

        @block.vector
        def _(dve):
            dve.wait_ge(s_bT, 1)
            nc.vector.tensor_copy(b1[:, :], pB[:, 0:EX * KF]).then_inc(s_bc, 1)
            with dve.Fori(0, EX // 4) as q:
                for r in range(4):
                    u, e = r % 2, 4 * q + r
                    after(dve, s_y, e + 1)
                    dve.wait_ge(s_w[r], 48 * (q + 1))
                    dve.wait_ge(s_Y[u], 64 * (2 * q + r // 2) + START)
                    nc.vector.tensor_tensor(ye[:, u, :, :], pY[:, u, :].rearrange("p (t c) -> p t c", t=NTK),
                                            bcast(b2[:, r, :], 1, NTK), ALU.add).then_inc(s_ye, 1)


def scatter(nc, env, consts, slot_idx, slot_val, Y):
    X, neghalf = env["X"], env["neghalf"]
    Q = EX // 4
    DVE_STEPS = 5
    with ExitStack() as ctx:
        def sb(name, shape, dt=F32):
            return ctx.enter_context(nc.sbuf_tensor("s_" + name, shape, dt))

        sems, every = [], []

        def sem(name, counted=True):
            s = ctx.enter_context(nc.semaphore("s_" + name))
            every.append(s)
            if counted:
                sems.append(s)
            return s

        iota = sb("iota", [P, T])
        sib = sb("sib", [P, 2, Q])
        svb = sb("svb", [P, 2, Q])
        hot = sb("hot", [P, 2, Q, T])
        z = sb("z", [P, NT, C])
        st = sb("st", [P, NT, 6])
        mv = sb("mv", [P, NT, 2])
        rstd = sb("rstd", [P, NT])
        pO = ctx.enter_context(nc.psum_tensor("s_pO", [P, 2, 512], F32))
        s_c = sem("loaded", False)
        s_s = sem("slots_staged")
        s_hot = sem("gates_placed")
        s_O = sem("scattered")
        s_z = sem("summed")
        s_mv = sem("stats_made")
        s_rstd = sem("rstd_made")
        s_x = sem("x_written")
        s_dve = sem("dve_steps")
        s_held = sem("waits_passed", False)
        ctx.callback(clear_semaphores, nc, every)
        block = ctx.enter_context(nc.Block())

        @block.sync
        def _(sp):
            sp.dma_start(iota[:, :], consts["iota"]).then_inc(s_c, 16)

        @block.gpsimd
        def _(pool):
            for s in sems:
                pool.sem_inc(s, START)

            def one(b, u, nxt):
                after(pool, s_mv, b + 1)
                nc.gpsimd.tensor_tensor(rstd[:, :], mv[:, :, 1], neghalf[:, 0:NT], ALU.pow).then_inc(s_rstd, 1)
            looped(pool, one)

        @block.scalar
        def _(act):
            def stage(q, u):
                after(act, s_hot, q - 1)
                nc.scalar.copy(sib[:, u, :], slot_idx[:, bass.ds(q, 1), :].rearrange("p o q -> p (o q)"))
                nc.scalar.copy(svb[:, u, :], slot_val[:, bass.ds(q, 1), :].rearrange("p o q -> p (o q)")
                               ).then_inc(s_s, 1)

            def one(b, u, nxt):
                if not (isinstance(b, int) and b >= NB - 2):
                    stage(b + 2, u)

            stage(0, 0)
            stage(1, 1)
            looped(act, one)

        @block.tensor
        def _(pe):
            def one(b, u, nxt):
                after(pe, s_hot, b + 1)
                after(pe, s_z, b - 1)
                for j in range(NT):
                    for q in range(Q):
                        last = nc.tensor.matmul(
                            pO[:, u, j * C:(j + 1) * C], hot[:, u, q, j * P:(j + 1) * P],
                            Y[:, q, bass.ds(b, 1), :].rearrange("p o c -> p (o c)"),
                            start=(q == 0), stop=(q == Q - 1))
                last.then_inc(s_O, 1)
            looped(pe, one)

        @block.vector
        def _(dve):
            steps = Steps(dve, s_dve, DVE_STEPS, s_held)
            dve.wait_ge(s_c, 16)

            def place(q, u):
                after(dve, s_s, q + 1)
                after(dve, s_O, q - 1)
                for k in range(Q):
                    last = nc.vector.tensor_scalar(hot[:, u, k, :], iota[:, :], sib[:, u, k:k + 1],
                                                   svb[:, u, k:k + 1], ALU.is_equal, ALU.mult)
                last.then_inc(s_hot, 1)

            def one(b, u, nxt):
                steps.start(b)
                after(dve, s_O, b + 1)
                nc.vector.tensor_tensor(z[:, :, :], pO[:, u, 0:T].rearrange("p (j c) -> p j c", j=NT),
                                        X[:, bass.ds(NT * b, NT), :], ALU.add).then_inc(s_z, 1)
                after(dve, s_z, b + 1)
                for j in range(NT):
                    steps.inc(nc.vector.bn_stats(st[:, j, :], z[:, j, :]))
                after(dve, s_dve, steps.base + steps.count)
                held(dve, s_held)
                for j in range(NT):
                    steps.inc(nc.vector.bn_aggr(mv[:, j, :], st[:, j, :]))
                after(dve, s_dve, steps.base + steps.count)
                steps.inc(nc.vector.tensor_scalar(mv[:, :, 1], mv[:, :, 1], LN_EPS, None, ALU.add))
                after(dve, s_dve, steps.base + steps.count)
                dve.sem_inc(s_mv, 1)
                if not (isinstance(b, int) and b >= NB - 2):
                    place(b + 2, u)
                after(dve, s_rstd, b + 1)
                for j in range(NT):
                    last = nc.vector.tensor_scalar(
                        X[:, bass.ds(NT * b + j, 1), :].rearrange("p o c -> p (o c)"), z[:, j, :],
                        mv[:, j, 0:1], rstd[:, j:j + 1], ALU.subtract, ALU.mult)
                last.then_inc(s_x, 1)
                after(dve, s_x, b + 1)
                held(dve, s_held)
                steps.end()

            place(0, 0)
            place(1, 1)
            looped(dve, one)


def l0_experts(nc, env, weights, consts):
    with ExitStack() as ctx:
        def sb(name, shape):
            return ctx.enter_context(nc.sbuf_tensor("m_" + name, shape, F32))

        idx = sb("idx", [P, EG, CAP])
        val = sb("val", [P, EG, CAP])
        slot_idx = sb("slot_idx", [P, NB, EX // 4])
        slot_val = sb("slot_val", [P, NB, EX // 4])
        XG = sb("XG", [P, EX, NB * CAP])
        Y = sb("Y", [P, EX // 4, NB, C])
        router(nc, env, weights, consts, idx, val)
        gather(nc, env, consts, idx, val, XG, slot_idx, slot_val)
        experts(nc, env, weights, XG, Y)
        scatter(nc, env, consts, slot_idx, slot_val, Y)


def l1_attention(nc, env, weights, consts):
    LOOK, START = 32, 64
    KW = LOOK + P
    SCALE = 1.0 / np.sqrt(C)
    TAKEN = -3.0e38
    BEST_STEPS, DVE_STEPS = 10, 6
    ident, X, neghalf = env["ident"], env["X"], env["neghalf"]
    with ExitStack() as ctx:
        def sb(name, shape, dt=F32):
            return ctx.enter_context(nc.sbuf_tensor("c_" + name, shape, dt))

        def ps(name, shape):
            return ctx.enter_context(nc.psum_tensor("c_" + name, shape, F32))

        sems, every = [], []

        def sem(name, counted=True):
            s = ctx.enter_context(nc.semaphore("c_" + name))
            every.append(s)
            if counted:
                sems.append(s)
            return s

        raw = sb("raw", [P, 5, C])
        wT = sb("wT", [P, 5, C])
        bias = sb("bias", [P, 3])
        vbias = sb("vbias", [P, 2, C])
        prefix = sb("prefix", [P, P])
        mask = sb("mask", [P, 2, KW])
        prev = sb("prev", [P, KW])
        notfirst = sb("notfirst", [P, NT])
        xs = sb("xs", [P, 2, NT, C])
        xT = sb("xT", [P, 2, T])
        qT = sb("qT", [P, 2, 3, T])
        v = sb("v", [P, 2, NT, 2, C])
        vp = sb("vp", [LOOK, 2, 2, C])
        S = sb("S", [P, NT, 2, KW])
        B = sb("B", [P, NT, KW])
        best = sb("best", [P, NT, 2, 8])
        E = sb("E", [P, NT, 2, KW])
        pick = sb("pick", [P, NT, 2, KW])
        Wt = sb("Wt", [P, NT, 2, KW])
        WT = sb("WT", [P, NT, 2 * P + 2 * LOOK])
        mx = sb("mx", [P, NT])
        nmx = sb("nmx", [P, NT])
        rs = sb("rs", [P, NT])
        ri = sb("ri", [P, NT])
        z = sb("z", [P, NT, C])
        st = sb("st", [P, NT, 6])
        mv = sb("mv", [P, NT, 2])
        rstd = sb("rstd", [P, NT])

        pX = ps("pX", [P, 512])
        pQ = ps("pQ", [P, 512])
        pK = ps("pK", [P, 512])
        pV = ps("pV", [P, 512])
        pS = ps("pS", [P, 2, 512])
        pT = ps("pT", [P, 512])
        pO = ps("pO", [P, 512])

        s_c = sem("constants_loaded", False)
        s_w = sem("weights_turned", False)
        s_wc = sem("weights_copied", False)
        s_one = sem("pick_set", False)
        s_xs = sem("x_staged")
        s_xTp = sem("x_turned")
        s_xT = sem("xT_copied")
        s_proj = sem("projected")
        s_q = sem("q_k_copied")
        s_pk = sem("pk_copied")
        s_v = sem("v_copied")
        s_S = sem("scored")
        s_m = sem("maxed")
        s_nm = sem("max_negated")
        s_E = sem("exped")
        s_W = sem("weights_made")
        s_T = sem("wts_turned")
        s_WT = sem("wts_copied")
        s_PV = sem("pv_done")
        s_z = sem("summed")
        s_mv = sem("stats_made")
        s_rstd = sem("rstd_made")
        s_x = sem("x_written")
        s_dve = sem("dve_steps")
        s_best = sem("best_steps")
        s_held = sem("waits_passed", False)
        ctx.callback(clear_semaphores, nc, every)
        block = ctx.enter_context(nc.Block())

        def after(eng, s, value):
            eng.wait_ge(s, value + START)

        def before(b, u):
            return [] if isinstance(b, int) and b == 0 else [(b - 1, 1 - u)]

        NAMES = ["q", "k", "pk", "v", "pv"]

        @block.sync
        def _(sp):
            for n, name in enumerate(NAMES):
                sp.dma_start(raw[:, n, :], weights[name + "_w"]).then_inc(s_c, 16)
            for n, name in enumerate(NAMES[:3]):
                sp.dma_start(bias[:, n:n + 1], weights[name + "_b"].rearrange("(p o) -> p o", o=1)).then_inc(s_c, 16)
            for n, name in enumerate(NAMES[3:]):
                sp.dma_start(vbias[:, n, :], weights[name + "_b"].rearrange("(o p) -> o p", o=1)
                             .broadcast_to([P, C])).then_inc(s_c, 16)
            sp.dma_start(prefix[:, :], consts["prefix"]).then_inc(s_c, 16)
            sp.dma_start(mask[:, :, :], consts["look_mask"].rearrange("p (t k) -> p t k", t=2)).then_inc(s_c, 16)
            sp.dma_start(prev[:, :], consts["prev"]).then_inc(s_c, 16)
            sp.dma_start(notfirst[:, :], consts["notfirst"]).then_inc(s_c, 16)
        N_C = 16 * 14

        @block.gpsimd
        def _(pool):
            for s in sems:
                pool.sem_inc(s, START)
            nc.gpsimd.memset(pick[:, :, 1, :], 1.0).then_inc(s_one, 1)

            def stage(q, u):
                after(pool, s_xTp, q - 1)
                held(pool, s_held)
                nc.gpsimd.tensor_copy(xs[:, u, :, :], X[:, bass.ds(NT * q, NT), :]).then_inc(s_xs, 1)

            def rsqrt(b):
                after(pool, s_mv, b + 1)
                nc.gpsimd.tensor_tensor(rstd[:, :], mv[:, :, 1], neghalf[:, 0:NT], ALU.pow).then_inc(s_rstd, 1)

            def one(b, u, nxt):
                if not (isinstance(b, int) and b >= NB - 2):
                    stage(b + 2, u)
                for done, _ in before(b, u):
                    rsqrt(done)

            stage(0, 0)
            stage(1, 1)
            passes(pool, one)
            rsqrt(NB - 1)

        @block.tensor
        def _(pe):
            pe.wait_ge(s_c, N_C)
            for n in range(5):
                if n >= 4:
                    pe.wait_ge(s_wc, n - 3)
                nc.tensor.transpose((pX, pQ, pK, pV)[n % 4][:, 0:C], raw[:, n, :], ident[:, :]).then_inc(s_w, 1)
            pe.wait_ge(s_wc, 5)

            def turn_x(q, u):
                after(pe, s_xs, q + 1)
                after(pe, s_xT, q)
                for j in range(NT):
                    nc.tensor.transpose(pX[:, j * P:(j + 1) * P], xs[:, u, j, :], ident[:, :])
                for j in range(NT):
                    last = nc.tensor.matmul(pX[:, T + j * P:T + (j + 1) * P], xs[:, u, j, :], prefix[:, :],
                                            start=True, stop=True)
                last.then_inc(s_xTp, 1)

            def project(q):
                after(pe, s_xT, q + 1)
                after(pe, s_q, 2 * q)
                for n in range(2):
                    last = nc.tensor.matmul(pQ[:, n * T:(n + 1) * T], wT[:, n, :], xT[:, 0, :], start=True, stop=True)
                last.then_inc(s_proj, 1)
                after(pe, s_pk, q)
                nc.tensor.matmul(pK[:, 0:T], wT[:, 2, :], xT[:, 1, :], start=True, stop=True)
                for n in range(2):
                    last = nc.tensor.matmul(pK[0:LOOK, T + n * C:T + (n + 1) * C], xT[:, n, P - LOOK:P],
                                            wT[:, 3 + n, :], start=True, stop=True)
                last.then_inc(s_proj, 1)
                after(pe, s_v, q)
                for j in range(NT):
                    for n in range(2):
                        last = nc.tensor.matmul(pV[:, (2 * j + n) * C:(2 * j + n + 1) * C],
                                                xT[:, n, j * P:(j + 1) * P], wT[:, 3 + n, :], start=True, stop=True)
                last.then_inc(s_proj, 1)

            def scores(b, u, j):
                if j == 0:
                    after(pe, s_q, 2 * b + 2)
                    after(pe, s_pk, b + 1)
                after(pe, s_m, 2 * b + j - 1)
                o = LOOK * (1 - j)
                lo = 0 if j == 0 else P - LOOK
                for n in range(2):
                    last = nc.tensor.matmul(pS[:, j, n * KW + o:(n + 1) * KW], qT[:, u, 0, j * P:(j + 1) * P],
                                            qT[:, u, 1 + n, lo:(j + 1) * P], start=True, stop=True)
                last.then_inc(s_S, 1)

            def mix(b, u, j):
                after(pe, s_W, 2 * b + j + 1)
                after(pe, s_WT, 2 * b + j)
                for n in range(2):
                    last = nc.tensor.transpose(pT[:, n * P:(n + 1) * P], Wt[:, j, n, LOOK:KW], ident[:, :])
                if j:
                    for n in range(2):
                        o = 2 * P + n * LOOK
                        last = nc.tensor.transpose(pT[0:LOOK, o:o + LOOK], Wt[0:LOOK, j, n, 0:LOOK],
                                                   ident[0:LOOK, 0:LOOK])
                last.then_inc(s_T, 1)
                after(pe, s_WT, 2 * b + j + 1)
                if j == 0:
                    after(pe, s_v, b + 1)
                    after(pe, s_z, b)
                out = pO[:, j * C:(j + 1) * C]
                for n in range(2):
                    last = nc.tensor.matmul(out, WT[:, j, n * P:(n + 1) * P], v[:, u, j, n, :],
                                            start=(n == 0), stop=(n == 1))
                if j:
                    for n in range(2):
                        o = 2 * P + n * LOOK
                        last = nc.tensor.matmul(out[0:LOOK, :], WT[0:LOOK, j, o:o + LOOK], vp[:, u, n, :],
                                                start=False, stop=True, skip_group_check=True)
                last.then_inc(s_PV, 1)

            def one(b, u, nxt):
                if nxt:
                    turn_x(nxt[0], nxt[2])
                scores(b, u, 0)
                scores(b, u, 1)
                for done, v in before(b, u):
                    mix(done, v, 0)
                    mix(done, v, 1)
                if nxt:
                    project(nxt[0])

            turn_x(0, 0)
            project(0)
            passes(pe, one)
            mix(NB - 1, 1, 0)
            mix(NB - 1, 1, 1)

        @block.scalar
        def _(act):
            act.wait_ge(s_c, N_C)

            def copy_x(q):
                after(act, s_proj, 3 * q)
                after(act, s_xTp, q + 1)
                nc.scalar.copy(xT[:, :, :].rearrange("p n t -> p (n t)"), pX[:, :]).then_inc(s_xT, 1)

            def copy_q(q, u):
                after(act, s_S, 2 * (q - 1))
                after(act, s_proj, 3 * q + 1)
                for n in range(2):
                    nc.scalar.activation(qT[:, u, n, :], pQ[:, n * T:(n + 1) * T], ACT.Identity,
                                         bias=bias[:, n:n + 1]).then_inc(s_q, 1)

            def exps(b, j):
                after(act, s_nm, 2 * b + j + 1)
                after(act, s_W, 2 * b + j - 1)
                o = LOOK * (1 - j)
                nc.scalar.activation(E[:, j, :, o:KW], S[:, j, :, o:KW], ACT.Exp, bias=nmx[:, j:j + 1]
                                     ).then_inc(s_E, 1)

            def copy_weights(b, j):
                after(act, s_T, 2 * b + j + 1)
                after(act, s_PV, 2 * b + j - 1)
                last = nc.scalar.copy(WT[:, j, 0:2 * P], pT[:, 0:2 * P])
                if j:
                    last = nc.scalar.copy(WT[0:LOOK, j, 2 * P:], pT[0:LOOK, 2 * P:2 * P + 2 * LOOK])
                last.then_inc(s_WT, 1)

            def one(b, u, nxt):
                if nxt:
                    copy_x(nxt[0])
                for done, _ in before(b, u):
                    copy_weights(done, 0)
                    copy_weights(done, 1)
                if nxt:
                    copy_q(nxt[0], nxt[2])
                exps(b, 0)
                exps(b, 1)

            copy_x(0)
            copy_q(0, 0)
            passes(act, one)
            copy_weights(NB - 1, 0)
            copy_weights(NB - 1, 1)

        @block.vector
        def _(dve):
            steps = Steps(dve, s_dve, DVE_STEPS, s_held)
            best_steps = Steps(dve, s_best, BEST_STEPS)

            def linked(ins):
                steps.inc(ins)
                after(dve, s_dve, steps.base + steps.count)
                held(dve, s_held)

            dve.wait_ge(s_c, N_C)
            for n in range(5):
                dve.wait_ge(s_w, n + 1)
                nc.vector.tensor_copy(wT[:, n, :], (pX, pQ, pK, pV)[n % 4][:, 0:C]).then_inc(s_wc, 1)
            dve.wait_ge(s_one, 1)

            def copy_pk_v(q, u):
                after(dve, s_PV, 2 * (q - 1))
                after(dve, s_proj, 3 * q + 2)
                nc.vector.tensor_scalar(qT[:, u, 2, :], pK[:, 0:T], bias[:, 2:3], None, ALU.add)
                nc.vector.tensor_tensor(vp[:, u, :, :], pK[0:LOOK, T:2 * T].rearrange("p (n c) -> p n c", n=2),
                                        vbias[0:LOOK, :, :], ALU.add).then_inc(s_pk, 1)
                after(dve, s_proj, 3 * q + 3)
                nc.vector.tensor_tensor(v[:, u, :, :, :].rearrange("p j n c -> p j (n c)"),
                                        pV[:, :].rearrange("p (j nc) -> p j nc", j=NT),
                                        bcast(vbias[:, :, :].rearrange("p n c -> p (n c)"), 1, NT), ALU.add
                                        ).then_inc(s_v, 1)

            def maxima(b, j):
                o = LOOK * (1 - j)
                after(dve, s_E, 2 * b + j - 1)
                after(dve, s_S, 2 * b + j + 1)
                held(dve, s_held)
                nc.vector.tensor_tensor_reduce(
                    out=S[:, j, :, o:KW], in0=pS[:, j, 0:2 * KW].rearrange("p (n k) -> p n k", n=2)[:, :, o:KW],
                    in1=mask[:, :, o:KW], scale=SCALE, scalar=-HUGE, op0=ALU.add, op1=ALU.max,
                    accum_out=mx[:, j:j + 1]).then_inc(s_m, 1)

            def negate(b, j):
                after(dve, s_m, 2 * b + j + 1)
                nc.vector.tensor_scalar(nmx[:, j:j + 1], mx[:, j:j + 1], -1.0, None, ALU.mult).then_inc(s_nm, 1)

            def best_16(b):
                best_steps.start(b)

                def both(step):
                    for j in range(NT):
                        best_steps.inc(step(j, slice(LOOK * (1 - j), KW)))
                    after(dve, s_best, best_steps.base + best_steps.count)
                    held(dve, s_held)

                both(lambda j, o: nc.vector.max(best[:, j, 0, :], S[:, j, 0, o]))
                both(lambda j, o: nc.vector.match_replace(B[:, j, o], best[:, j, 0, :], S[:, j, 0, o], TAKEN))
                both(lambda j, o: nc.vector.max(best[:, j, 1, :], B[:, j, o]))
                both(lambda j, o: nc.vector.match_replace(B[:, j, o], best[:, j, 1, :], B[:, j, o], TAKEN))
                both(lambda j, o: nc.vector.scalar_tensor_tensor(pick[:, j, 0, o], B[:, j, o], -2.0e38, prev[:, o],
                                                                 ALU.is_lt, ALU.add))
                best_steps.end()

            def make_weights(b, j):
                o = LOOK * (1 - j)
                after(dve, s_T, 2 * b + j - 1)
                after(dve, s_E, 2 * b + j + 1)
                held(dve, s_held)
                nc.vector.tensor_tensor_reduce(
                    out=Wt[:, j, :, o:KW], in0=pick[:, j, :, o:KW], in1=E[:, j, :, o:KW], scale=1.0, scalar=0.0,
                    op0=ALU.mult, op1=ALU.add, accum_out=rs[:, j:j + 1]).then_inc(s_W, 1)

            def stats(b):
                steps.start(b)
                after(dve, s_W, 2 * b + 2)
                linked(nc.vector.reciprocal(ri[:, :], rs[:, :]))
                linked(nc.vector.tensor_tensor(ri[:, :], ri[:, :], notfirst[:, :], ALU.mult))
                after(dve, s_PV, 2 * b + 2)
                for j in range(NT):
                    last = nc.vector.scalar_tensor_tensor(
                        z[:, j, :], pO[:, j * C:(j + 1) * C], ri[:, j:j + 1],
                        X[:, bass.ds(NT * b + j, 1), :].rearrange("p o c -> p (o c)"), ALU.mult, ALU.add)
                last.then_inc(s_z, 1)
                after(dve, s_z, b + 1)
                for j in range(NT):
                    steps.inc(nc.vector.bn_stats(st[:, j, :], z[:, j, :]))
                after(dve, s_dve, steps.base + steps.count)
                held(dve, s_held)
                for j in range(NT):
                    steps.inc(nc.vector.bn_aggr(mv[:, j, :], st[:, j, :]))
                after(dve, s_dve, steps.base + steps.count)
                nc.vector.tensor_scalar(mv[:, :, 1], mv[:, :, 1], LN_EPS, None, ALU.add).then_inc(s_mv, 1)
                steps.end()

            def write(b):
                after(dve, s_rstd, b + 1)
                for j in range(NT):
                    last = nc.vector.tensor_scalar(
                        X[:, bass.ds(NT * b + j, 1), :].rearrange("p o c -> p (o c)"), z[:, j, :],
                        mv[:, j, 0:1], rstd[:, j:j + 1], ALU.subtract, ALU.mult)
                last.then_inc(s_x, 1)
                after(dve, s_x, b + 1)
                held(dve, s_held)

            def one(b, u, nxt):
                maxima(b, 0)
                maxima(b, 1)
                negate(b, 0)
                negate(b, 1)
                best_16(b)
                for done, _ in before(b, u):
                    stats(done)
                if nxt:
                    copy_pk_v(nxt[0], nxt[2])
                make_weights(b, 0)
                make_weights(b, 1)
                for done, _ in before(b, u):
                    write(done)

            copy_pk_v(0, 0)
            passes(dve, one)
            stats(NB - 1)
            write(NB - 1)


def l1_network(nc, env, weights, consts):
    LAYERS, H, D, W = 6, 16, 64, 32
    I = H * D
    F = 341
    FC = [(0, P), (P, P), (2 * P, F - 2 * P)]
    KW = W + P
    NU, START, GR = 16, 64, 2
    NG = NB // GR
    TG = GR * NT
    NORM_STEPS = 13
    ident, X, neghalf = env["ident"], env["X"], env["neghalf"]

    def heads(n):
        h = 8 * (n % 8 // 4) + 4 * (n % 4 // 2) + n % 2
        return h, h + 2

    OWN = {11: [("o", 0)], 15: [("o", 1)], 19: [("o", 2)], 23: [("o", 3)], 25: [("y", 0)]}
    NEXT = {0: [("x", 0)]}
    for kind, at in (("qk", (1, 2, 3, 4, 6, 7, 8, 9)), ("v", (5, 10, 11, 12)),
                     ("turn", (10, 11, 12, 13, 13, 14, 14, 15))):
        for c, n in enumerate(at):
            NEXT.setdefault(n, []).append((kind, c))
    EXP_LAG, TURN_LAG, WEIGH_LAG, NORM_LAG, END = 1, 3, 5, 6, 26

    def place(c):
        return 1 - c // 4, c // 2 % 2, c % 2

    def slots(prev, nxt):
        before = [("turn", 6, 0), ("turn", 7, 0)]
        at = 0 if prev else 1
        out = {}
        for n in range(NU if nxt else END):
            out[n] = []
            for d, there, uses in ((-1, prev, OWN.get(n + NU, [])), (0, True, OWN.get(n, [])),
                                   (1, nxt, NEXT.get(n, []))):
                for kind, c in uses if there else []:
                    out[n].append((kind, c, d, at % 2, before[-2]))
                    before.append((kind, c, d))
                    at += 1
        assert not nxt or at % 2 == 0
        return out

    def lagged(N, u, n, lag, prev):
        m = n - lag
        if m < 0:
            return [(N - 1, 1 - u, m + NU)] if prev else []
        return [(N, u, m)] if m < NU else []

    PROLOGUE = [("x", 0)]
    for c in range(8):
        PROLOGUE += [("qk", c)] + ([("v", c // 2)] if c % 2 else [])
    PROLOGUE += [("turn", k) for k in range(8)]
    bank_of = {use: at % 2 for at, use in enumerate(u for u in PROLOGUE if u[0] != "v")}
    bank_of.update({("v", c): c % 2 for c in range(4)})

    with ExitStack() as ctx:
        def sb(name, shape, dt=F32):
            return ctx.enter_context(nc.sbuf_tensor("n_" + name, shape, dt))

        def ps(name, shape):
            return ctx.enter_context(nc.psum_tensor("n_" + name, shape, F32))

        sems, every = [], []

        def sem(name, counted=True):
            s = ctx.enter_context(nc.semaphore("n_" + name))
            every.append(s)
            if counted:
                sems.append(s)
            return s

        wqkv = sb("wqkv", [P, 3 * I])
        wo = sb("wo", [P, I // P, C])
        qks = sb("qks", [P, 2, D])
        w1 = sb("w1", [P, 2 * F])
        w2 = sb("w2", [P, 3, C])
        b1 = sb("b1", [P, 2, 3])
        lng = sb("lng", [P, 1])
        lnb = sb("lnb", [P, 1])
        b2 = sb("b2", [P, C])
        cos_c = sb("cos_c", [P, 2, NT, D])
        sin_c = sb("sin_c", [P, 2, NT, D])
        cosT = sb("cosT", [P, 2, NT, D])
        sinT = sb("sinT", [P, 2, NT, D])
        band = sb("band", [P, KW])
        xs = sb("xs", [P, 2, NT, C])
        xT = sb("xT", [P, T + 1])
        sq = sb("sq", [P, 2, 512])
        t1 = sb("t1", [P, 4, 512])
        t2 = sb("t2", [P, 4, 512])
        ss = sb("ss", [P, 2, 2, NT, H])
        rn = sb("rn", [P, 2, 2, NT, H])
        nt = sb("nt", [P, NT * H])
        pre = sb("pre", [P, NT, 2, I])
        qkT = sb("qkT", [P, 2, 2, I // P, T])
        V = sb("V", [P, 2, NT, I])
        vp = sb("vp", [W, 2, I])
        S = sb("S", [P, 4, 2, KW])
        E = sb("E", [P, 4, 2, KW])
        ET = sb("ET", [P, 4, 2 * P + 2 * W])
        nm = sb("nm", [P, 2, NT, H])
        rs = sb("rs", [P, 2, NT, H])
        ri = sb("ri", [P, 2, 8])
        On = sb("On", [P, NT, I])
        OT = sb("OT", [P, NT, I // P, P])
        fxs = sb("fxs", [P, TG, C])
        fsT = sb("fsT", [P, GR, T + 1])
        xn = sb("xn", [P, TG, C])
        xnT = sb("xnT", [P, 2, TG * P])
        gate = sb("gate", [P, 2, TG * P])
        hT = sb("hT", [P, 2, 3, TG * P])
        st = sb("st", [P, TG, 6])
        mv = sb("mv", [P, TG, 2])
        rstd = sb("rstd", [P, TG])
        ysum = sb("ysum", [P, TG, C])

        pp = ps("pp", [P, 2, 512])
        pS = ps("pS", [P, 2, 512])
        pT = ps("pT", [P, 2, 512])
        pO = ps("pO", [P, 2, 512])

        s_c = sem("constants_loaded", False)
        s_wa = sem("attention_weights_loaded", False)
        s_wf = sem("ff_weights_loaded", False)
        s_kept = sem("input_kept", False)
        s_clear = sem("cleared", False)
        s_vp = [sem(f"window_before_copied{u}", False) for u in range(2)]
        s_xs = sem("x_staged")
        s_xTp = sem("x_turned")
        s_xT = sem("xT_copied")
        s_qk = sem("qk_projected")
        s_v = sem("v_projected")
        s_V = sem("v_copied")
        s_sq = sem("squared")
        s_ss = sem("squares_summed")
        s_t = sem("rotary_products")
        s_add = sem("rotary_added")
        s_rn = sem("norms_made")
        s_kn = sem("k_normed")
        s_turn = sem("qk_turned")
        s_qkT = sem("qkT_copied")
        s_S = sem("scored")
        s_Sm = sem("maxed")
        s_E = sem("exped")
        s_ETp = sem("weights_turned")
        s_ETa = sem("wT_copied_by_act")
        s_ETd = sem("wT_copied_by_dve")
        s_PV = sem("pv_done")
        s_On = sem("output_normed")
        s_OTp = sem("output_turned")
        s_OT = sem("outT_copied")
        s_y = sem("y_made")
        s_x = sem("attention_added")
        f_xs = sem("ff_x_staged")
        f_T1 = sem("ff_x_turned")
        f_sT = sem("ff_shifted")
        f_T2 = sem("ff_turned_back")
        f_mv = sem("ff_stats")
        f_rstd = sem("ff_rstd")
        f_xn = sem("ff_normed")
        f_T3 = sem("ff_normed_turned")
        f_xnT = sem("ff_normedT_copied")
        f_h = sem("ff_hidden")
        f_g = sem("ff_gelu")
        f_hT = sem("ff_gated")
        f_o = sem("ff_out")
        f_y = sem("ff_summed")
        f_x = sem("ff_added")
        s_ri = sem("sums_inverted")
        f_dve = sem("ff_dve_steps")
        s_tab = sem("tables_made")
        s_nd = sem("norm_steps")
        s_held = sem("waits_passed", False)
        ctx.callback(clear_semaphores, nc, every)
        block = ctx.enter_context(nc.Block())

        def after(eng, s, value):
            eng.wait_ge(s, value + START)

        def visits(attention, l, on_pair=None):
            def pair(i, first, last):
                if on_pair:
                    on_pair(i)
                for u in range(2):
                    attention(l * NB + 2 * i + u, u, 2 * i + u, not (first and u == 0), not (last and u))
            return pair

        def layers(eng, attention, feed_forward, prologue, layer_start=None, on_pair=None):
            with eng.Fori(0, LAYERS) as l:
                if layer_start:
                    layer_start(l)
                prologue(l * NB, l)
                pair = visits(attention, l, on_pair and (lambda i: on_pair(l * (NB // 2) + i)))
                pair(0, True, False)
                with eng.Fori(1, NB // 2 - 1) as i:
                    pair(i, False, False)
                pair(NB // 2 - 1, False, True)
                feed_forward(l, l * NG)

        def groups(eng, l, one):
            def pair(i, first, last):
                for p in range(2):
                    one(l * NG + 2 * i + p, 2 * i + p, p, not (first and p == 0), 1 - p if last else 2)
            pair(0, True, False)
            with eng.Fori(1, NG // 2 - 1) as i:
                pair(i, False, False)
            pair(NG // 2 - 1, False, True)

        def inverse_norms(eng, ops, N, u, t, pass_waits):
            x = ss[:, u, t, :, :].rearrange("p j h -> p (j h)")
            y = rn[:, u, t, :, :].rearrange("p j h -> p (j h)")
            norm_steps = Steps(eng, s_nd, NORM_STEPS)
            norm_steps.start(2 * N + 1 - t)

            def link(ins):
                norm_steps.inc(ins)
                after(eng, s_nd, norm_steps.base + norm_steps.count)
                if pass_waits:
                    held(eng, s_held)

            after(eng, s_ss, 8 * N + 8 - 4 * t)
            after(eng, s_Sm, NU * (N - 1))
            after(eng, s_kn, 4 * (N - 1))
            after(eng, s_rn, 2 * N + 1 - t)
            held(eng, s_held)
            link(ops.tensor_scalar(x, x, 1e-24, None, ALU.max))
            link(ops.tensor_scalar(y.bitcast(I32), x.bitcast(I32), -0.5, RSQRT_GUESS,
                                         ALU.mult, ALU.add))
            for it in range(3):
                link(ops.tensor_tensor(nt[:, :], x, y, ALU.mult))
                link(ops.tensor_tensor(nt[:, :], nt[:, :], y, ALU.mult))
                link(ops.tensor_scalar(nt[:, :], nt[:, :], -0.5, 1.5, ALU.mult, ALU.add))
                last = ops.tensor_tensor(y, nt[:, :], y, ALU.mult)
                if it < 2:
                    link(last)
            last.then_inc(s_rn, 1)
            norm_steps.end()
            after(eng, s_rn, 2 * N + 2 - t)
            held(eng, s_held)

        @block.sync
        def _(sp):
            sp.dma_start(env["x_kept"], X[:, :, :]).then_inc(s_kept, 16)
            for t, (c, s) in enumerate((("l1_cos_q", "l1_sin_q"), ("l1_cos_k", "l1_sin_k"))):
                sp.dma_start(cos_c[:, t, :, :], consts[c].rearrange("(j p) d -> p j d", p=P)).then_inc(s_c, 16)
                sp.dma_start(sin_c[:, t, :, :], consts[s].rearrange("(j p) d -> p j d", p=P)).then_inc(s_c, 16)
            sp.dma_start(band[:, :], consts["band"]).then_inc(s_c, 16)
            with sp.Fori(0, LAYERS) as l:
                def of(name):
                    return weights[name][bass.ds(l, 1)]

                after(sp, s_x, NB * l)
                sp.dma_start(wqkv[:, :], of("Wqkv").rearrange("o c n -> c (o n)")).then_inc(s_wa, 16)
                sp.dma_start(wo[:, :, :], of("Wo").rearrange("o (k p) n -> p (o k) n", p=P)).then_inc(s_wa, 16)
                sp.dma_start(qks[:, 0, :], of("q_scale").broadcast_to([P, D])).then_inc(s_wa, 16)
                sp.dma_start(qks[:, 1, :], of("k_scale").broadcast_to([P, D])).then_inc(s_wa, 16)
                after(sp, f_x, NG * l)
                sp.dma_start(w1[:, :], of("W1").rearrange("o c n -> c (o n)")).then_inc(s_wf, 16)
                sp.dma_start(w2[:, 0:2, :], of("W2")[:, 0:2 * P, :].rearrange("o (k p) n -> p (o k) n", p=P)
                             ).then_inc(s_wf, 16)
                sp.dma_start(w2[0:F - 2 * P, 2, :], of("W2")[:, 2 * P:F, :].rearrange("o p n -> p (o n)")
                             ).then_inc(s_wf, 16)
                for part in range(2):
                    for k, (o, w) in enumerate(FC):
                        sp.dma_start(b1[0:w, part, k:k + 1],
                                     of("b1")[:, part * F + o:part * F + o + w].rearrange("o p -> p o")
                                     ).then_inc(s_wf, 16)
                sp.dma_start(lng[:, :], of("ln_g").rearrange("o p -> p o")).then_inc(s_wf, 16)
                sp.dma_start(lnb[:, :], of("ln_b").rearrange("o p -> p o")).then_inc(s_wf, 16)
                sp.dma_start(b2[:, :], of("b2").broadcast_to([P, C])).then_inc(s_wf, 16)

                with sp.Fori(0, NB // 2) as i:
                    for u in range(2):
                        N = l * NB + 2 * i + u
                        after(sp, s_V, 4 * N + 2)
                        after(sp, s_PV, NU * (N - 1))
                        sp.dma_start(vp[:, u, :], V[P - W:P, u, 0, :]).then_inc(s_vp[u], 16)
        W_A, W_F = 16 * 4, 16 * 12

        @block.gpsimd
        def _(pool):
            for s in sems:
                pool.sem_inc(s, START)
            nc.gpsimd.memset(xT[:, 0:1], 0.0).then_inc(s_clear, 1)
            nc.gpsimd.memset(fsT[:, :, 0:1], 0.0).then_inc(s_clear, 1)

            def stage(N, u, b):
                after(pool, s_xTp, N - 1)
                held(pool, s_held)
                nc.gpsimd.tensor_copy(xs[:, u, :, :], X[:, bass.ds(2 * b, NT), :]).then_inc(s_xs, 1)

            def chunk(N, u, c):
                t, j, half = place(c)
                cols = slice(512 * half, 512 * half + 512)
                after(pool, s_turn, 8 * N)
                after(pool, s_t, 8 * N + c + 1)
                nc.gpsimd.tensor_tensor(pre[:, j, t, cols], t1[:, c % 4, :], t2[:, c % 4, :], ALU.add
                                        ).then_inc(s_add, 1)

            def norm_k(N, u):
                after(pool, s_rn, 2 * N + 1)
                after(pool, s_add, 8 * N + 4)
                for half in range(2):
                    for j in range(NT):
                        k = pre[:, j, 1, 512 * half:512 * half + 512].rearrange("p (h d) -> p h d", d=D)
                        nc.gpsimd.tensor_tensor(
                            k, k, bcast(rn[:, u, 1, j, 8 * half:8 * half + 8], 2, D), ALU.mult
                        ).then_inc(s_kn, 1)

            def prologue(N, l):
                after(pool, f_x, NG * (l - 1) + 1)
                stage(N, 0, 0)
                for c in range(8):
                    chunk(N, 0, c)
                    if c == 3:
                        norm_k(N, 0)
                after(pool, f_x, NG * l)
                held(pool, s_held)

            def next_sequence(N, u, c):
                chunk(N, u, c)
                if c == 3:
                    inverse_norms(pool, nc.gpsimd, N, u, 1, True)
                    norm_k(N, u)
                if c == 7:
                    inverse_norms(pool, nc.gpsimd, N, u, 0, True)

            def attention(N, u, b, prev, nxt):
                if nxt:
                    stage(N + 1, 1 - u, b + 1)
                for n, uses in slots(prev, nxt).items():
                    for kind, c, d, bank, _ in uses:
                        if kind == "qk":
                            next_sequence(N + d, (u + d) % 2, c)

            def ff_stage(M, g):
                after(pool, f_T1, M)
                held(pool, s_held)
                nc.gpsimd.tensor_copy(fxs[:, :, :], X[:, bass.ds(TG * g, TG), :]).then_inc(f_xs, 1)

            def ff_rstd(M):
                after(pool, f_mv, M + 1)
                nc.gpsimd.tensor_tensor(rstd[:, :], mv[:, :, 1], neghalf[:, 0:TG], ALU.pow).then_inc(f_rstd, 1)

            def ff_one(M, g, p, prev, left):
                if left == 2:
                    ff_stage(M + 2, g + 2)
                if left:
                    ff_rstd(M + 1)

            def feed_forward(l, M0):
                after(pool, s_x, NB * (l + 1))
                ff_stage(M0, 0)
                ff_rstd(M0)
                ff_stage(M0 + 1, 1)
                groups(pool, l, ff_one)

            layers(pool, attention, feed_forward, prologue)

        @block.tensor
        def _(pe):
            def freed(kind, c, N):
                if kind == "x":
                    after(pe, s_xT, N + 1)
                elif kind == "qk":
                    after(pe, s_t, 8 * N + c + 1)
                elif kind == "v":
                    after(pe, s_V, 4 * N + c + 1)
                elif kind == "turn":
                    after(pe, s_qkT, 8 * N + c + 1)
                elif kind == "o":
                    after(pe, s_OT, 4 * N + c + 1)
                elif kind == "y":
                    after(pe, s_x, N + 1)

            def use(kind, c, bank, N, u, v_banks=pp):
                if kind == "x":
                    after(pe, s_xs, N + 1)
                    for j in range(NT):
                        last = nc.tensor.transpose(pp[:, bank, j * P:(j + 1) * P], xs[:, u, j, :], ident[:, :])
                    last.then_inc(s_xTp, 1)
                elif kind == "qk":
                    t, j, half = place(c)
                    after(pe, s_xT, N + 1)
                    nc.tensor.matmul(pp[:, bank, :], xT[:, j * P:(j + 1) * P],
                                     wqkv[:, t * I + 512 * half:t * I + 512 * half + 512],
                                     start=True, stop=True).then_inc(s_qk, 1)
                elif kind == "v":
                    j, half = c // 2, c % 2
                    nc.tensor.matmul(v_banks[:, bank, :], xT[:, j * P:(j + 1) * P],
                                     wqkv[:, 2 * I + 512 * half:2 * I + 512 * half + 512],
                                     start=True, stop=True).then_inc(s_v, 1)
                elif kind == "turn":
                    t, two = 1 - c // 4, c % 4
                    if t == 0:
                        after(pe, s_add, 8 * N + 8)
                    else:
                        after(pe, s_kn, 4 * N + 2 + 2 * (two // 2))
                    for g in range(2):
                        for j in range(NT):
                            o = (2 * two + g) * P
                            last = nc.tensor.transpose(pp[:, bank, g * T + j * P:g * T + (j + 1) * P],
                                                       pre[:, j, t, o:o + P], ident[:, :])
                    last.then_inc(s_turn, 1)
                elif kind == "o":
                    j, a = c // 2, c % 2
                    after(pe, s_On, 4 * N + c + 1)
                    for i in range(4):
                        o = a * 512 + i * P
                        last = nc.tensor.transpose(pp[:, bank, i * P:(i + 1) * P], On[:, j, o:o + P], ident[:, :])
                    last.then_inc(s_OTp, 1)
                elif kind == "y":
                    after(pe, s_OT, 4 * N + 4)
                    for j in range(NT):
                        for k in range(I // P):
                            last = nc.tensor.matmul(pp[:, bank, j * P:(j + 1) * P], OT[:, j, k, :], wo[:, k, :],
                                                    start=(k == 0), stop=(k == I // P - 1))
                    last.then_inc(s_y, 1)

            def scores(N, u, n):
                j = n // 8
                if n == 0:
                    after(pe, s_qkT, 8 * N + 8)
                after(pe, s_Sm, NU * N + n - 1)
                for m, h in enumerate(heads(n)):
                    r = D * (h % 2)
                    lo = 0 if j == 0 else P - W
                    last = nc.tensor.matmul(pS[:, n % 2, m * KW + W * (1 - j):(m + 1) * KW],
                                            qkT[r:r + D, u, 0, h // 2, j * P:(j + 1) * P],
                                            qkT[r:r + D, u, 1, h // 2, lo:(j + 1) * P], start=True, stop=True)
                last.then_inc(s_S, 1)

            def turn_weights(N, u, n):
                after(pe, s_E, NU * N + n + 1)
                after(pe, (s_ETa, s_ETd)[n % 2], 8 * N + n // 2)
                for m in range(2):
                    last = nc.tensor.transpose(pT[:, n % 2, m * P:(m + 1) * P], E[:, n % 4, m, W:KW], ident[:, :])
                if n >= 8:
                    for m in range(2):
                        last = nc.tensor.transpose(pT[0:W, n % 2, 2 * P + m * W:2 * P + (m + 1) * W],
                                                   E[0:W, n % 4, m, 0:W], ident[0:W, 0:W])
                last.then_inc(s_ETp, 1)

            def weigh(pair, N, u, n):
                j, r = n // 8, n // 4
                after(pe, (s_ETa, s_ETd)[n % 2], 8 * N + n // 2 + 1)
                if n == 0:
                    after(pe, s_V, 4 * N + 4)
                if n == 8:
                    pe.wait_ge(s_vp[u], 16 * (pair + 1))
                if n % 4 == 0:
                    after(pe, s_On, 4 * N + r - 1)
                for m, h in enumerate(heads(n)):
                    o = (h % 8) * D
                    last = nc.tensor.matmul(pO[:, r % 2, o:o + D], ET[:, n % 4, m * P:(m + 1) * P],
                                            V[:, u, j, h * D:(h + 1) * D], start=True, stop=True)
                    if j:
                        last = nc.tensor.matmul(pO[0:W, r % 2, o:o + D],
                                                ET[0:W, n % 4, 2 * P + m * W:2 * P + (m + 1) * W],
                                                vp[:, u, h * D:(h + 1) * D], start=False, stop=True,
                                                skip_group_check=True)
                last.then_inc(s_PV, 1)

            def prologue(N, l):
                before = []
                for kind, c in PROLOGUE:
                    if kind == "v":
                        after(pe, f_y, NG * l)
                        after(pe, s_V, 4 * N + c - 1)
                    else:
                        if len(before) >= 2:
                            freed(*before[-2], N)
                        before.append((kind, c))
                    use(kind, c, bank_of[kind, c], N, 0, pO)

            def attention(N, u, b, prev, nxt):
                for n, uses in slots(prev, nxt).items():
                    if n < NU:
                        scores(N, u, n)
                    for kind, c, d, bank, (kind2, c2, d2) in uses:
                        freed(kind2, c2, N + d2)
                        use(kind, c, bank, N + d, (u + d) % 2)
                    for unit in lagged(N, u, n, TURN_LAG, prev):
                        turn_weights(*unit)
                    for unit in lagged(N, u, n, WEIGH_LAG, prev):
                        weigh(pairs[0], *unit)

            def hidden(M, p, k):
                o, w = FC[k]
                q, bank = 3 * M + k, (3 * p + k) % 2
                after(pe, f_g, q - 1)
                after(pe, f_hT, q - 1)
                after(pe, f_xnT, M + 1)
                nc.tensor.matmul(pS[0:w, bank, :], w1[:, F + o:F + o + w], xnT[:, p, :], start=True, stop=True)
                nc.tensor.matmul(pT[0:w, bank, :], w1[:, o:o + w], xnT[:, p, :], start=True, stop=True
                                 ).then_inc(f_h, 1)

            def ff_out(M, p):
                after(pe, f_hT, 3 * M + 3)
                after(pe, f_y, M)
                for t in range(TG):
                    for k, (o, w) in enumerate(FC):
                        last = nc.tensor.matmul(pO[:, 1, t * P:(t + 1) * P], hT[0:w, p, k, t * P:(t + 1) * P],
                                                w2[0:w, k, :], start=(k == 0), stop=(k == 2))
                last.then_inc(f_o, 1)

            def ff_turn(M):
                after(pe, f_xs, M + 1)
                after(pe, f_sT, M)
                for t in range(TG):
                    last = nc.tensor.transpose(pp[:, 0, t * P:(t + 1) * P], fxs[:, t, :], ident[:, :])
                last.then_inc(f_T1, 1)

            def ff_turn_back(M):
                after(pe, f_sT, M + 1)
                after(pe, f_xn, M)
                for t in range(TG):
                    last = nc.tensor.transpose(pp[:, 1, t * P:(t + 1) * P],
                                               fsT[:, t // NT, t % NT * P:(t % NT + 1) * P], ident[:, :])
                last.then_inc(f_T2, 1)

            def ff_turn_normed(M):
                after(pe, f_xn, M + 1)
                after(pe, f_xnT, M)
                for t in range(TG):
                    last = nc.tensor.transpose(pO[:, 0, t * P:(t + 1) * P], xn[:, t, :], ident[:, :])
                last.then_inc(f_T3, 1)

            def ff_one(M, g, p, prev, left):
                if left:
                    ff_turn_back(M + 1)
                hidden(M, p, 0)
                hidden(M, p, 1)
                if prev:
                    ff_out(M - 1, 1 - p)
                if left:
                    ff_turn_normed(M + 1)
                if left == 2:
                    ff_turn(M + 2)
                hidden(M, p, 2)

            def feed_forward(l, M0):
                pe.wait_ge(s_wf, W_F * (l + 1))
                after(pe, s_x, NB * (l + 1))
                ff_turn(M0)
                ff_turn_back(M0)
                ff_turn_normed(M0)
                ff_turn(M0 + 1)
                groups(pe, l, ff_one)
                ff_out(M0 + NG - 1, 1)

            pairs = [None]
            pe.wait_ge(s_clear, 4)

            def on_pair(i):
                pairs[0] = i

            layers(pe, attention, feed_forward, prologue, lambda l: pe.wait_ge(s_wa, W_A * (l + 1)), on_pair)

        @block.scalar
        def _(act):
            act.wait_ge(s_clear, 4)

            def use(kind, c, bank, N, u, v_banks=pp):
                if kind == "x":
                    after(act, s_qk, 8 * N)
                    after(act, s_v, 4 * N)
                    after(act, s_xTp, N + 1)
                    nc.scalar.copy(xT[0:64, 0:T], pp[0:64, bank, 0:T])
                    nc.scalar.copy(xT[64:P, 1:T + 1], pp[64:P, bank, 0:T]).then_inc(s_xT, 1)
                elif kind == "qk":
                    after(act, s_ss, 8 * N + c - 1)
                    after(act, s_qk, 8 * N + c + 1)
                    nc.scalar.activation(sq[:, c % 2, :], pp[:, bank, :], ACT.Square).then_inc(s_sq, 1)
                elif kind == "v":
                    after(act, s_PV, NU * (N - 1))
                    after(act, s_v, 4 * N + c + 1)
                    nc.scalar.copy(V[:, u, c // 2, 512 * (c % 2):512 * (c % 2) + 512], v_banks[:, bank, :]
                                   ).then_inc(s_V, 1)
                elif kind == "turn":
                    after(act, s_S, NU * (N - 1))
                    after(act, s_turn, 8 * N + c + 1)
                    k = 2 * (c % 4)
                    nc.scalar.copy(qkT[:, u, 1 - c // 4, k:k + 2, :].rearrange("p g t -> p (g t)"), pp[:, bank, :]
                                   ).then_inc(s_qkT, 1)
                elif kind == "o":
                    after(act, s_y, N)
                    after(act, s_OTp, 4 * N + c + 1)
                    nc.scalar.copy(OT[:, c // 2, 4 * (c % 2):4 * (c % 2) + 4, :].rearrange("p k q -> p (k q)"),
                                   pp[:, bank, :]).then_inc(s_OT, 1)

            def exps(N, u, n):
                j = n // 8
                o = W * (1 - j)
                after(act, s_Sm, NU * N + n + 1)
                after(act, s_ETp, NU * N + n - 3)
                for m, h in enumerate(heads(n)):
                    last = nc.scalar.activation(E[:, n % 4, m, o:KW], S[:, n % 4, m, o:KW], ACT.Exp,
                                                bias=nm[:, u, j, h:h + 1], scale=-1.0,
                                                accum_out=rs[:, u, j, h:h + 1])
                last.then_inc(s_E, 1)

            def copy_weights(N, n):
                w = 2 * P + (2 * W if n >= 8 else 0)
                after(act, s_ETp, NU * N + n + 1)
                after(act, s_PV, NU * N + n - 3)
                nc.scalar.copy(ET[:, n % 4, 0:w], pT[:, 0, 0:w]).then_inc(s_ETa, 1)

            def prologue(N, l):
                for kind, c in PROLOGUE:
                    use(kind, c, bank_of[kind, c], N, 0, pO)

            def attention(N, u, b, prev, nxt):
                for n, uses in slots(prev, nxt).items():
                    for kind, c, d, bank, _ in uses:
                        use(kind, c, bank, N + d, (u + d) % 2)
                    for unit in lagged(N, u, n, EXP_LAG, prev):
                        exps(*unit)
                    for visit, v, m in lagged(N, u, n, TURN_LAG, prev):
                        if m % 2 == 0:
                            copy_weights(visit, m)

            def shift(M):
                after(act, f_T1, M + 1)
                after(act, f_T2, M)
                for e in range(2):
                    last = nc.scalar.copy(fsT[64 * e:64 * e + 64, :, e:T + e],
                                          pp[64 * e:64 * e + 64, 0, :].rearrange("p (s t) -> p s t", s=GR))
                last.then_inc(f_sT, 1)

            def gelu(M, p, k):
                w, q, bank = FC[k][1], 3 * M + k, (3 * p + k) % 2
                after(act, f_h, q + 1)
                after(act, f_hT, q - 1)
                nc.scalar.activation(gate[0:w, bank, :], pS[0:w, bank, :], ACT.Gelu, bias=b1[0:w, 1, k:k + 1]
                                     ).then_inc(f_g, 1)

            def ff_one(M, g, p, prev, left):
                gelu(M, p, 0)
                gelu(M, p, 1)
                if left == 2:
                    shift(M + 2)
                gelu(M, p, 2)

            def feed_forward(l, M0):
                act.wait_ge(s_wf, W_F * (l + 1))
                shift(M0)
                shift(M0 + 1)
                groups(act, l, ff_one)

            layers(act, attention, feed_forward, prologue)

        @block.vector
        def _(dve):
            for n in range(2):
                nc.vector.memset(pT[:, n, 2 * P:2 * P + 2 * W], 0.0).then_inc(s_clear, 1)
            dve.wait_ge(s_c, 16 * 5)
            dve.wait_ge(s_kept, 16)
            ff_steps = Steps(dve, f_dve, 8, s_held)

            def tables(l):
                dve.wait_ge(s_wa, W_A * (l + 1))
                for t in range(2):
                    nc.vector.tensor_tensor(cosT[:, t, :, :], cos_c[:, t, :, :], bcast(qks[:, t, :], 1, NT), ALU.mult)
                    for e in range(2):
                        a, b = 32 * e, 32 * (1 - e)
                        nc.vector.tensor_tensor(sinT[:, t, :, a:a + 32], sin_c[:, t, :, a:a + 32],
                                                bcast(qks[:, t, b:b + 32], 1, NT), ALU.mult).then_inc(s_tab, 1)
                after(dve, s_tab, 4 * (l + 1))

            def chunk(N, u, c, bank):
                t, j, half = place(c)
                p = pp[:, bank, :].rearrange("p (h d) -> p h d", d=D)
                after(dve, s_add, 8 * N + c - 3)
                after(dve, s_sq, 8 * N + c + 1)
                nc.vector.tensor_tensor(t1[:, c % 4, :].rearrange("p (h d) -> p h d", d=D), p,
                                        bcast(cosT[:, t, j, :], 1, 8), ALU.mult)
                for e in range(2):
                    a, b = 32 * e, 32 * (1 - e)
                    last = nc.vector.tensor_tensor(
                        t2[:, c % 4, :].rearrange("p (h d) -> p h d", d=D)[:, :, a:a + 32], p[:, :, b:b + 32],
                        bcast(sinT[:, t, j, a:a + 32], 1, 8), ALU.mult)
                last.then_inc(s_t, 1)
                after(dve, s_rn, 2 * (N - 1))
                nc.vector.tensor_reduce(ss[:, u, t, j, 8 * half:8 * half + 8],
                                        sq[:, c % 2, :].rearrange("p (h d) -> p h d", d=D), AX.X, ALU.add
                                        ).then_inc(s_ss, 1)

            def maxima(N, u, n):
                j = n // 8
                o = W * (1 - j)
                after(dve, s_E, NU * N + n - 3)
                if n == 0:
                    after(dve, s_rn, 2 * N + 2)
                after(dve, s_S, NU * N + n + 1)
                held(dve, s_held)
                for m, h in enumerate(heads(n)):
                    last = nc.vector.tensor_tensor_reduce(
                        out=S[:, n % 4, m, o:KW], in0=pS[:, n % 2, m * KW + o:(m + 1) * KW], in1=band[:, o:KW],
                        scale=rn[:, u, 0, j, h:h + 1], scalar=HUGE, op0=ALU.add, op1=ALU.min,
                        accum_out=nm[:, u, j, h:h + 1])
                last.then_inc(s_Sm, 1)

            def copy_weights(N, n):
                w = 2 * P + (2 * W if n >= 8 else 0)
                after(dve, s_ETp, NU * N + n + 1)
                after(dve, s_PV, NU * N + n - 3)
                nc.vector.tensor_copy(ET[:, n % 4, 0:w], pT[:, 1, 0:w]).then_inc(s_ETd, 1)

            def invert_sums(N, u, r):
                j, a = r // 2, r % 2
                after(dve, s_E, NU * N + 4 * r + 4)
                after(dve, s_On, 4 * N + r - 1)
                nc.vector.reciprocal(ri[:, r % 2, :], rs[:, u, j, 8 * a:8 * a + 8]).then_inc(s_ri, 1)

            def norm_output(N, r):
                j, a = r // 2, r % 2
                after(dve, s_ri, 4 * N + r + 1)
                after(dve, s_OTp, 4 * N + r - 3)
                after(dve, s_PV, NU * N + 4 * r + 4)
                nc.vector.tensor_tensor(
                    On[:, j, 512 * a:512 * a + 512].rearrange("p (h d) -> p h d", d=D),
                    pO[:, r % 2, :].rearrange("p (h d) -> p h d", d=D), bcast(ri[:, r % 2, :], 2, D), ALU.mult
                ).then_inc(s_On, 1)

            def add_attention(N, b, bank):
                after(dve, s_y, N + 1)
                x = X[:, bass.ds(2 * b, NT), :]
                nc.vector.tensor_tensor(x, pp[:, bank, 0:T].rearrange("p (j c) -> p j c", j=NT), x, ALU.add
                                        ).then_inc(s_x, 1)

            def prologue(N, l):
                for c in range(8):
                    chunk(N, 0, c, bank_of["qk", c])
                    if c % 4 == 3:
                        inverse_norms(dve, nc.vector, N, 0, 1 - c // 4, False)

            def attention(N, u, b, prev, nxt):
                for n, uses in slots(prev, nxt).items():
                    if n < NU:
                        maxima(N, u, n)
                    for visit, _, m in lagged(N, u, n, NORM_LAG, prev):
                        if m % 4 == 3:
                            norm_output(visit, m // 4)
                    for kind, c, d, bank, _ in uses:
                        if kind == "qk":
                            chunk(N + d, (u + d) % 2, c, bank)
                        elif kind == "y":
                            add_attention(N + d, b + d, bank)
                    for visit, v, m in lagged(N, u, n, TURN_LAG, prev):
                        if m % 2 == 1:
                            copy_weights(visit, m)
                    for visit, v, m in lagged(N, u, n, NORM_LAG - 1, prev):
                        if m % 4 == 3:
                            invert_sums(visit, v, m // 4)

            def stats(M):
                after(dve, f_T2, M + 1)
                ff_steps.start(M)
                for t in range(TG):
                    ff_steps.inc(nc.vector.bn_stats(st[:, t, :], pp[:, 1, t * P:(t + 1) * P]))
                after(dve, f_dve, ff_steps.base + ff_steps.count)
                held(dve, s_held)
                for t in range(TG):
                    ff_steps.inc(nc.vector.bn_aggr(mv[:, t, :], st[:, t, :]))
                after(dve, f_dve, ff_steps.base + ff_steps.count)
                nc.vector.tensor_scalar(mv[:, :, 1], mv[:, :, 1], LN_EPS, None, ALU.add).then_inc(f_mv, 1)
                ff_steps.end()

            def normalise(M):
                after(dve, f_rstd, M + 1)
                after(dve, f_T3, M)
                for t in range(TG):
                    last = nc.vector.tensor_scalar(xn[:, t, :], pp[:, 1, t * P:(t + 1) * P], mv[:, t, 0:1],
                                                   rstd[:, t:t + 1], ALU.subtract, ALU.mult)
                last.then_inc(f_xn, 1)
                after(dve, f_xn, M + 1)
                held(dve, s_held)

            def copy_normed(M, p):
                after(dve, f_T3, M + 1)
                after(dve, f_h, 3 * (M - 1))
                held(dve, s_held)
                nc.vector.tensor_scalar(xnT[:, p, :], pO[:, 0, :], lng[:, :], lnb[:, :], ALU.mult, ALU.add
                                        ).then_inc(f_xnT, 1)

            def gated(M, p, k):
                w, q, bank = FC[k][1], 3 * M + k, (3 * p + k) % 2
                after(dve, f_o, M - 1)
                after(dve, f_g, q + 1)
                nc.vector.scalar_tensor_tensor(hT[0:w, p, k, :], pT[0:w, bank, :], b1[0:w, 0, k:k + 1],
                                               gate[0:w, bank, :], ALU.add, ALU.mult).then_inc(f_hT, 1)

            def add_ff(M, g):
                after(dve, f_o, M + 1)
                x = X[:, bass.ds(TG * g, TG), :]
                nc.vector.tensor_tensor(ysum[:, :, :], pO[:, 1, :].rearrange("p (t c) -> p t c", t=TG), x, ALU.add
                                        ).then_inc(f_y, 1)
                after(dve, f_y, M + 1)
                nc.vector.tensor_tensor(x, ysum[:, :, :], bcast(b2[:, :], 1, TG), ALU.add).then_inc(f_x, 1)

            def ff_one(M, g, p, prev, left):
                if left:
                    stats(M + 1)
                gated(M, p, 0)
                if left:
                    normalise(M + 1)
                gated(M, p, 1)
                if left:
                    copy_normed(M + 1, 1 - p)
                if prev:
                    add_ff(M - 1, g - 1)
                gated(M, p, 2)

            def feed_forward(l, M0):
                dve.wait_ge(s_wf, W_F * (l + 1))
                stats(M0)
                normalise(M0)
                copy_normed(M0, 0)
                groups(dve, l, ff_one)
                add_ff(M0 + NG - 1, NG - 1)

            layers(dve, attention, feed_forward, prologue, tables)


def last_norm(nc, env, out):
    X, neghalf = env["X"], env["neghalf"]
    with ExitStack() as ctx:
        def sb(name, shape):
            return ctx.enter_context(nc.sbuf_tensor("z_" + name, shape, F32))

        def sem(name):
            return ctx.enter_context(nc.semaphore("z_" + name))

        x0 = sb("x0", [P, NB * NT, C])
        st = sb("st", [P, NB * NT, 6])
        mv = sb("mv", [P, NB * NT, 2])
        rstd = sb("rstd", [P, NB * NT])
        s_st, s_ag, s_mv, s_rstd, s_x, s_out, s_x0, s_add = (
            sem(n) for n in ("stats", "aggregated", "eps_added", "rstd", "normed", "stored", "input_loaded", "input_added"))
        block = ctx.enter_context(nc.Block())
        NTILES = NB * NT

        @block.vector
        def _(dve):
            dve.wait_ge(s_x0, 16)
            for q in range(4):
                tiles = slice(NTILES // 4 * q, NTILES // 4 * (q + 1))
                nc.vector.tensor_tensor(X[:, tiles, :], X[:, tiles, :], x0[:, tiles, :], ALU.add).then_inc(s_add, 1)
            dve.wait_ge(s_add, 4)
            for t in range(NTILES):
                nc.vector.bn_stats(st[:, t, :], X[:, t, :]).then_inc(s_st, 1)
            dve.wait_ge(s_st, NTILES)
            for t in range(NTILES):
                nc.vector.bn_aggr(mv[:, t, :], st[:, t, :]).then_inc(s_ag, 1)
            dve.wait_ge(s_ag, NTILES)
            nc.vector.tensor_scalar(mv[:, :, 1], mv[:, :, 1], LN_EPS, None, ALU.add).then_inc(s_mv, 1)
            dve.wait_ge(s_rstd, 1)
            for t in range(NTILES):
                nc.vector.tensor_scalar(X[:, t, :], X[:, t, :], mv[:, t, 0:1], rstd[:, t:t + 1],
                                        ALU.subtract, ALU.mult).then_inc(s_x, 1)

        @block.gpsimd
        def _(pool):
            pool.wait_ge(s_mv, 1)
            nc.gpsimd.tensor_tensor(rstd[:, :], mv[:, :, 1], neghalf[:, 0:NTILES], ALU.pow).then_inc(s_rstd, 1)

        @block.sync
        def _(sp):
            sp.dma_start(x0[:, :, :], env["x_kept"]).then_inc(s_x0, 16)
            for q in range(4):
                sp.wait_ge(s_x, NTILES // 4 * (q + 1))
                b = NB // 4 * q
                sp.dma_start(out[b:b + NB // 4].rearrange("b (j p) c -> p (b j) c", p=P),
                             X[:, NT * b:NT * (b + NB // 4), :]).then_inc(s_out, 16)
            sp.wait_ge(s_out, 16 * 4)


def program(nc, ins, consts, out):
    with ExitStack() as ctx:
        X = ctx.enter_context(nc.sbuf_tensor("X", [P, NB * NT, C], F32))
        ident = ctx.enter_context(nc.sbuf_tensor("ident", [P, P], F32))
        neghalf = ctx.enter_context(nc.sbuf_tensor("neghalf", [P, 64], F32))
        x_kept = nc.dram_tensor("x_kept", (P, NB * NT, C), F32).ap()
        env = {"x_kept": x_kept, "X": X, "ident": ident, "neghalf": neghalf, "x_dram": ins["L0_attn_x"]}

        def of(prefix):
            return {k[len(prefix):]: v for k, v in ins.items() if k.startswith(prefix)}

        l0_attention(nc, env, of("L0_attn_"), consts)
        l0_experts(nc, env, of("L0_ffn_"), consts)
        l1_attention(nc, env, of("L1_attn_"), consts)
        l1_network(nc, env, of("L1_ffn_"), consts)
        last_norm(nc, env, out)


def shape_constants():
    f = np.float32
    t = np.arange(T, dtype=f)
    inv = (1.0 / 10000.0 ** (np.arange(0, 4, 2, dtype=f) / f(4))).astype(f)
    emb = np.concatenate([t[:, None] * inv[None, :]] * 2, axis=-1).astype(f)
    sign = np.array([-1, 1, -1, 1], f)
    row, col = np.arange(P)[:, None], np.arange(P)[None, :]
    causal = np.concatenate([np.zeros((P, P), f), np.where(col <= row, 0, MASKED).astype(f)], axis=1)
    half = np.arange(0, 64, 2, dtype=f)
    inv_freq = (1.0 / f(10000.0) ** (half / f(64))).astype(f)
    freqs = (t[:, None] * inv_freq[None, :]).astype(f)
    freqs = np.concatenate([freqs, freqs], -1)
    base = ((half + f(0.4 * 64)) / f(1.4 * 64)).astype(f)
    power = ((t - T // 2) / f(16)).astype(f)
    scale = (base[None, :] ** power[:, None]).astype(f)
    scale = np.concatenate([scale, scale], -1)
    cos, sin = np.cos(freqs).astype(f), np.sin(freqs).astype(f)
    sin[:, :32] *= -1
    rel = row - (np.arange(160)[None, :] - 32)
    chunk = (row // 32 == col // 32) & (row <= col)
    look = np.where((rel >= 1) & (rel <= 32), 0, MASKED).astype(f)
    before = np.where(rel == 1, 0, MASKED).astype(f)
    notfirst = np.ones((P, NT), f)
    notfirst[0, 0] = 0
    pr = np.arange(P)
    return {
        "row_sequence": (pr[:, None] // 16 == np.arange(8)[None, :]).astype(f),
        "row_expert": (pr[:, None] % 16 == np.arange(16)[None, :]).astype(f),
        "token": (pr[:, None] + P * np.arange(NT)[None, :]).astype(f),
        "iota": np.broadcast_to(t[None, :], (P, T)),
        "prefix": np.where(chunk, f(1) / (col % 32 + 1).astype(f), 0).astype(f),
        "look_mask": np.concatenate([look, before], axis=1),
        "prev": (rel == 1).astype(f),
        "notfirst": notfirst,
        "l1_cos_q": -8 * cos * scale, "l1_sin_q": -8 * sin * scale,
        "l1_cos_k": cos / scale, "l1_sin_k": sin / scale,
        "band": np.where((rel >= 0) & (rel <= 32), 0, -MASKED).astype(f),
        "ident": np.eye(P, dtype=f),
        "causal": causal,
        "l0_cos": np.cos(emb).astype(f),
        "l0_sin": (np.sin(emb) * sign).astype(f),
    }


def kernel(**inputs):
    import concourse.bacc as bacc
    from concourse.bass_utils import run_bass_kernel_spmd as run

    nc = bacc.Bacc("TRN2", target_bir_lowering=False, num_devices=1)
    arrays, ins, consts = {}, {}, {}
    for name, value in inputs.items():
        a = np.ascontiguousarray(value)
        if a.ndim == 0:
            a = a.reshape(1, 1)
        arrays[f"in_{name}"] = a
        ins[name] = nc.dram_tensor(f"in_{name}", a.shape, mybir.dt.from_np(a.dtype), kind="ExternalInput").ap()
    for name, a in shape_constants().items():
        a = np.ascontiguousarray(a)
        arrays[f"const_{name}"] = a
        consts[name] = nc.dram_tensor(f"const_{name}", a.shape, mybir.dt.from_np(a.dtype), kind="ExternalInput").ap()
    out = nc.dram_tensor("out", (NB, T, C), F32, kind="ExternalOutput").ap()
    program(nc, ins, consts, out)
    return run(nc, [arrays], core_ids=[0]).results[0]["out"]
```
